# Optimizing a Trainium2 kernel written in Bass

```python
import numpy as np
import jax
import jax.numpy as jnp

def _softmax(x, axis=-1):
    return jax.nn.softmax(x, axis=axis)

def _gelu(x):
    return jax.nn.gelu(x, approximate=True)

def _silu(x):
    return jax.nn.silu(x)

def _sigmoid(x):
    return jax.nn.sigmoid(x)

def _layernorm(x, axis=-1, eps=1e-05):
    m = jnp.mean(x, axis=axis, keepdims=True)
    v = jnp.var(x, axis=axis, keepdims=True)
    return (x - m) / jnp.sqrt(v + eps)

def _scatter_add(tgt, idx, src, axis=0):
    return tgt.at[idx].add(src)

def _segment_sum(src, seg, n):
    return jax.ops.segment_sum(src, seg, n)
kernel_name = 'mk_gnn_preln_d4_gnn_r16_659530'

def setup_inputs(seed: int=0):
    np.random.seed(seed)
    _w = jnp.asarray

    def _rec_inputs():
        import jax
        import jax.numpy as jnp
        _gk = jax.random.key(seed)
        x = -0.0001126 + 1 * jax.random.normal(jax.random.fold_in(_gk, 1), (625, 768), jnp.float32)
        _s = jax.random.randint(jax.random.fold_in(_gk, 2), (5000,), 0, 625, jnp.int32)
        _d = jax.random.randint(jax.random.fold_in(_gk, 3), (5000,), 0, 625, jnp.int32)
        _loop = jnp.arange(625, dtype=jnp.int32)
        src = jnp.concatenate([_s, _d, _loop])
        dst = jnp.concatenate([_d, _s, _loop])
        _o = jnp.argsort(dst, stable=True)
        src = src[_o]
        dst = dst[_o]
        edge_type_3 = jax.random.randint(jax.random.fold_in(_gk, 12), (10625,), 0, 3, jnp.int32)
        edge_type_34 = jax.random.randint(jax.random.fold_in(_gk, 13), (10625,), 0, 34, jnp.int32)
        node_type_3 = jax.random.randint(jax.random.fold_in(_gk, 14), (625,), 0, 3, jnp.int32)
        return (x, src, dst, edge_type_3, edge_type_34, node_type_3)
    x, src, dst, edge_type_3, edge_type_34, node_type_3 = _rec_inputs()

    def _L0_gnn_setup():
        import jax, jax.numpy as jnp
        import numpy as np
        N_NODES = 625
        N_EDGES = 6250
        N_REL = 34
        DIM = 768

        def _graph_encoder(x, edge_index, edge_type, W_rel, W_root, b_rgcn, W_gcn, b_gcn):
            n = x.shape[0]
            src, dst = (edge_index[0], edge_index[1])
            ones = jnp.ones((src.shape[0],), dtype=x.dtype)
            seg = edge_type * n + dst
            agg = jax.ops.segment_sum(x[src], seg, num_segments=N_REL * n)
            cnt = jax.ops.segment_sum(ones, seg, num_segments=N_REL * n)
            mean = agg.reshape(N_REL, n, -1) / jnp.maximum(cnt, 1.0).reshape(N_REL, n, 1)
            h1 = jnp.einsum('rni,rio->no', mean, W_rel) + x @ W_root + b_rgcn
            xw = h1 @ W_gcn
            deg = jax.ops.segment_sum(ones, dst, num_segments=n) + 1.0
            dinv = jax.lax.rsqrt(deg)
            norm = dinv[src] * dinv[dst]
            out = jax.ops.segment_sum(xw[src] * norm[:, None], dst, num_segments=n)
            out = out + xw * (dinv * dinv)[:, None]
            return out + b_gcn
        key = jax.random.key(seed)
        ks = jax.random.split(key, 6)
        scale = 1.0 / np.sqrt(DIM)
        x = jax.random.normal(ks[0], (N_NODES, DIM), dtype=jnp.float32)
        edge_index = jax.random.randint(ks[1], (2, N_EDGES), 0, N_NODES, dtype=jnp.int32)
        edge_type = jax.random.randint(ks[2], (N_EDGES,), 0, N_REL, dtype=jnp.int32)
        W_rel = jax.random.normal(ks[3], (N_REL, DIM, DIM), dtype=jnp.float32) * scale
        W_root = jax.random.normal(ks[4], (DIM, DIM), dtype=jnp.float32) * scale
        b_rgcn = jnp.zeros((DIM,), dtype=jnp.float32)
        W_gcn = jax.random.normal(ks[5], (DIM, DIM), dtype=jnp.float32) * scale
        b_gcn = jnp.zeros((DIM,), dtype=jnp.float32)
        return {'x': x, 'edge_index': edge_index, 'edge_type': edge_type, 'W_rel': W_rel, 'W_root': W_root, 'b_rgcn': b_rgcn, 'W_gcn': W_gcn, 'b_gcn': b_gcn}
    _L0_gnn_all = _L0_gnn_setup()
    _L0_gnn_in = {k: v for k, v in _L0_gnn_all.items() if k in ('W_rel', 'W_root', 'b_rgcn', 'W_gcn', 'b_gcn')}
    del _L0_gnn_all

    def _L1_gnn_setup():
        import jax, jax.numpy as jnp
        import numpy as np
        N_NODES = 625
        D = 768
        N_EDGES = 10000

        def gcn_conv(x, W, b, src, dst, n_nodes):
            h = x @ W
            deg = jax.ops.segment_sum(jnp.ones_like(dst, dtype=h.dtype), dst, num_segments=n_nodes)
            dinv = jnp.where(deg > 0, jax.lax.rsqrt(deg), 0.0)
            norm = dinv[src] * dinv[dst]
            msgs = h[src] * norm[:, None]
            out = jax.ops.segment_sum(msgs, dst, num_segments=n_nodes)
            return out + b

        def add_self_loops(edge_index, n_nodes):
            loop = jnp.arange(n_nodes, dtype=edge_index.dtype)
            src = jnp.concatenate([edge_index[0], loop])
            dst = jnp.concatenate([edge_index[1], loop])
            return (src, dst)
        key = jax.random.key(seed)
        k1, k2, k3, k4 = jax.random.split(key, 4)
        x = jax.random.normal(k1, (N_NODES, D), dtype=jnp.float32)
        edge_index = jax.random.randint(k2, (2, N_EDGES), 0, N_NODES, dtype=jnp.int32)
        glorot = float(np.sqrt(6.0 / (D + D)))
        W1 = jax.random.uniform(k3, (D, D), jnp.float32, -glorot, glorot)
        W2 = jax.random.uniform(k4, (D, D), jnp.float32, -glorot, glorot)
        b1 = jnp.zeros((D,), jnp.float32)
        b2 = jnp.zeros((D,), jnp.float32)
        return {'x': x, 'W1': W1, 'b1': b1, 'W2': W2, 'b2': b2, 'edge_index': edge_index}
    _L1_gnn_all = _L1_gnn_setup()
    _L1_gnn_in = {k: v for k, v in _L1_gnn_all.items() if k in ('W1', 'b1', 'W2', 'b2')}
    del _L1_gnn_all

    def _L2_gnn_setup():
        import jax, jax.numpy as jnp
        import numpy as np
        NUM_NODES = 625
        NUM_EDGES = 10000
        IN_CH = 768
        TYPE_DIM = 128
        HID = 768
        OUT = 768
        NUM_REL = 3
        NUM_NODE_TYPE = 3

        def _glorot(key, shape):
            fan_in, fan_out = (shape[-2], shape[-1])
            lim = (6.0 / (fan_in + fan_out)) ** 0.5
            return jax.random.uniform(key, shape, jnp.float32, -lim, lim)

        def rgcn_conv(h, src, dst, edge_type, w_rel, w_root, bias):
            num_nodes = h.shape[0]
            xw = jnp.einsum('nd,rde->rne', h, w_rel)
            msg = xw[edge_type, src]
            onehot = jax.nn.one_hot(edge_type, NUM_REL, dtype=h.dtype)
            count = jax.ops.segment_sum(onehot, dst, num_segments=num_nodes)
            inv = jnp.where(count > 0, 1.0 / jnp.maximum(count, 1.0), 0.0)
            msg = msg * inv[dst, edge_type][:, None]
            agg = jax.ops.segment_sum(msg, dst, num_segments=num_nodes)
            return agg + h @ w_root + bias
        key = jax.random.key(seed)
        ks = jax.random.split(key, 16)
        d1 = IN_CH + TYPE_DIM
        inp = {'x': jax.random.normal(ks[0], (NUM_NODES, IN_CH), jnp.float32), 'node_type': jax.random.randint(ks[1], (NUM_NODES,), 0, NUM_NODE_TYPE, jnp.int32), 'edge_index': jax.random.randint(ks[2], (2, NUM_EDGES), 0, NUM_NODES, jnp.int32), 'edge_type': jax.random.randint(ks[3], (NUM_EDGES,), 0, NUM_REL, jnp.int32), 'node_emb': jax.random.normal(ks[4], (NUM_NODE_TYPE, TYPE_DIM), jnp.float32), 'w_rel1': _glorot(ks[5], (NUM_REL, d1, d1)), 'w_root1': _glorot(ks[6], (d1, d1)), 'b1': jnp.zeros((d1,), jnp.float32), 'w_rel2': _glorot(ks[7], (NUM_REL, d1, HID)), 'w_root2': _glorot(ks[8], (d1, HID)), 'b2': jnp.zeros((HID,), jnp.float32), 'w_rel3': _glorot(ks[9], (NUM_REL, HID, OUT)), 'w_root3': _glorot(ks[10], (HID, OUT)), 'b3': jnp.zeros((OUT,), jnp.float32)}
        return inp
    _L2_gnn_all = _L2_gnn_setup()
    _L2_gnn_in = {k: v for k, v in _L2_gnn_all.items() if k in ('node_emb', 'w_rel1', 'w_root1', 'b1', 'w_rel2', 'w_root2', 'b2', 'w_rel3', 'w_root3', 'b3')}
    del _L2_gnn_all

    def _L3_gnn_setup():
        import jax, jax.numpy as jnp
        import numpy as np
        N_NODES = 625
        N_EDGES = 6250
        DIM = 768
        key = jax.random.key(seed)
        k1, k2, k3, k4 = jax.random.split(key, 4)
        x = jax.random.normal(k1, (N_NODES, DIM), dtype=jnp.float32)
        edge_index = jax.random.randint(k2, (2, N_EDGES), 0, N_NODES, dtype=jnp.int32)
        W = jax.random.normal(k3, (DIM, DIM), dtype=jnp.float32) / np.sqrt(DIM)
        b = jnp.zeros((DIM,), dtype=jnp.float32)
        return {'x': x, 'edge_index': edge_index, 'W': W, 'b': b}
    _L3_gnn_all = _L3_gnn_setup()
    _L3_gnn_in = {k: v for k, v in _L3_gnn_all.items() if k in ('W', 'b')}
    del _L3_gnn_all
    return {'x': x, 'src': src, 'dst': dst, 'edge_type_3': edge_type_3, 'edge_type_34': edge_type_34, 'node_type_3': node_type_3, 'L0_gnn_W_rel': _L0_gnn_in['W_rel'], 'L0_gnn_W_root': _L0_gnn_in['W_root'], 'L0_gnn_b_rgcn': _L0_gnn_in['b_rgcn'], 'L0_gnn_W_gcn': _L0_gnn_in['W_gcn'], 'L0_gnn_b_gcn': _L0_gnn_in['b_gcn'], 'L1_gnn_W1': _L1_gnn_in['W1'], 'L1_gnn_b1': _L1_gnn_in['b1'], 'L1_gnn_W2': _L1_gnn_in['W2'], 'L1_gnn_b2': _L1_gnn_in['b2'], 'L2_gnn_node_emb': _L2_gnn_in['node_emb'], 'L2_gnn_w_rel1': _L2_gnn_in['w_rel1'], 'L2_gnn_w_root1': _L2_gnn_in['w_root1'], 'L2_gnn_b1': _L2_gnn_in['b1'], 'L2_gnn_w_rel2': _L2_gnn_in['w_rel2'], 'L2_gnn_w_root2': _L2_gnn_in['w_root2'], 'L2_gnn_b2': _L2_gnn_in['b2'], 'L2_gnn_w_rel3': _L2_gnn_in['w_rel3'], 'L2_gnn_w_root3': _L2_gnn_in['w_root3'], 'L2_gnn_b3': _L2_gnn_in['b3'], 'L3_gnn_W': _L3_gnn_in['W'], 'L3_gnn_b': _L3_gnn_in['b']}

def reference(x, src, dst, edge_type_3, edge_type_34, node_type_3, L0_gnn_W_rel, L0_gnn_W_root, L0_gnn_b_rgcn, L0_gnn_W_gcn, L0_gnn_b_gcn, L1_gnn_W1, L1_gnn_b1, L1_gnn_W2, L1_gnn_b2, L2_gnn_node_emb, L2_gnn_w_rel1, L2_gnn_w_root1, L2_gnn_b1, L2_gnn_w_rel2, L2_gnn_w_root2, L2_gnn_b2, L2_gnn_w_rel3, L2_gnn_w_root3, L2_gnn_b3, L3_gnn_W, L3_gnn_b):
    import jax
    import jax.numpy as jnp

    def _L0_gnn_ref(x, edge_index, edge_type, W_rel, W_root, b_rgcn, W_gcn, b_gcn):
        import jax, jax.numpy as jnp
        import numpy as np
        N_NODES = 625
        N_EDGES = 6250
        N_REL = 34
        DIM = 768

        def _graph_encoder(x, edge_index, edge_type, W_rel, W_root, b_rgcn, W_gcn, b_gcn):
            n = x.shape[0]
            src, dst = (edge_index[0], edge_index[1])
            ones = jnp.ones((src.shape[0],), dtype=x.dtype)
            seg = edge_type * n + dst
            agg = jax.ops.segment_sum(x[src], seg, num_segments=N_REL * n)
            cnt = jax.ops.segment_sum(ones, seg, num_segments=N_REL * n)
            mean = agg.reshape(N_REL, n, -1) / jnp.maximum(cnt, 1.0).reshape(N_REL, n, 1)
            h1 = jnp.einsum('rni,rio->no', mean, W_rel) + x @ W_root + b_rgcn
            xw = h1 @ W_gcn
            deg = jax.ops.segment_sum(ones, dst, num_segments=n) + 1.0
            dinv = jax.lax.rsqrt(deg)
            norm = dinv[src] * dinv[dst]
            out = jax.ops.segment_sum(xw[src] * norm[:, None], dst, num_segments=n)
            out = out + xw * (dinv * dinv)[:, None]
            return out + b_gcn
        return _graph_encoder(x, edge_index, edge_type, W_rel, W_root, b_rgcn, W_gcn, b_gcn)

    def _L1_gnn_ref(x, W1, b1, W2, b2, edge_index):
        import jax, jax.numpy as jnp
        import numpy as np
        N_NODES = 625
        D = 768
        N_EDGES = 10000

        def gcn_conv(x, W, b, src, dst, n_nodes):
            h = x @ W
            deg = jax.ops.segment_sum(jnp.ones_like(dst, dtype=h.dtype), dst, num_segments=n_nodes)
            dinv = jnp.where(deg > 0, jax.lax.rsqrt(deg), 0.0)
            norm = dinv[src] * dinv[dst]
            msgs = h[src] * norm[:, None]
            out = jax.ops.segment_sum(msgs, dst, num_segments=n_nodes)
            return out + b

        def add_self_loops(edge_index, n_nodes):
            loop = jnp.arange(n_nodes, dtype=edge_index.dtype)
            src = jnp.concatenate([edge_index[0], loop])
            dst = jnp.concatenate([edge_index[1], loop])
            return (src, dst)
        n = x.shape[0]
        src, dst = add_self_loops(edge_index, n)
        h = gcn_conv(x, W1, b1, src, dst, n)
        h = jax.nn.relu(h)
        out = gcn_conv(h, W2, b2, src, dst, n)
        return out

    def _L2_gnn_ref(x, node_type, edge_index, edge_type, node_emb, w_rel1, w_root1, b1, w_rel2, w_root2, b2, w_rel3, w_root3, b3):
        import jax, jax.numpy as jnp
        import numpy as np
        NUM_NODES = 625
        NUM_EDGES = 10000
        IN_CH = 768
        TYPE_DIM = 128
        HID = 768
        OUT = 768
        NUM_REL = 3
        NUM_NODE_TYPE = 3

        def _glorot(key, shape):
            fan_in, fan_out = (shape[-2], shape[-1])
            lim = (6.0 / (fan_in + fan_out)) ** 0.5
            return jax.random.uniform(key, shape, jnp.float32, -lim, lim)

        def rgcn_conv(h, src, dst, edge_type, w_rel, w_root, bias):
            num_nodes = h.shape[0]
            xw = jnp.einsum('nd,rde->rne', h, w_rel)
            msg = xw[edge_type, src]
            onehot = jax.nn.one_hot(edge_type, NUM_REL, dtype=h.dtype)
            count = jax.ops.segment_sum(onehot, dst, num_segments=num_nodes)
            inv = jnp.where(count > 0, 1.0 / jnp.maximum(count, 1.0), 0.0)
            msg = msg * inv[dst, edge_type][:, None]
            agg = jax.ops.segment_sum(msg, dst, num_segments=num_nodes)
            return agg + h @ w_root + bias
        src, dst = (edge_index[0], edge_index[1])
        h = jnp.concatenate([x, node_emb[node_type]], axis=-1)
        h = jax.nn.relu(rgcn_conv(h, src, dst, edge_type, w_rel1, w_root1, b1))
        h = jax.nn.relu(rgcn_conv(h, src, dst, edge_type, w_rel2, w_root2, b2))
        h = jax.nn.relu(rgcn_conv(h, src, dst, edge_type, w_rel3, w_root3, b3))
        return h

    def _L3_gnn_ref(x, edge_index, W, b):
        import jax, jax.numpy as jnp
        import numpy as np
        N_NODES = 625
        N_EDGES = 6250
        DIM = 768
        n = x.shape[0]
        loop = jnp.arange(n, dtype=edge_index.dtype)
        src = jnp.concatenate([edge_index[0], loop])
        dst = jnp.concatenate([edge_index[1], loop])
        deg = jax.ops.segment_sum(jnp.ones_like(dst, dtype=x.dtype), dst, num_segments=n)
        deg_inv_sqrt = jnp.where(deg > 0, jax.lax.rsqrt(deg), 0.0)
        norm = deg_inv_sqrt[src] * deg_inv_sqrt[dst]
        h = x @ W
        msg = h[src] * norm[:, None]
        out = jax.ops.segment_sum(msg, dst, num_segments=n)
        return out + b
    edge_index = jnp.stack([src, dst])
    h = jnp.maximum(_layernorm(x, axis=-1), 0.0)
    x = x + _L0_gnn_ref(h, edge_index, edge_type_34, L0_gnn_W_rel, L0_gnn_W_root, L0_gnn_b_rgcn, L0_gnn_W_gcn, L0_gnn_b_gcn)
    h = jnp.maximum(_layernorm(x, axis=-1), 0.0)
    x = x + _L1_gnn_ref(h, L1_gnn_W1, L1_gnn_b1, L1_gnn_W2, L1_gnn_b2, edge_index)
    h = jnp.maximum(_layernorm(x, axis=-1), 0.0)
    x = x + _L2_gnn_ref(h, node_type_3, edge_index, edge_type_3, L2_gnn_node_emb, L2_gnn_w_rel1, L2_gnn_w_root1, L2_gnn_b1, L2_gnn_w_rel2, L2_gnn_w_root2, L2_gnn_b2, L2_gnn_w_rel3, L2_gnn_w_root3, L2_gnn_b3)
    h = jnp.maximum(_layernorm(x, axis=-1), 0.0)
    x = x + _L3_gnn_ref(h, edge_index, L3_gnn_W, L3_gnn_b)
    return x

_drawn_inputs = setup_inputs


def setup_inputs(seed=0):
    import zlib

    import numpy as np

    out = dict(_drawn_inputs(seed))
    spreads = {'L0_gnn_b_rgcn': (0.0, 0.1),
     'L0_gnn_b_gcn': (0.0, 0.1),
     'L1_gnn_b1': (0.0, 0.1),
     'L1_gnn_b2': (0.0, 0.1),
     'L2_gnn_b1': (0.0, 0.1),
     'L2_gnn_b2': (0.0, 0.1),
     'L2_gnn_b3': (0.0, 0.1),
     'L3_gnn_b': (0.0, 0.1)}
    factors = {}
    for name, (base, spread) in spreads.items():
        noise = np.random.default_rng([zlib.crc32(name.encode()), seed]).standard_normal(out[name].shape)
        drawn = base * np.exp(spread * noise) if base else spread * noise
        out[name] = jnp.asarray(drawn.astype(out[name].dtype))
    for name, factor in factors.items():
        out[name] = (out[name] * factor).astype(out[name].dtype)
    return out
```

```python
from contextlib import ExitStack

import concourse.bass as bass
from concourse import mybir

ALU = mybir.AluOpType
ACT = mybir.ActivationFunctionType
AX_X = mybir.AxisListType.X
F32 = mybir.dt.float32
F32R = mybir.dt.float32r
F16 = mybir.dt.float16
I32 = mybir.dt.int32
U16 = mybir.dt.uint16

N = 625
NT = 5
NP = N // NT
NPC = NP + 1
NC = NT * NPC
PART = (3 * NPC, 2 * NPC)
BANK = 512
LEFT = BANK - PART[0]
E = 10625
EP = 125
EC = E // EP
SLOT = 128
EPS = 1e-5


def column(n_tile):
    return n_tile * NPC


def slots_of(keys):
    return E // SLOT + keys


def semaphores(nc, tag, ctx):
    made = []

    def clear():
        nc.clear_and_free_semaphores(made)
        nc.all_engine_barrier()

    ctx.callback(clear)

    def sem(name):
        made.append(nc.alloc_semaphore(f"{tag}_{name}"))
        return made[-1]

    return sem


def slot_tile(nc, i, keys):
    return nc.s_assert_within(i, 0, slots_of(keys) - 1, skip_runtime_bounds_check_because="all edges fit slots_of(keys) tiles")


def sort_edges(nc, tag, src, dst, etype, keys, slot_src, slot_dst, counts):
    slots = slots_of(keys)
    chunk = 17 if 2 * slots > 256 else 17
    assert EC % chunk == 0 and 2 * slots <= BANK
    with ExitStack() as ctx:
        def sb(name, shape, dt):
            return ctx.enter_context(nc.sbuf_tensor(f"{tag}_{name}", shape, dt))

        sem = semaphores(nc, tag, ctx)

        raw = sb("raw", [EP, 3, EC], I32)
        val = sb("val", [EP, 3, EC], F32)
        node_tile = sb("node_tile", [EP, 2, EC], F32)
        key = sb("key", [EP, EC], F32)
        local_src = sb("local_src", [EP, EC], F32)
        col_dst = sb("col_dst", [EP, EC], F32)
        key_iota = sb("key_iota", [EP, keys], F32)
        is_key = sb("is_key", [EP, keys, EC], F16)
        running = sb("running", [EP, keys, EC], F32)
        zeros = sb("zeros", [EP, 1], F32)
        part_cnt = sb("part_cnt", [EP, keys], F16)
        before = sb("before", [EP, keys], F32)
        lower = sb("lower", [EP, EP], F16)
        ones = sb("ones", [EP, 128], F16)
        total_i = sb("total_i", [EP, keys], I32)
        tiles_f = sb("tiles_f", [EP, keys], F32)
        tiles_end = sb("tiles_end", [EP, keys], F32)
        base = sb("base", [EP, keys], F32)
        pos = sb("pos", [EP, EC], F32)
        pos_i = sb("pos_i", [EP, EC], I32)
        hi_i = sb("hi_i", [EP, EC], I32)
        lo_i = sb("lo_i", [EP, EC], I32)
        hi = sb("hi", [EP, EC], F32)
        lo = sb("lo", [EP, EC], F32)
        slot_iota = sb("slot_iota", [EP, SLOT], F16)
        tile_iota = sb("tile_iota", [EP, slots], F16)
        is_slot = sb("is_slot", [EP, chunk, SLOT], F16)
        is_tile = sb("is_tile", [EP, chunk, slots], F16)
        load = sb("load", [EP, chunk, 2, slots], F16)
        ps_cnt = ctx.enter_context(nc.psum_tensor(f"{tag}_ps_cnt", [EP, 2, BANK], F32))
        ps_slot = ctx.enter_context(nc.psum_tensor(f"{tag}_ps_slot", [SLOT, BANK], F32))

        loaded = sem("loaded")
        consts_ready = sem("consts_ready")
        counted = sem("counted")
        summed = sem("summed")
        chunk_ready = sem("chunk_ready")
        chunk_used = sem("chunk_used")
        step = sem("step")
        done = sem("done")

        block = ctx.enter_context(nc.Block())

        @block.sync
        def _(sp):
            for i, a in enumerate((src, dst, etype)):
                sp.dma_start(raw[:, i, :], a.rearrange("(p c) -> p c", p=EP)).then_inc(loaded, 16)

        @block.gpsimd
        def _(pool):
            nc.gpsimd.iota(key_iota[:], [[1, keys]], base=0, channel_multiplier=0,
                           allow_small_or_imprecise_dtypes=True).then_inc(consts_ready, 1)
            nc.gpsimd.iota(slot_iota[:], [[1, SLOT]], base=0, channel_multiplier=0,
                           allow_small_or_imprecise_dtypes=True).then_inc(consts_ready, 1)
            nc.gpsimd.iota(tile_iota[:], [[1, slots]], base=0, channel_multiplier=0,
                           allow_small_or_imprecise_dtypes=True).then_inc(consts_ready, 1)
            nc.gpsimd.memset(ones[:], 1.0).then_inc(consts_ready, 1)
            nc.gpsimd.memset(zeros[:], 0.0).then_inc(consts_ready, 1)
            nc.gpsimd.memset(lower[:], 1.0).then_inc(consts_ready, 1)
            pool.wait_ge(consts_ready, 6)
            nc.gpsimd.affine_select(out=lower[:], in_=lower[:], compare_op=ALU.is_gt, fill=0.0, base=0,
                                    pattern=[[1, EP]], channel_multiplier=-1).then_inc(consts_ready, 1)

        @block.vector
        def _(dve):
            chain = [0]

            def then(ins):
                chain[0] += 1
                ins.then_inc(step, 1)
                dve.wait_ge(step, chain[0])

            v = nc.vector
            dve.wait_ge(loaded, 48)
            then(v.tensor_copy(val[:], raw[:]))
            then(v.tensor_scalar(node_tile[:], val[:, 0:2, :], float(NP), None, ALU.is_ge))
            for j in range(2, NT):
                then(v.scalar_tensor_tensor(node_tile[:], val[:, 0:2, :], float(j * NP), node_tile[:],
                                            ALU.is_ge, ALU.add))
            then(v.scalar_tensor_tensor(local_src[:], node_tile[:, 0, :], float(-NP), val[:, 0, :], ALU.mult, ALU.add))
            then(v.tensor_tensor(col_dst[:], node_tile[:, 1, :], val[:, 1, :], ALU.add))
            then(v.scalar_tensor_tensor(key[:], val[:, 2, :], float(NT), node_tile[:, 0, :], ALU.mult, ALU.add))
            dve.wait_ge(consts_ready, 7)
            then(v.tensor_tensor(is_key[:], key_iota[:].unsqueeze(2).broadcast_to([EP, keys, EC]),
                                 key[:].unsqueeze(1).broadcast_to([EP, keys, EC]), ALU.is_equal))
            flat = is_key[:].rearrange("p k c -> p (k c)")
            then(v.tensor_tensor_scan(running[:].rearrange("p k c -> p (k c)"), flat,
                                      zeros[:].broadcast_to([EP, keys * EC]), 0.0, ALU.add, ALU.add))
            ends = running[:, :, EC - 1]
            then(v.tensor_copy(part_cnt[:, 0:1], ends[:, 0:1]))
            v.tensor_tensor(part_cnt[:, 1:keys], ends[:, 1:keys], ends[:, 0:keys - 1], ALU.subtract).then_inc(counted, 1)
            dve.wait_ge(summed, 1)
            then(v.tensor_scalar(total_i[:], ps_cnt[:, 1, 0:keys], float(SLOT - 1), None, ALU.add))
            then(v.tensor_scalar(total_i[:], total_i[:], 7, None, ALU.logical_shift_right))
            then(v.tensor_scalar(tiles_f[:], total_i[:], 1.0, None, ALU.max))
            then(v.tensor_tensor_scan(tiles_end[:], tiles_f[:], zeros[:].broadcast_to([EP, keys]), 0.0, ALU.add, ALU.add))
            then(v.tensor_tensor(base[:], tiles_end[:], tiles_f[:], ALU.subtract))
            then(v.tensor_copy(counts[0:1, 0, 0:keys], base[0:1, :]))
            then(v.tensor_copy(counts[0:1, 1, 0:keys], tiles_f[0:1, :]))
            then(v.scalar_tensor_tensor(before[:], base[:], float(SLOT), ps_cnt[:, 0, 0:keys], ALU.mult, ALU.add))
            then(v.tensor_scalar(before[:], before[:], 1.0, None, ALU.subtract))
            then(v.tensor_tensor(before[:, 1:keys], before[:, 1:keys], ends[:, 0:keys - 1], ALU.subtract))
            then(v.tensor_tensor(running[:], running[:], before[:].unsqueeze(2).broadcast_to([EP, keys, EC]), ALU.add))
            then(v.tensor_tensor(running[:], running[:], is_key[:], ALU.mult))
            then(v.tensor_reduce(pos[:], running[:].rearrange("p k c -> p c k"), AX_X, ALU.add))
            then(v.tensor_copy(pos_i[:], pos[:]))
            then(v.tensor_scalar(hi_i[:], pos_i[:], 7, None, ALU.logical_shift_right))
            then(v.tensor_scalar(lo_i[:], pos_i[:], SLOT - 1, None, ALU.bitwise_and))
            then(v.tensor_copy(hi[:], hi_i[:]))
            then(v.tensor_copy(lo[:], lo_i[:]))
            then(v.tensor_scalar(local_src[:], local_src[:], 1.0, None, ALU.add))
            then(v.tensor_scalar(col_dst[:], col_dst[:], 1.0, None, ALU.add))
            for n in range(EC // chunk):
                at = slice(n * chunk, (n + 1) * chunk)
                if n:
                    dve.wait_ge(chunk_used, n)
                v.tensor_tensor(is_slot[:], slot_iota[:].unsqueeze(1).broadcast_to([EP, chunk, SLOT]),
                                lo[:, at].unsqueeze(2).broadcast_to([EP, chunk, SLOT]), ALU.is_equal)
                then(v.tensor_tensor(is_tile[:], tile_iota[:].unsqueeze(1).broadcast_to([EP, chunk, slots]),
                                     hi[:, at].unsqueeze(2).broadcast_to([EP, chunk, slots]), ALU.is_equal))
                v.tensor_tensor(load[:, :, 0, :], is_tile[:],
                                local_src[:, at].unsqueeze(2).broadcast_to([EP, chunk, slots]), ALU.mult)
                then(v.tensor_tensor(load[:, :, 1, :], is_tile[:],
                                     col_dst[:, at].unsqueeze(2).broadcast_to([EP, chunk, slots]), ALU.mult))
                v.engine_nop().then_inc(chunk_ready, 1)
            dve.wait_ge(done, 1)
            then(v.tensor_scalar(slot_src[:, 0:slots], ps_slot[:, 0:slots], 1.0, None, ALU.subtract))
            then(v.tensor_scalar(slot_dst[:, 0:slots], ps_slot[:, slots:2 * slots], 1.0, None, ALU.subtract))

        @block.tensor
        def _(pe):
            pe.wait_ge(consts_ready, 7)
            pe.wait_ge(counted, 1)
            nc.tensor.matmul(ps_cnt[:, 0, 0:keys], lower[:], part_cnt[:], start=True, stop=True)
            nc.tensor.matmul(ps_cnt[:, 1, 0:keys], ones[:, 0:EP], part_cnt[:], start=True, stop=True).then_inc(summed, 1)
            for n in range(EC // chunk):
                pe.wait_ge(chunk_ready, n + 1)
                for c in range(chunk):
                    last = nc.tensor.matmul(ps_slot[:, 0:2 * slots], is_slot[:, c, :],
                                            load[:, c].rearrange("p a s -> p (a s)"),
                                            start=(n == 0 and c == 0), stop=(n == EC // chunk - 1 and c == chunk - 1))
                last.then_inc(chunk_used, 1)
            pe.wait_ge(chunk_used, EC // chunk)
            nc.tensor.nop().then_inc(done, 1)


def build_adjacency(nc, tag, keys, slot_src, slot_dst, counts, adj):
    assert keys % 2 == 0
    with ExitStack() as ctx:
        def sb(name, shape, dt):
            return ctx.enter_context(nc.sbuf_tensor(f"{tag}_{name}", shape, dt))

        sem = semaphores(nc, tag, ctx)

        node_iota = sb("node_iota", [SLOT, NC], F16)
        is_src = sb("is_src", [SLOT, 2, NP], F16)
        is_dst = sb("is_dst", [SLOT, 2, NC], F16)
        zeros = sb("zeros", [SLOT, 2 * BANK], F16)
        cnt = sb("cnt", [NP, 2, NC], U16)
        ps = ctx.enter_context(nc.psum_tensor(f"{tag}_ps", [NP, 2, 2 * BANK], F32))

        consts_ready = sem("consts_ready")
        onehots_ready = sem("onehots_ready")
        onehots_free = sem("onehots_free")
        counted = sem("counted")
        copied = sem("copied")
        stored = [sem(f"stored{b}") for b in range(2)]

        block = ctx.enter_context(nc.Block())

        @block.gpsimd
        def _(pool):
            nc.gpsimd.iota(node_iota[:], [[1, NC]], base=0, channel_multiplier=0,
                           allow_small_or_imprecise_dtypes=True).then_inc(consts_ready, 1)
            nc.gpsimd.memset(zeros[:], 0.0).then_inc(consts_ready, 1)

        @block.vector
        def _(dve):
            dve.wait_ge(consts_ready, 2)
            first = dve.value_load(counts[0:1, 0, keys - 1:keys], min_val=0, max_val=slots_of(keys))
            last = dve.value_load(counts[0:1, 1, keys - 1:keys], min_val=1, max_val=slots_of(keys))
            with dve.Fori(0, first + last) as tile:
                i = slot_tile(nc, tile, keys)
                dve.wait_ge(onehots_free, i + 1)
                nc.vector.tensor_scalar(is_src[:, i % 2, :], node_iota[:, 0:NP], slot_src[:, bass.ds(i, 1)], None,
                                        ALU.is_equal)
                nc.vector.tensor_scalar(is_dst[:, i % 2, :], node_iota[:], slot_dst[:, bass.ds(i, 1)], None,
                                        ALU.is_equal).then_inc(onehots_ready, 1)

        @block.tensor
        def _(pe):
            pe.wait_ge(consts_ready, 2)
            nc.tensor.nop().then_inc(onehots_free, 2)
            with pe.Fori(0, keys // 2) as pair:
                for b in range(2):
                    key = 2 * pair + b
                    pe.wait_ge(copied, key + 1)
                    for h in range(2):
                        nc.tensor.matmul(ps[:, b, h * BANK:(h + 1) * BANK], zeros[:, 0:NP], zeros[:, 0:BANK],
                                         start=True, stop=False)
                    first = pe.value_load(counts[0:1, 0, bass.ds(key, 1)], min_val=0, max_val=slots_of(keys))
                    tiles = pe.value_load(counts[0:1, 1, bass.ds(key, 1)], min_val=1, max_val=slots_of(keys))
                    with pe.Fori(first, first + tiles) as tile:
                        i = slot_tile(nc, tile, keys)
                        pe.wait_ge(onehots_ready, i + 1)
                        for h in range(2):
                            cols = slice(0, PART[0]) if h == 0 else slice(PART[0], NC)
                            at = LEFT if h == 0 else BANK
                            mm = nc.tensor.matmul(ps[:, b, at:at + PART[h]], is_src[:, i % 2, :],
                                                  is_dst[:, i % 2, cols], start=False, stop=False)
                        mm.then_inc(onehots_free, 1)
                    for h in range(2):
                        mm = nc.tensor.matmul(ps[:, b, h * BANK:(h + 1) * BANK], zeros[:, 0:NP], zeros[:, 0:BANK],
                                              start=False, stop=True)
                    mm.then_inc(counted, 1)

        @block.scalar
        def _(act):
            nc.scalar.preload_act_table(ACT.Copy)
            nc.scalar.nop().then_inc(copied, 2)

            def copy(pair, first):
                for b in range(2):
                    act.wait_ge(counted, 2 * pair + b + 1)
                    if not first:
                        act.wait_ge(stored[b], pair * 16)
                    nc.scalar.copy(cnt[:, b, :], ps[:, b, LEFT:LEFT + NC]).then_inc(copied, 1)

            copy(0, True)
            with act.Fori(1, keys // 2) as pair:
                copy(pair, False)

        @block.sync
        def _(sp):
            with sp.Fori(0, keys // 2) as pair:
                for b in range(2):
                    sp.wait_ge(copied, 2 * pair + b + 3)
                    sp.dma_start(adj[bass.ds(2 * pair + b, 1), :, :].rearrange("k p c -> p (k c)"),
                                 cnt[:, b, :]).then_inc(stored[b], 16)
            for b in range(2):
                sp.wait_ge(stored[b], 8 * keys)


def newton_rsqrt(v, then, out, d, half, tmp):
    then(v.tensor_tensor(tmp, out, out, ALU.mult))
    then(v.tensor_tensor(tmp, tmp, d, ALU.mult))
    then(v.tensor_scalar(tmp, tmp, -0.5, 1.5, ALU.mult, ALU.add))
    then(v.tensor_tensor(out, out, tmp, ALU.mult))


def sum_adjacency(nc, tag, adj, types, adj_all, dinv, ident):
    with ExitStack() as ctx:
        def sb(name, shape, dt):
            return ctx.enter_context(nc.sbuf_tensor(f"{tag}_{name}", shape, dt))

        sem = semaphores(nc, tag, ctx)

        part = sb("part", [NP, types * NT, NC], U16)
        total = sb("total", [NP, NT, NC], F32)
        ones = sb("ones", [NP, 2], F32)
        deg = sb("deg", [NP, NT], F32)
        tmp = sb("tmp", [NP, NT], F32)
        ps = ctx.enter_context(nc.psum_tensor(f"{tag}_ps", [NP, NT, 2], F32))

        loaded = sem("loaded")
        summed = sem("summed")
        counted = sem("counted")
        inverted = sem("inverted")
        rooted = sem("rooted")
        step = sem("step")

        block = ctx.enter_context(nc.Block())

        @block.sync
        def _(sp):
            sp.dma_start(part[:], adj[0:types * NT, :, :].rearrange("k p c -> p k c")).then_inc(loaded, 16)

        @block.vector
        def _(dve):
            chain = [0]

            def then(ins):
                chain[0] += 1
                ins.then_inc(step, 1)
                dve.wait_ge(step, chain[0])

            v = nc.vector
            v.memset(ones[:], 1.0)
            dve.wait_ge(loaded, 16)
            then(v.tensor_tensor(total[:], part[:, 0:NT, :], part[:, NT:2 * NT, :], ALU.add))
            for t in range(2, types):
                then(v.tensor_tensor(total[:], total[:], part[:, t * NT:(t + 1) * NT, :], ALU.add))
            for k in range(NT):
                own = total[:, k, column(k):column(k) + NP]
                then(v.tensor_tensor(own, own, ident[0:NP, 0:NP], ALU.add))
            v.tensor_copy(adj_all[:], total[:]).then_inc(summed, 1)
            dve.wait_ge(counted, 1)
            then(v.tensor_copy(deg[:], ps[:, :, 0]))
            v.reciprocal(dinv[:], deg[:]).then_inc(inverted, 1)
            dve.wait_ge(rooted, 1)
            newton_rsqrt(v, then, dinv[:], deg[:], None, tmp[:])

        @block.scalar
        def _(act):
            act.wait_ge(inverted, 1)
            nc.scalar.activation(dinv[:], dinv[:], ACT.Sqrt).then_inc(rooted, 1)

        @block.tensor
        def _(pe):
            pe.wait_ge(summed, 1)
            for d in range(NT):
                for k in range(NT):
                    last = nc.tensor.matmul(ps[:, d, :], total[:, k, column(d):column(d) + NP], ones[:],
                                            start=(k == 0 and d == 0), stop=(k == NT - 1 and d == NT - 1),
                                            skip_group_check=True)
            last.then_inc(counted, 1)


def normalise(nc, tag, x, h, extra=None):
    width = x.shape[2]
    with ExitStack() as ctx:
        def sb(name, shape, dt):
            return ctx.enter_context(nc.sbuf_tensor(f"{tag}_{name}", shape, dt))

        sem = semaphores(nc, tag, ctx)

        stats = sb("stats", [NP, NT, 2, 6], F32)
        moments = sb("moments", [NP, NT, 2], F32)
        var = sb("var", [NP, NT], F32)
        rstd = sb("rstd", [NP, NT], F32)
        tmp = sb("tmp", [NP, NT], F32)
        if extra is not None:
            types, emb = extra
            rows, dim = emb.shape
            type_i = sb("type_i", [NP, NT], I32)
            type_f = sb("type_f", [NP, NT], F32)
            is_type = sb("is_type", [NP, NT], F32)
            emb_rows = sb("emb_rows", [NP, rows, dim], F32)

        loaded = sem("loaded")
        inverted = sem("inverted")
        rooted = sem("rooted")
        step = sem("step")

        block = ctx.enter_context(nc.Block())

        if extra is not None:
            @block.sync
            def _(sp):
                with nc.allow_non_contiguous_dma(reason="five node types per partition"):
                    sp.dma_start(type_i[:], types.rearrange("(k p) -> p k", p=NP)).then_inc(loaded, 16)
                sp.dma_start(emb_rows[:], emb.unsqueeze(0).broadcast_to([NP, rows, dim])).then_inc(loaded, 16)

        @block.scalar
        def _(act):
            act.wait_ge(inverted, 1)
            nc.scalar.activation(rstd[:], rstd[:], ACT.Sqrt).then_inc(rooted, 1)

        @block.vector
        def _(dve):
            chain = [0]

            def then(ins):
                chain[0] += 1
                ins.then_inc(step, 1)
                dve.wait_ge(step, chain[0])

            v = nc.vector
            for k in range(NT):
                for half in range(2):
                    last = v.bn_stats(stats[:, k, half, :], x[:, k, half * (width // 2):(half + 1) * (width // 2)])
            then(last)
            for k in range(NT):
                last = v.bn_aggr(moments[:, k, :], stats[:, k])
            then(last)
            then(v.tensor_scalar(var[:], moments[:, :, 1], EPS, None, ALU.add))
            v.reciprocal(rstd[:], var[:]).then_inc(inverted, 1)
            dve.wait_ge(rooted, 1)
            newton_rsqrt(v, then, rstd[:], var[:], None, tmp[:])
            for k in range(NT):
                last = v.tensor_scalar(h[:, k, 0:width], x[:, k, :], moments[:, k, 0:1], rstd[:, k:k + 1],
                                       ALU.subtract, ALU.mult)
            then(last)
            v.tensor_scalar(h[:, :, 0:width], h[:, :, 0:width], 0.0, None, ALU.max)
            if extra is not None:
                dve.wait_ge(loaded, 32)
                then(v.tensor_copy(type_f[:], type_i[:]))
                for t in range(rows):
                    then(v.tensor_scalar(is_type[:], type_f[:], float(t), None, ALU.is_equal))
                    for k in range(NT):
                        out = h[:, k, width:width + dim]
                        if t == 0:
                            last = v.tensor_scalar(out, emb_rows[:, t, :], is_type[:, k:k + 1], None, ALU.mult)
                        else:
                            last = v.scalar_tensor_tensor(out, emb_rows[:, t, :], is_type[:, k:k + 1], out,
                                                          ALU.mult, ALU.add)
                    then(last)


def layer(nc, tag, h, width, out_width, bias, w_rel, relations, adj=None, w_root=None, adj_all=None, dinv=None,
          relu=False, x=None, ident=None):
    mean = adj is not None
    fc = width // 128
    half = out_width // 2
    steps = relations + (w_root is not None)
    ring = 3
    with ExitStack() as ctx:
        def sb(name, shape, dt):
            return ctx.enter_context(nc.sbuf_tensor(f"{tag}_{name}", shape, dt))

        sem = semaphores(nc, tag, ctx)

        h_hi = sb("h_hi", [NP, NT, width], F32R)
        h_lo = sb("h_lo", [NP, NT, width], F32R)
        a_raw = sb("a_raw", [NP, NT, NC], U16) if mean else None
        a = sb("a", [NP, NT, NC], F32R)
        ones = sb("ones", [NP, 128], F32R) if mean else None
        ones_f = sb("ones_f", [NP, 128], F32) if mean else None
        inv = sb("inv", [128, NC], F32) if mean else None
        scaled = sb("scaled", [128, 2, NC], F32) if mean else None
        g_hi = sb("g_hi", [128, fc, NC], F32R)
        g_lo = sb("g_lo", [128, fc, NC], F32R)
        w_raw = sb("w_raw", [128, ring, out_width], F32)
        w_hi = sb("w_hi", [128, fc, out_width], F32R)
        w_lo = sb("w_lo", [128, fc, out_width], F32R)
        bias_rows = sb("bias_rows", [NP, out_width], F32)
        ps_g = ctx.enter_context(nc.psum_tensor(f"{tag}_ps_g", [128, 2, 2 * BANK], F32))
        ps_o = ctx.enter_context(nc.psum_tensor(f"{tag}_ps_o", [128, 2, 2, BANK], F32))

        bias_loaded = sem("bias_loaded")
        w_loaded = [sem(f"w_loaded{s}") for s in range(ring)]
        w_hi_ready = sem("w_hi_ready")
        w_ready = sem("w_ready")
        h_scaled = sem("h_scaled")
        h_hi_ready = sem("h_hi_ready")
        h_ready = sem("h_ready")
        a_loaded = sem("a_loaded")
        a_ready = sem("a_ready")
        ones_ready = sem("ones_ready")
        inv_ready = sem("inv_ready")
        g_summed = sem("g_summed")
        g_freed = sem("g_freed")
        g_hi_ready = sem("g_hi_ready")
        g_ready = sem("g_ready")
        o_summed = sem("o_summed")
        o_taken = sem("o_taken")
        done = sem("done")

        root = w_root is not None
        per = fc + 1 if mean else fc

        def sums_before(r):
            return (fc if root else 0) + r * per

        def step_of(r):
            return r + root

        def all_nodes(cols):
            return cols.rearrange("p (k c) -> p k c", c=NPC)[:, :, 0:NP]

        block = ctx.enter_context(nc.Block())

        @block.sync
        def _(sp):
            def load_w(w, s):
                for f in range(fc):
                    if f >= ring:
                        sp.wait_ge(w_ready, s * fc + f - ring + 1)
                    elif not (isinstance(s, int) and s == 0):
                        sp.wait_ge(w_ready, s * fc - (fc - 1 - last_in(f)))
                    sp.dma_start(w_raw[:, f % ring, :], w(f)).then_inc(w_loaded[f % ring], 16)

            def last_in(place):
                return max(f for f in range(fc) if f % ring == place)

            sp.dma_start(bias_rows[:], bias.unsqueeze(0).broadcast_to([NP, out_width])).then_inc(bias_loaded, 16)
            if root:
                load_w(lambda f: w_root[f * 128:(f + 1) * 128, :], 0)
            if mean:
                with sp.Fori(0, relations) as r:
                    sp.wait_ge(a_ready, r + 1)
                    sp.dma_start(a_raw[:], adj[bass.ds(r * NT, NT), :, :].rearrange("k p c -> p k c")).then_inc(a_loaded, 16)
                    load_w(lambda f: w_rel[bass.ds(r, 1), f * 128:(f + 1) * 128, :].rearrange("a f o -> f (a o)"), step_of(r))
            else:
                load_w(lambda f: w_rel[f * 128:(f + 1) * 128, :], 0)

        @block.gpsimd
        def _(pool):
            if mean:
                nc.gpsimd.memset(ones_f[:], 1.0).then_inc(ones_ready, 1)
                pool.wait_ge(ones_ready, 1)
                nc.gpsimd.tensor_copy(ones[:], ones_f[:]).then_inc(ones_ready, 1)
            else:
                nc.gpsimd.tensor_copy(a[:], adj_all[:]).then_inc(a_ready, 1)

        @block.scalar
        def _(act):
            nc.scalar.preload_act_table(ACT.Copy)
            if dinv is not None:
                act.wait_ge(h_scaled, 1)
            for k in range(NT):
                nc.scalar.copy(h_hi[:, k, :], h[:, k, 0:width]).then_inc(h_hi_ready, 1)

            def chunk(s, f, to, source, uses, which, k):
                act.wait_ge(w_loaded[f % ring], 16 * (s * uses + f // ring + 1))
                if f == 0 and not (isinstance(s, int) and s == 0):
                    act.wait_ge(o_summed, s * NT)
                nc.scalar.copy(w_hi[:, f, :], w_raw[:, f % ring, :]).then_inc(w_hi_ready, 1)
                act.wait_ge(which, k)
                nc.scalar.copy(to, source).then_inc(g_hi_ready, 1)

            def uses_of(f):
                return len([g for g in range(fc) if g % ring == f % ring])

            if root:
                for f in range(fc):
                    chunk(0, f, all_nodes(g_hi[:, f, :]), all_nodes(ps_g[:, f % 2, LEFT:LEFT + NC]), uses_of(f),
                          g_summed, f + 1)
            if mean:
                nc.scalar.nop().then_inc(a_ready, 1)
                with act.Fori(0, relations) as r:
                    act.wait_ge(a_loaded, 16 * r + 16)
                    act.wait_ge(g_summed, sums_before(r))
                    nc.scalar.copy(a[:], a_raw[:]).then_inc(a_ready, 1)
                    for f in range(fc):
                        chunk(step_of(r), f, g_hi[:, f, :], scaled[:, f % 2, :], uses_of(f), g_freed, r * per + f + 3)
            else:
                for f in range(fc):
                    chunk(0, f, g_hi[:, f, :], ps_g[:, f % 2, LEFT:LEFT + NC], uses_of(f), g_summed, f + 1)

        @block.vector
        def _(dve):
            v = nc.vector
            if dinv is not None:
                for k in range(NT):
                    last = v.tensor_scalar(h[:, k, 0:width], h[:, k, 0:width], dinv[:, k:k + 1], None, ALU.mult)
                last.then_inc(h_scaled, 1)
                dve.wait_ge(h_scaled, 1)
            for k in range(NT):
                dve.wait_ge(h_hi_ready, k + 1)
                v.tensor_tensor(h_lo[:, k, :], h[:, k, 0:width], h_hi[:, k, :].bitcast(F32), ALU.subtract).then_inc(h_ready, 1)

            def w_low(s, f):
                dve.wait_ge(w_hi_ready, s * fc + f + 1)
                v.tensor_tensor(w_lo[:, f, :], w_raw[:, f % ring, :], w_hi[:, f, :].bitcast(F32),
                                ALU.subtract).then_inc(w_ready, 1)

            def g_low(s, f, source, only=lambda cols: cols):
                dve.wait_ge(g_hi_ready, s * fc + f + 1)
                v.tensor_tensor(only(g_lo[:, f, :]), only(source), only(g_hi[:, f, :].bitcast(F32)),
                                ALU.subtract).then_inc(g_ready, 1)

            def take(s, first):
                for d in range(NT):
                    dve.wait_ge(o_summed, s * NT + d + 1)
                    ps = ps_o[0:NP, d % 2, :, 0:half]
                    to = h[:, d, 0:out_width].rearrange("p (a o) -> p a o", a=2)
                    by = dinv[:, d:d + 1] if dinv is not None else 1.0
                    if first:
                        base = bias_rows[:].rearrange("p (a o) -> p a o", a=2)
                    else:
                        base = to
                    v.scalar_tensor_tensor(to, ps, by, base, ALU.mult, ALU.add).then_inc(o_taken, 1)

            dve.wait_ge(bias_loaded, 16)
            if root:
                for f in range(fc):
                    w_low(0, f)
                    g_low(0, f, ps_g[:, f % 2, LEFT:LEFT + NC], all_nodes)
                take(0, True)
            if mean:
                v.engine_nop().then_inc(g_freed, 1)
                with dve.Fori(0, relations) as r:
                    s = step_of(r)
                    dve.wait_ge(g_summed, sums_before(r) + 1)
                    v.tensor_scalar(inv[:], ps_g[:, 0, LEFT:LEFT + NC], 1.0, None, ALU.max).then_inc(g_freed, 1)
                    dve.wait_ge(g_freed, r * per + 2)
                    v.reciprocal(inv[:], inv[:]).then_inc(inv_ready, 1)
                    dve.wait_ge(inv_ready, r + 1)
                    for f in range(fc + 1):
                        if f < fc:
                            dve.wait_ge(g_summed, sums_before(r) + f + 2)
                            if f >= 2:
                                dve.wait_ge(g_ready, s * fc + f - 1)
                            v.tensor_tensor(scaled[:, f % 2, :], ps_g[:, (f + 1) % 2, LEFT:LEFT + NC], inv[:],
                                            ALU.mult).then_inc(g_freed, 1)
                            w_low(s, f)
                        if f >= 1:
                            dve.wait_ge(g_freed, r * per + f + 2)
                            g_low(s, f - 1, scaled[:, (f - 1) % 2, :])
                    take(s, False)
            else:
                for f in range(fc):
                    w_low(0, f)
                    g_low(0, f, ps_g[:, f % 2, LEFT:LEFT + NC])
                take(0, True)
            dve.wait_ge(o_taken, steps * NT)
            if relu:
                v.tensor_scalar(h[:, :, 0:out_width], h[:, :, 0:out_width], 0.0, None, ALU.max).then_inc(done, 1)
                dve.wait_ge(done, 1)
            if x is not None:
                v.tensor_tensor(x[:], x[:], h[:, :, 0:out_width], ALU.add)

        @block.tensor
        def _(pe):
            t = nc.tensor

            def products(s):
                for d in range(NT):
                    if d >= 2:
                        pe.wait_ge(o_taken, s * NT + d - 1)
                    elif not (isinstance(s, int) and s == 0):
                        pe.wait_ge(o_taken, s * NT)
                    for a_half in range(2):
                        cols = slice(a_half * half, (a_half + 1) * half)
                        for f in range(fc):
                            if d == 0 and a_half == 0:
                                pe.wait_ge(g_ready, s * fc + f + 1)
                                pe.wait_ge(w_ready, s * fc + f + 1)
                            rows = slice(column(d), column(d) + NP)
                            out = ps_o[0:NP, d % 2, a_half, 0:half]
                            t.matmul(out, g_hi[:, f, rows], w_hi[:, f, cols], start=(f == 0), stop=False)
                            t.matmul(out, g_hi[:, f, rows], w_lo[:, f, cols], start=False, stop=False)
                            mm = t.matmul(out, g_lo[:, f, rows], w_hi[:, f, cols], start=False, stop=(f == fc - 1))
                    mm.then_inc(o_summed, 1)

            def over_edges(r, first):
                for f in range(fc):
                    if mean:
                        pe.wait_ge(g_freed, r * per + f + 1)
                    elif f >= 2:
                        pe.wait_ge(g_ready, f - 1)
                    buf = (first + f) % 2
                    for k in range(NT):
                        for part, rows in enumerate((h_hi, h_lo)):
                            for p in range(2):
                                at, cols = (LEFT, slice(0, PART[0])) if p == 0 else (BANK, slice(PART[0], NC))
                                mm = t.matmul(ps_g[:, buf, at:at + PART[p]], rows[:, k, f * 128:(f + 1) * 128],
                                              a[:, k, cols], start=(k == 0 and part == 0),
                                              stop=(k == NT - 1 and part == 1))
                    mm.then_inc(g_summed, 1)

            if root:
                for f in range(fc):
                    if f >= 2:
                        pe.wait_ge(g_ready, f - 1)
                    for d in range(NT):
                        at = LEFT + column(d)
                        mm = t.transpose(ps_g[:, f % 2, at:at + NP], h[:, d, f * 128:(f + 1) * 128], ident[0:NP, 0:NP])
                    mm.then_inc(g_summed, 1)
                pe.wait_ge(h_ready, NT)
                products(0)
            pe.wait_ge(h_ready, NT)
            if mean:
                pe.wait_ge(ones_ready, 2)
                with pe.Fori(0, relations) as r:
                    pe.wait_ge(a_ready, r + 2)
                    pe.wait_ge(g_freed, r * per + 1)
                    for k in range(NT):
                        for p in range(2):
                            at, cols = (LEFT, slice(0, PART[0])) if p == 0 else (BANK, slice(PART[0], NC))
                            mm = t.matmul(ps_g[:, 0, at:at + PART[p]], ones[:], a[:, k, cols],
                                          start=(k == 0), stop=(k == NT - 1))
                    mm.then_inc(g_summed, 1)
                    over_edges(r, 1)
                    products(step_of(r))
            else:
                pe.wait_ge(a_ready, 1)
                over_edges(0, 0)
                products(0)


def setup(nc, x_dram, x, ident):
    with ExitStack() as ctx:
        x_loaded = ctx.enter_context(nc.semaphore("x_loaded"))
        ident_cleared = ctx.enter_context(nc.semaphore("ident_cleared"))
        block = ctx.enter_context(nc.Block())

        @block.sync
        def _(sp):
            sp.dma_start(x[:], x_dram.rearrange("(k p) f -> p k f", p=NP)).then_inc(x_loaded, 16)
            sp.wait_ge(x_loaded, 16)

        @block.gpsimd
        def _(pool):
            nc.gpsimd.memset(ident[:], 0.0).then_inc(ident_cleared, 1)
            pool.wait_ge(ident_cleared, 1)
            nc.gpsimd.affine_select(out=ident[:], in_=ident[:], compare_op=ALU.not_equal, fill=1.0, base=0,
                                    pattern=[[-1, 128]], channel_multiplier=1)


def gnn_kernel(nc, d, out):
    dim = d["x"].shape[1]
    wide = dim + d["L2_gnn_node_emb"].shape[1]
    types0 = d["L0_gnn_W_rel"].shape[0]
    types2 = d["L2_gnn_w_rel1"].shape[0]
    keys0, keys2 = (t * NT + t * NT % 2 for t in (types0, types2))
    adj0 = nc.dram_tensor("adj0", (keys0, NP, NC), U16, kind="Internal").ap()
    adj2 = nc.dram_tensor("adj2", (keys2, NP, NC), U16, kind="Internal").ap()
    for tag, etype, keys, adj in (("s0", "edge_type_34", keys0, adj0), ("s2", "edge_type_3", keys2, adj2)):
        with ExitStack() as ctx:
            slot_src = ctx.enter_context(nc.sbuf_tensor(f"{tag}_slot_src", [SLOT, slots_of(keys)], F32))
            slot_dst = ctx.enter_context(nc.sbuf_tensor(f"{tag}_slot_dst", [SLOT, slots_of(keys)], F32))
            counts = ctx.enter_context(nc.sbuf_tensor(f"{tag}_counts", [1, 2, keys], I32))
            sort_edges(nc, f"{tag}_sort", d["src"], d["dst"], d[etype], keys, slot_src, slot_dst, counts)
            build_adjacency(nc, f"{tag}_build", keys, slot_src, slot_dst, counts, adj)
    with ExitStack() as ctx:
        x = ctx.enter_context(nc.sbuf_tensor("x_rows", [NP, NT, dim], F32))
        h = ctx.enter_context(nc.sbuf_tensor("h_rows", [NP, NT, wide], F32))
        ident = ctx.enter_context(nc.sbuf_tensor("ident", [128, 128], F32))
        adj_all = ctx.enter_context(nc.sbuf_tensor("adj_all", [NP, NT, NC], U16))
        dinv = ctx.enter_context(nc.sbuf_tensor("dinv", [NP, NT], F32))
        setup(nc, d["x"], x, ident)
        sum_adjacency(nc, "all", adj2, types2, adj_all, dinv, ident)

        def gcn(tag, w, b, **how):
            layer(nc, tag, h, dim, dim, d[b], d[w], 1, adj_all=adj_all, dinv=dinv, **how)

        normalise(nc, "n0", x, h)
        layer(nc, "l0a", h, dim, dim, d["L0_gnn_b_rgcn"], d["L0_gnn_W_rel"], types0, adj=adj0,
              w_root=d["L0_gnn_W_root"], ident=ident)
        gcn("l0b", "L0_gnn_W_gcn", "L0_gnn_b_gcn", x=x)
        normalise(nc, "n1", x, h)
        gcn("l1a", "L1_gnn_W1", "L1_gnn_b1", relu=True)
        gcn("l1b", "L1_gnn_W2", "L1_gnn_b2", x=x)
        normalise(nc, "n2", x, h, extra=(d["node_type_3"], d["L2_gnn_node_emb"]))
        for i, (a, b) in enumerate(((wide, wide), (wide, dim), (dim, dim)), 1):
            layer(nc, f"l2{i}", h, a, b, d[f"L2_gnn_b{i}"], d[f"L2_gnn_w_rel{i}"], types2, adj=adj2,
                  w_root=d[f"L2_gnn_w_root{i}"], ident=ident, relu=True, x=x if i == 3 else None)
        normalise(nc, "n3", x, h)
        gcn("l3", "L3_gnn_W", "L3_gnn_b", x=x)
        stored = ctx.enter_context(nc.semaphore("out_stored"))
        with nc.Block() as block:
            @block.sync
            def _(sp):
                sp.dma_start(out.rearrange("(k p) f -> p k f", p=NP), x[:]).then_inc(stored, 16)
                sp.wait_ge(stored, 16)


_INS = ["x", "src", "dst", "edge_type_3", "edge_type_34", "node_type_3", "L0_gnn_W_rel", "L0_gnn_W_root",
        "L0_gnn_b_rgcn", "L0_gnn_W_gcn", "L0_gnn_b_gcn", "L1_gnn_W1", "L1_gnn_b1", "L1_gnn_W2", "L1_gnn_b2",
        "L2_gnn_node_emb", "L2_gnn_w_rel1", "L2_gnn_w_root1", "L2_gnn_b1", "L2_gnn_w_rel2", "L2_gnn_w_root2",
        "L2_gnn_b2", "L2_gnn_w_rel3", "L2_gnn_w_root3", "L2_gnn_b3", "L3_gnn_W", "L3_gnn_b"]


def kernel(**inputs):
    import numpy as _np
    import concourse.bacc as _bacc
    from concourse import mybir as _mybir
    from concourse.bass_utils import run_bass_kernel_spmd as _run

    nc = _bacc.Bacc("TRN2", target_bir_lowering=False, num_devices=1)
    arrays, aps = {}, {}
    for name in _INS:
        a = _np.ascontiguousarray(inputs[name])
        arrays[f"in_{name}"] = a
        aps[name] = nc.dram_tensor(f"in_{name}", a.shape, _mybir.dt.from_np(a.dtype), kind="ExternalInput").ap()
    out = nc.dram_tensor("out_0", arrays["in_x"].shape, F32, kind="ExternalOutput").ap()
    gnn_kernel(nc, aps, out)
    r = _run(nc, [arrays], core_ids=[0])
    return r.results[0]["out_0"]
```

```python
from contextlib import ExitStack

import concourse.bass as bass
from concourse import mybir

ALU = mybir.AluOpType
ACT = mybir.ActivationFunctionType
AX_X = mybir.AxisListType.X
F32 = mybir.dt.float32
F32R = mybir.dt.float32r
F16 = mybir.dt.float16
I32 = mybir.dt.int32
U16 = mybir.dt.uint16

N = 625
NT = 5
NP = N // NT
NPC = NP + 1
NC = NT * NPC
PART = (3 * NPC, 2 * NPC)
BANK = 512
LEFT = BANK - PART[0]
E = 10625
EP = 125
EC = E // EP
SLOT = 128
EPS = 1e-5


def column(n_tile):
    return n_tile * NPC


def slots_of(keys, lot=1):
    return (E // (lot * SLOT) + keys + (lot > 1)) * lot


def semaphores(nc, tag, ctx):
    made = []

    def clear():
        nc.clear_and_free_semaphores(made)
        nc.all_engine_barrier()

    ctx.callback(clear)

    def sem(name):
        made.append(nc.alloc_semaphore(f"{tag}_{name}"))
        return made[-1]

    return sem


def slot_tile(nc, i, keys):
    return nc.s_assert_within(i, 0, slots_of(keys) - 1, skip_runtime_bounds_check_because="all edges fit slots_of(keys) tiles")


def sort_edges(nc, tag, src, dst, etype, keys, lot, slot_src, slot_dst, counts, lots=None, tile_of=None):
    slots = slots_of(keys, lot)
    by_tile = tile_of is None
    chunk = 17
    assert EC % chunk == 0 and 2 * slots <= BANK and lot in (1, 3)
    with ExitStack() as ctx:
        def sb(name, shape, dt):
            return ctx.enter_context(nc.sbuf_tensor(f"{tag}_{name}", shape, dt))

        sem = semaphores(nc, tag, ctx)

        raw = sb("raw", [EP, 3, EC], I32)
        val = sb("val", [EP, 3, EC], F32)
        node_tile = sb("node_tile", [EP, 2, EC], F32)
        key = sb("key", [EP, EC], F32)
        local_src = sb("local_src", [EP, EC], F32)
        col_dst = sb("col_dst", [EP, EC], F32)
        key_iota = sb("key_iota", [EP, keys], F32)
        is_key = sb("is_key", [EP, keys, EC], F16)
        running = sb("running", [EP, keys, EC], F32)
        zeros = sb("zeros", [EP, 1], F32)
        part_cnt = sb("part_cnt", [EP, keys], F16)
        before = sb("before", [EP, keys], F32)
        lower = sb("lower", [EP, EP], F16)
        ones = sb("ones", [EP, 128], F16)
        total_i = sb("total_i", [EP, keys], I32)
        tiles_f = sb("tiles_f", [EP, keys], F32)
        tiles_end = sb("tiles_end", [EP, keys], F32)
        base = sb("base", [EP, keys], F32)
        pos = sb("pos", [EP, EC], F32)
        pos_i = sb("pos_i", [EP, EC], I32)
        hi_i = sb("hi_i", [EP, EC], I32)
        lo_i = sb("lo_i", [EP, EC], I32)
        hi = sb("hi", [EP, EC], F32)
        lo = sb("lo", [EP, EC], F32)
        slot_iota = sb("slot_iota", [EP, SLOT], F16)
        tile_iota = sb("tile_iota", [EP, slots], F16)
        is_slot = sb("is_slot", [EP, chunk, SLOT], F16)
        is_tile = sb("is_tile", [EP, chunk, slots], F16)
        load = sb("load", [EP, chunk, 2, slots], F16)
        lots_i = sb("lots_i", [EP, keys], I32)
        ps_cnt = ctx.enter_context(nc.psum_tensor(f"{tag}_ps_cnt", [EP, 2, BANK], F32))
        ps_slot = ctx.enter_context(nc.psum_tensor(f"{tag}_ps_slot", [SLOT, BANK], F32))

        loaded = sem("loaded")
        consts_ready = sem("consts_ready")
        counted = sem("counted")
        summed = sem("summed")
        chunk_ready = sem("chunk_ready")
        chunk_used = sem("chunk_used")
        step = sem("step")
        done = sem("done")

        block = ctx.enter_context(nc.Block())

        @block.sync
        def _(sp):
            for i, a in enumerate((src, dst, etype)):
                sp.dma_start(raw[:, i, :], a.rearrange("(p c) -> p c", p=EP)).then_inc(loaded, 16)

        @block.gpsimd
        def _(pool):
            nc.gpsimd.iota(key_iota[:], [[1, keys]], base=0, channel_multiplier=0,
                           allow_small_or_imprecise_dtypes=True).then_inc(consts_ready, 1)
            nc.gpsimd.iota(slot_iota[:], [[1, SLOT]], base=0, channel_multiplier=0,
                           allow_small_or_imprecise_dtypes=True).then_inc(consts_ready, 1)
            nc.gpsimd.iota(tile_iota[:], [[1, slots]], base=0, channel_multiplier=0,
                           allow_small_or_imprecise_dtypes=True).then_inc(consts_ready, 1)
            nc.gpsimd.memset(ones[:], 1.0).then_inc(consts_ready, 1)
            nc.gpsimd.memset(zeros[:], 0.0).then_inc(consts_ready, 1)
            nc.gpsimd.memset(lower[:], 1.0).then_inc(consts_ready, 1)
            pool.wait_ge(consts_ready, 6)
            nc.gpsimd.affine_select(out=lower[:], in_=lower[:], compare_op=ALU.is_gt, fill=0.0, base=0,
                                    pattern=[[1, EP]], channel_multiplier=-1).then_inc(consts_ready, 1)

        @block.vector
        def _(dve):
            chain = [0]

            def then(ins):
                chain[0] += 1
                ins.then_inc(step, 1)
                dve.wait_ge(step, chain[0])

            v = nc.vector
            dve.wait_ge(loaded, 48)
            then(v.tensor_copy(val[:], raw[:]))
            if by_tile:
                then(v.tensor_scalar(node_tile[:], val[:, 0:2, :], float(NP), None, ALU.is_ge))
                for j in range(2, NT):
                    then(v.scalar_tensor_tensor(node_tile[:], val[:, 0:2, :], float(j * NP), node_tile[:],
                                                ALU.is_ge, ALU.add))
                then(v.scalar_tensor_tensor(local_src[:], node_tile[:, 0, :], float(-NP), val[:, 0, :],
                                            ALU.mult, ALU.add))
                then(v.tensor_tensor(col_dst[:], node_tile[:, 1, :], val[:, 1, :], ALU.add))
                then(v.scalar_tensor_tensor(key[:], val[:, 2, :], float(NT), node_tile[:, 0, :], ALU.mult, ALU.add))
            else:
                then(v.tensor_copy(local_src[:], val[:, 0, :]))
                then(v.tensor_copy(col_dst[:], val[:, 1, :]))
                then(v.tensor_copy(key[:], val[:, 2, :]))
            dve.wait_ge(consts_ready, 7)
            then(v.tensor_tensor(is_key[:], key_iota[:].unsqueeze(2).broadcast_to([EP, keys, EC]),
                                 key[:].unsqueeze(1).broadcast_to([EP, keys, EC]), ALU.is_equal))
            flat = is_key[:].rearrange("p k c -> p (k c)")
            then(v.tensor_tensor_scan(running[:].rearrange("p k c -> p (k c)"), flat,
                                      zeros[:].broadcast_to([EP, keys * EC]), 0.0, ALU.add, ALU.add))
            ends = running[:, :, EC - 1]
            then(v.tensor_copy(part_cnt[:, 0:1], ends[:, 0:1]))
            v.tensor_tensor(part_cnt[:, 1:keys], ends[:, 1:keys], ends[:, 0:keys - 1], ALU.subtract).then_inc(counted, 1)
            dve.wait_ge(summed, 1)
            then(v.tensor_scalar(total_i[:], ps_cnt[:, 1, 0:keys], float(SLOT - 1), None, ALU.add))
            then(v.tensor_scalar(total_i[:], total_i[:], 7, None, ALU.logical_shift_right))
            if lot == 1:
                then(v.tensor_scalar(tiles_f[:], total_i[:], 1.0, None, ALU.max))
            else:
                then(v.tensor_scalar(lots_i[:], total_i[:], 1.0 / lot, 1.0 / lot, ALU.mult, ALU.add))
                then(v.tensor_scalar(tiles_f[:], lots_i[:], 1.0, float(lot), ALU.max, ALU.mult))
            then(v.tensor_tensor_scan(tiles_end[:], tiles_f[:], zeros[:].broadcast_to([EP, keys]), 0.0, ALU.add, ALU.add))
            then(v.tensor_tensor(base[:], tiles_end[:], tiles_f[:], ALU.subtract))
            then(v.tensor_copy(counts[0:1, 0, 0:keys], base[0:1, :]))
            then(v.tensor_copy(counts[0:1, 1, 0:keys], tiles_f[0:1, :]))
            then(v.scalar_tensor_tensor(before[:], base[:], float(SLOT), ps_cnt[:, 0, 0:keys], ALU.mult, ALU.add))
            then(v.tensor_scalar(before[:], before[:], 1.0, None, ALU.subtract))
            then(v.tensor_tensor(before[:, 1:keys], before[:, 1:keys], ends[:, 0:keys - 1], ALU.subtract))
            then(v.tensor_tensor(running[:], running[:], before[:].unsqueeze(2).broadcast_to([EP, keys, EC]), ALU.add))
            then(v.tensor_tensor(running[:], running[:], is_key[:], ALU.mult))
            then(v.tensor_reduce(pos[:], running[:].rearrange("p k c -> p c k"), AX_X, ALU.add))
            then(v.tensor_copy(pos_i[:], pos[:]))
            then(v.tensor_scalar(hi_i[:], pos_i[:], 7, None, ALU.logical_shift_right))
            then(v.tensor_scalar(lo_i[:], pos_i[:], SLOT - 1, None, ALU.bitwise_and))
            then(v.tensor_copy(hi[:], hi_i[:]))
            if not by_tile:
                then(v.tensor_copy(tile_of[:], hi_i[:]))
                then(v.tensor_scalar(lots[:], tiles_end[:], 1.0 / lot, None, ALU.mult))
            then(v.tensor_copy(lo[:], lo_i[:]))
            then(v.tensor_scalar(local_src[:], local_src[:], 1.0, None, ALU.add))
            then(v.tensor_scalar(col_dst[:], col_dst[:], 1.0, None, ALU.add))
            for n in range(EC // chunk):
                at = slice(n * chunk, (n + 1) * chunk)
                if n:
                    dve.wait_ge(chunk_used, n)
                v.tensor_tensor(is_slot[:], slot_iota[:].unsqueeze(1).broadcast_to([EP, chunk, SLOT]),
                                lo[:, at].unsqueeze(2).broadcast_to([EP, chunk, SLOT]), ALU.is_equal)
                then(v.tensor_tensor(is_tile[:], tile_iota[:].unsqueeze(1).broadcast_to([EP, chunk, slots]),
                                     hi[:, at].unsqueeze(2).broadcast_to([EP, chunk, slots]), ALU.is_equal))
                v.tensor_tensor(load[:, :, 0, :], is_tile[:],
                                local_src[:, at].unsqueeze(2).broadcast_to([EP, chunk, slots]), ALU.mult)
                then(v.tensor_tensor(load[:, :, 1, :], is_tile[:],
                                     col_dst[:, at].unsqueeze(2).broadcast_to([EP, chunk, slots]), ALU.mult))
                v.engine_nop().then_inc(chunk_ready, 1)
            dve.wait_ge(done, 1)
            then(v.tensor_scalar(slot_src[:, 0:slots], ps_slot[:, 0:slots], 1.0, None, ALU.subtract))
            then(v.tensor_scalar(slot_dst[:, 0:slots], ps_slot[:, slots:2 * slots], 1.0, None, ALU.subtract))

        @block.tensor
        def _(pe):
            pe.wait_ge(consts_ready, 7)
            pe.wait_ge(counted, 1)
            nc.tensor.matmul(ps_cnt[:, 0, 0:keys], lower[:], part_cnt[:], start=True, stop=True)
            nc.tensor.matmul(ps_cnt[:, 1, 0:keys], ones[:, 0:EP], part_cnt[:], start=True, stop=True).then_inc(summed, 1)
            for n in range(EC // chunk):
                pe.wait_ge(chunk_ready, n + 1)
                for c in range(chunk):
                    last = nc.tensor.matmul(ps_slot[:, 0:2 * slots], is_slot[:, c, :],
                                            load[:, c].rearrange("p a s -> p (a s)"),
                                            start=(n == 0 and c == 0), stop=(n == EC // chunk - 1 and c == chunk - 1))
                last.then_inc(chunk_used, 1)
            pe.wait_ge(chunk_used, EC // chunk)
            nc.tensor.nop().then_inc(done, 1)


def build_adjacency(nc, tag, keys, slot_src, slot_dst, counts, adj):
    assert keys % 2 == 0
    with ExitStack() as ctx:
        def sb(name, shape, dt):
            return ctx.enter_context(nc.sbuf_tensor(f"{tag}_{name}", shape, dt))

        sem = semaphores(nc, tag, ctx)

        node_iota = sb("node_iota", [SLOT, NC], F16)
        is_src = sb("is_src", [SLOT, 2, NP], F16)
        is_dst = sb("is_dst", [SLOT, 2, NC], F16)
        zeros = sb("zeros", [SLOT, 2 * BANK], F16)
        cnt = sb("cnt", [NP, 2, NC], U16)
        ps = ctx.enter_context(nc.psum_tensor(f"{tag}_ps", [NP, 2, 2 * BANK], F32))

        consts_ready = sem("consts_ready")
        onehots_ready = sem("onehots_ready")
        onehots_free = sem("onehots_free")
        counted = sem("counted")
        copied = sem("copied")
        stored = [sem(f"stored{b}") for b in range(2)]

        block = ctx.enter_context(nc.Block())

        @block.gpsimd
        def _(pool):
            nc.gpsimd.iota(node_iota[:], [[1, NC]], base=0, channel_multiplier=0,
                           allow_small_or_imprecise_dtypes=True).then_inc(consts_ready, 1)
            nc.gpsimd.memset(zeros[:], 0.0).then_inc(consts_ready, 1)

        @block.vector
        def _(dve):
            dve.wait_ge(consts_ready, 2)
            first = dve.value_load(counts[0:1, 0, keys - 1:keys], min_val=0, max_val=slots_of(keys))
            last = dve.value_load(counts[0:1, 1, keys - 1:keys], min_val=1, max_val=slots_of(keys))
            with dve.Fori(0, first + last) as tile:
                i = slot_tile(nc, tile, keys)
                dve.wait_ge(onehots_free, i + 1)
                nc.vector.tensor_scalar(is_src[:, i % 2, :], node_iota[:, 0:NP], slot_src[:, bass.ds(i, 1)], None,
                                        ALU.is_equal)
                nc.vector.tensor_scalar(is_dst[:, i % 2, :], node_iota[:], slot_dst[:, bass.ds(i, 1)], None,
                                        ALU.is_equal).then_inc(onehots_ready, 1)

        @block.tensor
        def _(pe):
            pe.wait_ge(consts_ready, 2)
            nc.tensor.nop().then_inc(onehots_free, 2)
            with pe.Fori(0, keys // 2) as pair:
                for b in range(2):
                    key = 2 * pair + b
                    pe.wait_ge(copied, key + 1)
                    for h in range(2):
                        nc.tensor.matmul(ps[:, b, h * BANK:(h + 1) * BANK], zeros[:, 0:NP], zeros[:, 0:BANK],
                                         start=True, stop=False)
                    first = pe.value_load(counts[0:1, 0, bass.ds(key, 1)], min_val=0, max_val=slots_of(keys))
                    tiles = pe.value_load(counts[0:1, 1, bass.ds(key, 1)], min_val=1, max_val=slots_of(keys))
                    with pe.Fori(first, first + tiles) as tile:
                        i = slot_tile(nc, tile, keys)
                        pe.wait_ge(onehots_ready, i + 1)
                        for h in range(2):
                            cols = slice(0, PART[0]) if h == 0 else slice(PART[0], NC)
                            at = LEFT if h == 0 else BANK
                            mm = nc.tensor.matmul(ps[:, b, at:at + PART[h]], is_src[:, i % 2, :],
                                                  is_dst[:, i % 2, cols], start=False, stop=False)
                        mm.then_inc(onehots_free, 1)
                    for h in range(2):
                        mm = nc.tensor.matmul(ps[:, b, h * BANK:(h + 1) * BANK], zeros[:, 0:NP], zeros[:, 0:BANK],
                                              start=False, stop=True)
                    mm.then_inc(counted, 1)

        @block.scalar
        def _(act):
            nc.scalar.preload_act_table(ACT.Copy)
            nc.scalar.nop().then_inc(copied, 2)

            def copy(pair, first):
                for b in range(2):
                    act.wait_ge(counted, 2 * pair + b + 1)
                    if not first:
                        act.wait_ge(stored[b], pair * 16)
                    nc.scalar.copy(cnt[:, b, :], ps[:, b, LEFT:LEFT + NC]).then_inc(copied, 1)

            copy(0, True)
            with act.Fori(1, keys // 2) as pair:
                copy(pair, False)

        @block.sync
        def _(sp):
            with sp.Fori(0, keys // 2) as pair:
                for b in range(2):
                    sp.wait_ge(copied, 2 * pair + b + 3)
                    sp.dma_start(adj[bass.ds(2 * pair + b, 1), :, :].rearrange("k p c -> p (k c)"),
                                 cnt[:, b, :]).then_inc(stored[b], 16)
            for b in range(2):
                sp.wait_ge(stored[b], 8 * keys)


def newton_rsqrt(v, then, out, d, half, tmp):
    then(v.tensor_tensor(tmp, out, out, ALU.mult))
    then(v.tensor_tensor(tmp, tmp, d, ALU.mult))
    then(v.tensor_scalar(tmp, tmp, -0.5, 1.5, ALU.mult, ALU.add))
    then(v.tensor_tensor(out, out, tmp, ALU.mult))


def sum_adjacency(nc, tag, adj, types, adj_all, dinv, ident):
    with ExitStack() as ctx:
        def sb(name, shape, dt):
            return ctx.enter_context(nc.sbuf_tensor(f"{tag}_{name}", shape, dt))

        sem = semaphores(nc, tag, ctx)

        part = sb("part", [NP, types * NT, NC], U16)
        total = sb("total", [NP, NT, NC], F32)
        ones = sb("ones", [NP, 2], F32)
        deg = sb("deg", [NP, NT], F32)
        tmp = sb("tmp", [NP, NT], F32)
        ps = ctx.enter_context(nc.psum_tensor(f"{tag}_ps", [NP, NT, 2], F32))

        loaded = sem("loaded")
        summed = sem("summed")
        counted = sem("counted")
        inverted = sem("inverted")
        rooted = sem("rooted")
        step = sem("step")

        block = ctx.enter_context(nc.Block())

        @block.sync
        def _(sp):
            sp.dma_start(part[:], adj[0:types * NT, :, :].rearrange("k p c -> p k c")).then_inc(loaded, 16)

        @block.vector
        def _(dve):
            chain = [0]

            def then(ins):
                chain[0] += 1
                ins.then_inc(step, 1)
                dve.wait_ge(step, chain[0])

            v = nc.vector
            v.memset(ones[:], 1.0)
            dve.wait_ge(loaded, 16)
            then(v.tensor_tensor(total[:], part[:, 0:NT, :], part[:, NT:2 * NT, :], ALU.add))
            for t in range(2, types):
                then(v.tensor_tensor(total[:], total[:], part[:, t * NT:(t + 1) * NT, :], ALU.add))
            for k in range(NT):
                own = total[:, k, column(k):column(k) + NP]
                then(v.tensor_tensor(own, own, ident[0:NP, 0:NP], ALU.add))
            v.tensor_copy(adj_all[:], total[:]).then_inc(summed, 1)
            dve.wait_ge(counted, 1)
            then(v.tensor_copy(deg[:], ps[:, :, 0]))
            v.reciprocal(dinv[:], deg[:]).then_inc(inverted, 1)
            dve.wait_ge(rooted, 1)
            newton_rsqrt(v, then, dinv[:], deg[:], None, tmp[:])

        @block.scalar
        def _(act):
            act.wait_ge(inverted, 1)
            nc.scalar.activation(dinv[:], dinv[:], ACT.Sqrt).then_inc(rooted, 1)

        @block.tensor
        def _(pe):
            pe.wait_ge(summed, 1)
            for d in range(NT):
                for k in range(NT):
                    last = nc.tensor.matmul(ps[:, d, :], total[:, k, column(d):column(d) + NP], ones[:],
                                            start=(k == 0 and d == 0), stop=(k == NT - 1 and d == NT - 1),
                                            skip_group_check=True)
            last.then_inc(counted, 1)


def normalise(nc, tag, x, h, extra=None):
    width = x.shape[2]
    with ExitStack() as ctx:
        def sb(name, shape, dt):
            return ctx.enter_context(nc.sbuf_tensor(f"{tag}_{name}", shape, dt))

        sem = semaphores(nc, tag, ctx)

        stats = sb("stats", [NP, NT, 2, 6], F32)
        moments = sb("moments", [NP, NT, 2], F32)
        var = sb("var", [NP, NT], F32)
        rstd = sb("rstd", [NP, NT], F32)
        tmp = sb("tmp", [NP, NT], F32)
        if extra is not None:
            types, emb = extra
            rows, dim = emb.shape
            type_i = sb("type_i", [NP, NT], I32)
            type_f = sb("type_f", [NP, NT], F32)
            is_type = sb("is_type", [NP, NT], F32)
            emb_rows = sb("emb_rows", [NP, rows, dim], F32)

        loaded = sem("loaded")
        inverted = sem("inverted")
        rooted = sem("rooted")
        step = sem("step")

        block = ctx.enter_context(nc.Block())

        if extra is not None:
            @block.sync
            def _(sp):
                with nc.allow_non_contiguous_dma(reason="five node types per partition"):
                    sp.dma_start(type_i[:], types.rearrange("(k p) -> p k", p=NP)).then_inc(loaded, 16)
                sp.dma_start(emb_rows[:], emb.unsqueeze(0).broadcast_to([NP, rows, dim])).then_inc(loaded, 16)

        @block.scalar
        def _(act):
            act.wait_ge(inverted, 1)
            nc.scalar.activation(rstd[:], rstd[:], ACT.Sqrt).then_inc(rooted, 1)

        @block.vector
        def _(dve):
            chain = [0]

            def then(ins):
                chain[0] += 1
                ins.then_inc(step, 1)
                dve.wait_ge(step, chain[0])

            v = nc.vector
            for k in range(NT):
                for half in range(2):
                    last = v.bn_stats(stats[:, k, half, :], x[:, k, half * (width // 2):(half + 1) * (width // 2)])
            then(last)
            for k in range(NT):
                last = v.bn_aggr(moments[:, k, :], stats[:, k])
            then(last)
            then(v.tensor_scalar(var[:], moments[:, :, 1], EPS, None, ALU.add))
            v.reciprocal(rstd[:], var[:]).then_inc(inverted, 1)
            dve.wait_ge(rooted, 1)
            newton_rsqrt(v, then, rstd[:], var[:], None, tmp[:])
            for k in range(NT):
                last = v.tensor_scalar(h[:, k, 0:width], x[:, k, :], moments[:, k, 0:1], rstd[:, k:k + 1],
                                       ALU.subtract, ALU.mult)
            then(last)
            v.tensor_scalar(h[:, :, 0:width], h[:, :, 0:width], 0.0, None, ALU.max)
            if extra is not None:
                dve.wait_ge(loaded, 32)
                then(v.tensor_copy(type_f[:], type_i[:]))
                for t in range(rows):
                    then(v.tensor_scalar(is_type[:], type_f[:], float(t), None, ALU.is_equal))
                    for k in range(NT):
                        out = h[:, k, width:width + dim]
                        if t == 0:
                            last = v.tensor_scalar(out, emb_rows[:, t, :], is_type[:, k:k + 1], None, ALU.mult)
                        else:
                            last = v.scalar_tensor_tensor(out, emb_rows[:, t, :], is_type[:, k:k + 1], out,
                                                          ALU.mult, ALU.add)
                    then(last)


def layer(nc, tag, h, width, out_width, bias, w_rel, relations, adj=None, w_root=None, adj_all=None, dinv=None,
          relu=False, x=None, ident=None):
    mean = adj is not None
    fc = width // 128
    half = out_width // 2
    steps = relations + (w_root is not None)
    ring = 3
    with ExitStack() as ctx:
        def sb(name, shape, dt):
            return ctx.enter_context(nc.sbuf_tensor(f"{tag}_{name}", shape, dt))

        sem = semaphores(nc, tag, ctx)

        h_hi = sb("h_hi", [NP, NT, width], F32R)
        h_lo = sb("h_lo", [NP, NT, width], F32R)
        a_raw = sb("a_raw", [NP, NT, NC], U16) if mean else None
        a = sb("a", [NP, NT, NC], F32R) if relations else None
        ones = sb("ones", [NP, 128], F32R) if mean else None
        ones_f = sb("ones_f", [NP, 128], F32) if mean else None
        inv = sb("inv", [128, NC], F32) if mean else None
        scaled = sb("scaled", [128, 2, NC], F32) if mean else None
        g_hi = sb("g_hi", [128, fc, NC], F32R)
        g_lo = sb("g_lo", [128, fc, NC], F32R)
        w_raw = sb("w_raw", [128, ring, out_width], F32)
        w_hi = sb("w_hi", [128, fc, out_width], F32R)
        w_lo = sb("w_lo", [128, fc, out_width], F32R)
        bias_rows = sb("bias_rows", [NP, out_width], F32)
        ps_g = ctx.enter_context(nc.psum_tensor(f"{tag}_ps_g", [128, 2, 2 * BANK], F32))
        ps_o = ctx.enter_context(nc.psum_tensor(f"{tag}_ps_o", [128, 2, 2, BANK], F32))

        bias_loaded = sem("bias_loaded")
        w_loaded = [sem(f"w_loaded{s}") for s in range(ring)]
        w_hi_ready = sem("w_hi_ready")
        w_ready = sem("w_ready")
        h_scaled = sem("h_scaled")
        h_hi_ready = sem("h_hi_ready")
        h_ready = sem("h_ready")
        a_loaded = sem("a_loaded")
        a_ready = sem("a_ready")
        ones_ready = sem("ones_ready")
        inv_ready = sem("inv_ready")
        g_summed = sem("g_summed")
        g_freed = sem("g_freed")
        g_hi_ready = sem("g_hi_ready")
        g_ready = sem("g_ready")
        o_summed = sem("o_summed")
        o_taken = sem("o_taken")
        done = sem("done")

        root = w_root is not None
        per = fc + 1 if mean else fc

        def sums_before(r):
            return (fc if root else 0) + r * per

        def step_of(r):
            return r + root

        def all_nodes(cols):
            return cols.rearrange("p (k c) -> p k c", c=NPC)[:, :, 0:NP]

        block = ctx.enter_context(nc.Block())

        @block.sync
        def _(sp):
            def load_w(w, s):
                for f in range(fc):
                    if f >= ring:
                        sp.wait_ge(w_ready, s * fc + f - ring + 1)
                    elif not (isinstance(s, int) and s == 0):
                        sp.wait_ge(w_ready, s * fc - (fc - 1 - last_in(f)))
                    sp.dma_start(w_raw[:, f % ring, :], w(f)).then_inc(w_loaded[f % ring], 16)

            def last_in(place):
                return max(f for f in range(fc) if f % ring == place)

            sp.dma_start(bias_rows[:], bias.unsqueeze(0).broadcast_to([NP, out_width])).then_inc(bias_loaded, 16)
            if root:
                load_w(lambda f: w_root[f * 128:(f + 1) * 128, :], 0)
            if mean:
                with sp.Fori(0, relations) as r:
                    sp.wait_ge(a_ready, r + 1)
                    sp.dma_start(a_raw[:], adj[bass.ds(r * NT, NT), :, :].rearrange("k p c -> p k c")).then_inc(a_loaded, 16)
                    load_w(lambda f: w_rel[bass.ds(r, 1), f * 128:(f + 1) * 128, :].rearrange("a f o -> f (a o)"), step_of(r))
            elif relations:
                load_w(lambda f: w_rel[f * 128:(f + 1) * 128, :], 0)

        @block.gpsimd
        def _(pool):
            if mean:
                nc.gpsimd.memset(ones_f[:], 1.0).then_inc(ones_ready, 1)
                pool.wait_ge(ones_ready, 1)
                nc.gpsimd.tensor_copy(ones[:], ones_f[:]).then_inc(ones_ready, 1)
            elif relations:
                nc.gpsimd.tensor_copy(a[:], adj_all[:]).then_inc(a_ready, 1)

        @block.scalar
        def _(act):
            nc.scalar.preload_act_table(ACT.Copy)
            if dinv is not None:
                act.wait_ge(h_scaled, 1)
            for k in range(NT):
                nc.scalar.copy(h_hi[:, k, :], h[:, k, 0:width]).then_inc(h_hi_ready, 1)

            def chunk(s, f, to, source, uses, which, k):
                act.wait_ge(w_loaded[f % ring], 16 * (s * uses + f // ring + 1))
                if f == 0 and not (isinstance(s, int) and s == 0):
                    act.wait_ge(o_summed, s * NT)
                nc.scalar.copy(w_hi[:, f, :], w_raw[:, f % ring, :]).then_inc(w_hi_ready, 1)
                act.wait_ge(which, k)
                nc.scalar.copy(to, source).then_inc(g_hi_ready, 1)

            def uses_of(f):
                return len([g for g in range(fc) if g % ring == f % ring])

            if root:
                for f in range(fc):
                    chunk(0, f, all_nodes(g_hi[:, f, :]), all_nodes(ps_g[:, f % 2, LEFT:LEFT + NC]), uses_of(f),
                          g_summed, f + 1)
            if mean:
                nc.scalar.nop().then_inc(a_ready, 1)
                with act.Fori(0, relations) as r:
                    act.wait_ge(a_loaded, 16 * r + 16)
                    act.wait_ge(g_summed, sums_before(r))
                    nc.scalar.copy(a[:], a_raw[:]).then_inc(a_ready, 1)
                    for f in range(fc):
                        chunk(step_of(r), f, g_hi[:, f, :], scaled[:, f % 2, :], uses_of(f), g_freed, r * per + f + 3)
            elif relations:
                for f in range(fc):
                    chunk(0, f, g_hi[:, f, :], ps_g[:, f % 2, LEFT:LEFT + NC], uses_of(f), g_summed, f + 1)

        @block.vector
        def _(dve):
            v = nc.vector
            if dinv is not None:
                for k in range(NT):
                    last = v.tensor_scalar(h[:, k, 0:width], h[:, k, 0:width], dinv[:, k:k + 1], None, ALU.mult)
                last.then_inc(h_scaled, 1)
                dve.wait_ge(h_scaled, 1)
            for k in range(NT):
                dve.wait_ge(h_hi_ready, k + 1)
                v.tensor_tensor(h_lo[:, k, :], h[:, k, 0:width], h_hi[:, k, :].bitcast(F32), ALU.subtract).then_inc(h_ready, 1)

            def w_low(s, f):
                dve.wait_ge(w_hi_ready, s * fc + f + 1)
                v.tensor_tensor(w_lo[:, f, :], w_raw[:, f % ring, :], w_hi[:, f, :].bitcast(F32),
                                ALU.subtract).then_inc(w_ready, 1)

            def g_low(s, f, source, only=lambda cols: cols):
                dve.wait_ge(g_hi_ready, s * fc + f + 1)
                v.tensor_tensor(only(g_lo[:, f, :]), only(source), only(g_hi[:, f, :].bitcast(F32)),
                                ALU.subtract).then_inc(g_ready, 1)

            def take(s, first):
                for d in range(NT):
                    dve.wait_ge(o_summed, s * NT + d + 1)
                    ps = ps_o[0:NP, d % 2, :, 0:half]
                    to = h[:, d, 0:out_width].rearrange("p (a o) -> p a o", a=2)
                    by = dinv[:, d:d + 1] if dinv is not None else 1.0
                    if first:
                        base = bias_rows[:].rearrange("p (a o) -> p a o", a=2)
                    else:
                        base = to
                    v.scalar_tensor_tensor(to, ps, by, base, ALU.mult, ALU.add).then_inc(o_taken, 1)

            dve.wait_ge(bias_loaded, 16)
            if root:
                for f in range(fc):
                    w_low(0, f)
                    g_low(0, f, ps_g[:, f % 2, LEFT:LEFT + NC], all_nodes)
                take(0, True)
            if mean:
                v.engine_nop().then_inc(g_freed, 1)
                with dve.Fori(0, relations) as r:
                    s = step_of(r)
                    dve.wait_ge(g_summed, sums_before(r) + 1)
                    v.tensor_scalar(inv[:], ps_g[:, 0, LEFT:LEFT + NC], 1.0, None, ALU.max).then_inc(g_freed, 1)
                    dve.wait_ge(g_freed, r * per + 2)
                    v.reciprocal(inv[:], inv[:]).then_inc(inv_ready, 1)
                    dve.wait_ge(inv_ready, r + 1)
                    for f in range(fc + 1):
                        if f < fc:
                            dve.wait_ge(g_summed, sums_before(r) + f + 2)
                            if f >= 2:
                                dve.wait_ge(g_ready, s * fc + f - 1)
                            v.tensor_tensor(scaled[:, f % 2, :], ps_g[:, (f + 1) % 2, LEFT:LEFT + NC], inv[:],
                                            ALU.mult).then_inc(g_freed, 1)
                            w_low(s, f)
                        if f >= 1:
                            dve.wait_ge(g_freed, r * per + f + 2)
                            g_low(s, f - 1, scaled[:, (f - 1) % 2, :])
                    take(s, False)
            elif relations:
                for f in range(fc):
                    w_low(0, f)
                    g_low(0, f, ps_g[:, f % 2, LEFT:LEFT + NC])
                take(0, True)
            dve.wait_ge(o_taken, steps * NT)
            if relu:
                v.tensor_scalar(h[:, :, 0:out_width], h[:, :, 0:out_width], 0.0, None, ALU.max).then_inc(done, 1)
                dve.wait_ge(done, 1)
            if x is not None:
                v.tensor_tensor(x[:], x[:], h[:, :, 0:out_width], ALU.add)

        @block.tensor
        def _(pe):
            t = nc.tensor

            def products(s):
                for d in range(NT):
                    if d >= 2:
                        pe.wait_ge(o_taken, s * NT + d - 1)
                    elif not (isinstance(s, int) and s == 0):
                        pe.wait_ge(o_taken, s * NT)
                    for a_half in range(2):
                        cols = slice(a_half * half, (a_half + 1) * half)
                        for f in range(fc):
                            if d == 0 and a_half == 0:
                                pe.wait_ge(g_ready, s * fc + f + 1)
                                pe.wait_ge(w_ready, s * fc + f + 1)
                            rows = slice(column(d), column(d) + NP)
                            out = ps_o[0:NP, d % 2, a_half, 0:half]
                            t.matmul(out, g_hi[:, f, rows], w_hi[:, f, cols], start=(f == 0), stop=False)
                            t.matmul(out, g_hi[:, f, rows], w_lo[:, f, cols], start=False, stop=False)
                            mm = t.matmul(out, g_lo[:, f, rows], w_hi[:, f, cols], start=False, stop=(f == fc - 1))
                    mm.then_inc(o_summed, 1)

            def over_edges(r, first):
                for f in range(fc):
                    if mean:
                        pe.wait_ge(g_freed, r * per + f + 1)
                    elif f >= 2:
                        pe.wait_ge(g_ready, f - 1)
                    buf = (first + f) % 2
                    for k in range(NT):
                        for part, rows in enumerate((h_hi, h_lo)):
                            for p in range(2):
                                at, cols = (LEFT, slice(0, PART[0])) if p == 0 else (BANK, slice(PART[0], NC))
                                mm = t.matmul(ps_g[:, buf, at:at + PART[p]], rows[:, k, f * 128:(f + 1) * 128],
                                              a[:, k, cols], start=(k == 0 and part == 0),
                                              stop=(k == NT - 1 and part == 1))
                    mm.then_inc(g_summed, 1)

            if root:
                for f in range(fc):
                    if f >= 2:
                        pe.wait_ge(g_ready, f - 1)
                    for d in range(NT):
                        at = LEFT + column(d)
                        mm = t.transpose(ps_g[:, f % 2, at:at + NP], h[:, d, f * 128:(f + 1) * 128], ident[0:NP, 0:NP])
                    mm.then_inc(g_summed, 1)
                pe.wait_ge(h_ready, NT)
                products(0)
            pe.wait_ge(h_ready, NT)
            if mean:
                pe.wait_ge(ones_ready, 2)
                with pe.Fori(0, relations) as r:
                    pe.wait_ge(a_ready, r + 2)
                    pe.wait_ge(g_freed, r * per + 1)
                    for k in range(NT):
                        for p in range(2):
                            at, cols = (LEFT, slice(0, PART[0])) if p == 0 else (BANK, slice(PART[0], NC))
                            mm = t.matmul(ps_g[:, 0, at:at + PART[p]], ones[:], a[:, k, cols],
                                          start=(k == 0), stop=(k == NT - 1))
                    mm.then_inc(g_summed, 1)
                    over_edges(r, 1)
                    products(step_of(r))
            elif relations:
                pe.wait_ge(a_ready, 1)
                over_edges(0, 0)
                products(0)


UNIT = 3
UNIT_COLS = UNIT * SLOT
TWO = 2 * SLOT


def plan_units(nc, tag, dst, types, tile_of, lots, slot_src, slot_dst, units, src_index, row_index, row_inv, targets,
               plan):
    u_max = units
    with ExitStack() as ctx:
        def sb(name, shape, dt):
            return ctx.enter_context(nc.sbuf_tensor(f"{tag}_{name}", shape, dt))

        sem = semaphores(nc, tag, ctx)
        node_half = (320, N - 320)
        cols = 3 * UNIT
        dst_i = sb("dst_i", [EP, EC], I32)
        dst_f = sb("dst_f", [EP, EC], F32)
        unit_i = sb("unit_i", [EP, EC], I32)
        unit = sb("unit", [EP, EC], F32)
        node_iota = sb("node_iota", [EP, N], F16)
        unit_iota = sb("unit_iota", [EP, u_max], F32)
        is_unit = sb("is_unit", [EP, EC, u_max], F16)
        is_node = sb("is_node", [EP, 4, N], F16)
        lot_ge = sb("lot_ge", [EP, u_max, types], F32)
        type_of = sb("type_of", [EP, u_max], F32)
        type_col = sb("type_col", [u_max, 1], F32)
        same_type = sb("same_type", [u_max, u_max], F32)
        cnt = sb("cnt", [u_max, N], F32)
        present = sb("present", [u_max, N], F32)
        zeros = sb("zeros", [u_max, 1], F32)
        rank = sb("rank", [u_max, N], F32)
        third = sb("third", [u_max, 1], F32)
        type_cnt = sb("type_cnt", [u_max, N], F32)
        rank_t = sb("rank_t", [NP, NT, u_max], F32)
        cnt_t = sb("cnt_t", [NP, NT, u_max], F32)
        rank_ti = sb("rank_ti", [NP, NT, u_max], I32)
        hi_i = sb("hi_i", [NP, NT, u_max], I32)
        lo_i = sb("lo_i", [NP, NT, u_max], I32)
        rank_hi = sb("rank_hi", [NP, NT, u_max], F32)
        rank_lo = sb("rank_lo", [NP, NT, u_max], F32)
        cnt_hi = sb("cnt_hi", [NP, NT, u_max], F32)
        cnt_lo = sb("cnt_lo", [NP, NT, u_max], F32)
        node_num = sb("node_num", [NP, NT], F32)
        slot_iota = sb("slot_iota", [NP, SLOT], F16)
        tile_iota = sb("tile_iota", [NP, UNIT], F32)
        is_slot = sb("is_slot", [NP, u_max, SLOT], F16)
        is_tile = sb("is_tile", [NP, u_max, UNIT], F32)
        load = sb("load", [NP, u_max, 3, UNIT], F16)
        ident = sb("ident", [128, 128], F32)
        lane = sb("lane", [128, 1], F32)
        row_dst = sb("row_dst", [SLOT, u_max, UNIT], F32)
        empty = sb("empty", [SLOT, u_max, UNIT], F32)
        row_cnt = sb("row_cnt", [SLOT, u_max, UNIT], F32)
        row_f = sb("row_f", [SLOT, u_max, UNIT], F32)
        list_rows = sb("list_rows", [128, 2, SLOT], F32)
        flags = sb("flags", [1, u_max], F32)
        ps_cnt = ctx.enter_context(nc.psum_tensor(f"{tag}_ps_cnt", [u_max, 2, BANK], F32))
        ps_t = ctx.enter_context(nc.psum_tensor(f"{tag}_ps_t", [NP, 2, BANK], F32))
        per_bank = BANK // cols
        ps_row = ctx.enter_context(nc.psum_tensor(f"{tag}_ps_row", [SLOT, 2, BANK], F32))
        ps_x = ctx.enter_context(nc.psum_tensor(f"{tag}_ps_x", [128, 2, 256], F32))
        assert u_max <= 2 * per_bank

        loaded = sem("loaded")
        consts_ready = sem("consts_ready")
        nodes_ready = sem("nodes_ready")
        nodes_used = sem("nodes_used")
        counted = sem("counted")
        type_ready = sem("type_ready")
        type_turned = sem("type_turned")
        same_ready = sem("same_ready")
        type_counted = sem("type_counted")
        ranked = sem("ranked")
        turned = sem("turned")
        rows_ready = sem("rows_ready")
        rows_used = sem("rows_used")
        rows_done = sem("rows_done")
        lists_ready = sem("lists_ready")
        lists_turned = sem("lists_turned")
        lists_copied = sem("lists_copied")
        stored = sem("stored")
        step = sem("step")

        block = ctx.enter_context(nc.Block())

        @block.sync
        def _(sp):
            sp.dma_start(dst_i[:], dst.rearrange("(p c) -> p c", p=EP)).then_inc(loaded, 16)
            sp.wait_ge(lists_copied, 1)
            flat = targets.rearrange("u (t s) -> (u t) s", s=SLOT)
            sp.dma_start(flat[0:128, :], list_rows[:, 0, :]).then_inc(stored, 16)
            sp.dma_start(flat[128:UNIT * u_max, :], list_rows[0:UNIT * u_max - 128, 1, :]).then_inc(stored, 16)
            sp.wait_ge(stored, 32)

        @block.gpsimd
        def _(pool):
            def iota(to, pattern, channel=0, base=0):
                nc.gpsimd.iota(to, pattern, base=base, channel_multiplier=channel,
                               allow_small_or_imprecise_dtypes=True).then_inc(consts_ready, 1)

            iota(node_iota[:], [[1, N]])
            iota(unit_iota[:], [[1, u_max]])
            iota(slot_iota[:], [[1, SLOT]])
            iota(tile_iota[:], [[1, UNIT]])
            iota(node_num[:], [[NP, NT]], channel=1, base=1)
            iota(lane[:], [[0, 1]], channel=1, base=N)
            nc.gpsimd.memset(zeros[:], 0.0).then_inc(consts_ready, 1)
            nc.gpsimd.memset(ident[:], 0.0).then_inc(consts_ready, 1)
            pool.wait_ge(consts_ready, 8)
            nc.gpsimd.affine_select(out=ident[:], in_=ident[:], compare_op=ALU.not_equal, fill=1.0, base=0,
                                    pattern=[[-1, 128]], channel_multiplier=1).then_inc(consts_ready, 1)

        @block.vector
        def _(dve):
            chain = [0]

            def then(ins):
                chain[0] += 1
                ins.then_inc(step, 1)
                dve.wait_ge(step, chain[0])

            v = nc.vector
            dve.wait_ge(loaded, 16)
            dve.wait_ge(consts_ready, 9)
            then(v.tensor_copy(dst_f[:], dst_i[:]))
            then(v.tensor_scalar(unit_i[:], tile_of[:], 1.0 / UNIT, -1.0 / UNIT, ALU.mult, ALU.add))
            then(v.tensor_copy(unit[:], unit_i[:]))
            then(v.tensor_tensor(is_unit[:], unit_iota[:].unsqueeze(1).broadcast_to([EP, EC, u_max]),
                                 unit[:].unsqueeze(2).broadcast_to([EP, EC, u_max]), ALU.is_equal))
            for c in range(EC):
                if c >= 4:
                    dve.wait_ge(nodes_used, c - 3)
                v.tensor_scalar(is_node[:, c % 4, :], node_iota[:], dst_f[:, c:c + 1], None,
                                ALU.is_equal).then_inc(nodes_ready, 1)
            then(v.tensor_tensor(lot_ge[:], unit_iota[:].unsqueeze(2).broadcast_to([EP, u_max, types]),
                                 lots[:].unsqueeze(1).broadcast_to([EP, u_max, types]), ALU.is_ge))
            then(v.tensor_reduce(type_of[:], lot_ge[:], AX_X, ALU.add))
            v.tensor_scalar(type_of[:], type_of[:], float(types - 1), None, ALU.min).then_inc(type_ready, 1)
            dve.wait_ge(type_ready, 1)
            then(v.tensor_copy(plan[0:1, 0, 0:u_max], type_of[0:1, :]))
            then(v.tensor_copy(plan[0:1, 3, 0:1], lots[0:1, types - 1:types]))
            dve.wait_ge(type_turned, 1)
            then(v.tensor_copy(type_col[:], ps_x[0:u_max, 0, 0:1]))
            v.tensor_scalar(same_type[:], type_of[0:u_max, :], type_col[:], None, ALU.is_equal).then_inc(same_ready, 1)
            dve.wait_ge(counted, 1)
            then(v.tensor_copy(cnt[:, 0:node_half[0]], ps_cnt[:, 0, 0:node_half[0]]))
            v.tensor_copy(cnt[:, node_half[0]:N], ps_cnt[:, 1, 0:node_half[1]]).then_inc(same_ready, 1)
            dve.wait_ge(same_ready, 2)
            then(v.tensor_scalar(present[:], cnt[:], 1.0, None, ALU.min))
            then(v.tensor_tensor_scan(rank[:], present[:], zeros[:].broadcast_to([u_max, N]), 0.0, ALU.add, ALU.add))
            then(v.tensor_scalar(third[:], rank[:, N - 1:N], float(TWO), None, ALU.is_gt))
            then(v.tensor_scalar(rank[:], rank[:], -1.0 - (4 * SLOT - 1), None, ALU.add))
            then(v.tensor_tensor(rank[:], rank[:], present[:], ALU.mult))
            then(v.tensor_scalar(rank[:], rank[:], float(4 * SLOT - 1), None, ALU.add))
            dve.wait_ge(type_counted, 1)
            then(v.tensor_copy(type_cnt[:, 0:node_half[0]], ps_cnt[:, 0, 0:node_half[0]]))
            v.tensor_copy(type_cnt[:, node_half[0]:N], ps_cnt[:, 1, 0:node_half[1]]).then_inc(ranked, 1)
            dve.wait_ge(turned, 1)
            then(v.tensor_copy(rank_t[:], ps_t[:, 0, 0:NT * u_max].rearrange("p (k u) -> p k u", k=NT)))
            then(v.tensor_copy(cnt_t[:], ps_t[:, 1, 0:NT * u_max].rearrange("p (k u) -> p k u", k=NT)))
            then(v.tensor_copy(plan[0:1, 1, 0:u_max], ps_x[0:1, 1, 0:u_max]))
            then(v.tensor_tensor_scan(flags[:], ps_x[0:1, 1, 0:u_max], zeros[0:1, :].broadcast_to([1, u_max]), 0.0,
                                      ALU.add, ALU.add))
            then(v.tensor_copy(plan[0:1, 2, 0:u_max], flags[:]))
            for whole, high, low in ((rank_t, rank_hi, rank_lo), (cnt_t, cnt_hi, cnt_lo)):
                then(v.tensor_copy(rank_ti[:], whole[:]))
                then(v.tensor_scalar(hi_i[:], rank_ti[:], 7, None, ALU.logical_shift_right))
                then(v.tensor_scalar(lo_i[:], rank_ti[:], SLOT - 1, None, ALU.bitwise_and))
                then(v.tensor_copy(high[:], hi_i[:]))
                then(v.tensor_copy(low[:], lo_i[:]))
            for k in range(NT):
                if k:
                    dve.wait_ge(rows_used, k)
                then(v.tensor_tensor(is_tile[:], tile_iota[:].unsqueeze(1).broadcast_to([NP, u_max, UNIT]),
                                     rank_hi[:, k, :].unsqueeze(2).broadcast_to([NP, u_max, UNIT]), ALU.is_equal))
                v.tensor_scalar(load[:, :, 0, :], is_tile[:], node_num[:, k:k + 1], None, ALU.mult)
                v.tensor_tensor(load[:, :, 1, :], is_tile[:],
                                cnt_hi[:, k, :].unsqueeze(2).broadcast_to([NP, u_max, UNIT]), ALU.mult)
                v.tensor_tensor(load[:, :, 2, :], is_tile[:],
                                cnt_lo[:, k, :].unsqueeze(2).broadcast_to([NP, u_max, UNIT]), ALU.mult)
                v.tensor_tensor(is_slot[:], slot_iota[:].unsqueeze(1).broadcast_to([NP, u_max, SLOT]),
                                rank_lo[:, k, :].unsqueeze(2).broadcast_to([NP, u_max, SLOT]),
                                ALU.is_equal).then_inc(rows_ready, 1)
            dve.wait_ge(rows_done, 1)
            for bank in range(2):
                u0, u1 = bank * per_bank, min(u_max, (bank + 1) * per_bank)
                ps = ps_row[:, bank, 0:(u1 - u0) * cols].rearrange("p (u a t) -> p u a t", a=3, t=UNIT)
                v.tensor_scalar(row_dst[:, u0:u1, :], ps[:, :, 0, :], -1.0, None, ALU.add)
                v.tensor_scalar(row_f[:, u0:u1, :], ps[:, :, 1, :], float(SLOT), None, ALU.mult)
                then(v.tensor_copy(row_cnt[:, u0:u1, :], ps[:, :, 2, :]))
            then(v.tensor_tensor(row_cnt[:], row_cnt[:], row_f[:], ALU.add))
            then(v.tensor_scalar(row_cnt[:], row_cnt[:], 1.0, None, ALU.max))
            v.reciprocal(row_inv[:].rearrange("p (u t) -> p u t", t=UNIT), row_cnt[:])
            then(v.tensor_scalar(empty[:], row_dst[:], 0.0, None, ALU.is_lt))
            then(v.tensor_scalar(row_f[:], empty[:], lane[:], None, ALU.mult))
            then(v.tensor_tensor(row_f[:], row_f[:], empty[:], ALU.add))
            then(v.tensor_tensor(row_index[:].rearrange("p (u t) -> p u t", t=UNIT), row_f[:], row_dst[:], ALU.add))
            v.tensor_tensor(row_dst[:], row_dst[:], empty[:], ALU.subtract).then_inc(lists_ready, 1)
            then(v.tensor_scalar(src_index[:], slot_src[:], 0.0, None, ALU.max))
            dve.wait_ge(lists_turned, 1)
            then(v.tensor_copy(list_rows[:, 0, :], ps_x[:, 0, 0:SLOT]))
            v.tensor_copy(list_rows[0:UNIT * u_max - 128, 1, :],
                          ps_x[0:UNIT * u_max - 128, 1, 0:SLOT]).then_inc(lists_copied, 1)

        @block.tensor
        def _(pe):
            t = nc.tensor
            for c in range(EC):
                pe.wait_ge(nodes_ready, c + 1)
                t.matmul(ps_cnt[:, 0, 0:node_half[0]], is_unit[:, c, :], is_node[:, c % 4, 0:node_half[0]],
                         start=(c == 0), stop=(c == EC - 1))
                t.matmul(ps_cnt[:, 1, 0:node_half[1]], is_unit[:, c, :], is_node[:, c % 4, node_half[0]:N],
                         start=(c == 0), stop=(c == EC - 1)).then_inc(nodes_used, 1)
            pe.wait_ge(nodes_used, EC)
            t.nop().then_inc(counted, 1)
            pe.wait_ge(type_ready, 1)
            t.transpose(ps_x[0:u_max, 0, 0:1], type_of[0:1, :], ident[0:1, 0:1]).then_inc(type_turned, 1)
            pe.wait_ge(same_ready, 2)
            t.matmul(ps_cnt[:, 0, 0:node_half[0]], same_type[:], cnt[:, 0:node_half[0]], start=True, stop=True)
            t.matmul(ps_cnt[:, 1, 0:node_half[1]], same_type[:], cnt[:, node_half[0]:N],
                     start=True, stop=True).then_inc(type_counted, 1)
            pe.wait_ge(ranked, 1)
            for k in range(NT):
                for i, a in enumerate((rank, type_cnt)):
                    t.transpose(ps_t[:, i, k * u_max:(k + 1) * u_max], a[:, k * NP:(k + 1) * NP], ident[0:u_max, 0:u_max])
            t.transpose(ps_x[0:1, 1, 0:u_max], third[:], ident[0:u_max, 0:u_max]).then_inc(turned, 1)
            for k in range(NT):
                pe.wait_ge(rows_ready, k + 1)
                for u in range(u_max):
                    at = u % per_bank * cols
                    mm = t.matmul(ps_row[:, u // per_bank, at:at + cols], is_slot[:, u, :],
                                  load[:, u].rearrange("p a t -> p (a t)"), start=(k == 0 and u % per_bank == 0),
                                  stop=(k == NT - 1 and u in (per_bank - 1, u_max - 1)), skip_group_check=True)
                mm.then_inc(rows_used, 1)
            pe.wait_ge(rows_used, NT)
            t.nop().then_inc(rows_done, 1)
            pe.wait_ge(lists_ready, 1)
            flat = row_dst[:].rearrange("p u t -> p (u t)")
            t.transpose(ps_x[:, 0, 0:SLOT], flat[:, 0:128], ident[:])
            t.transpose(ps_x[0:UNIT * u_max - 128, 1, 0:SLOT], flat[:, 128:UNIT * u_max], ident[:]).then_inc(lists_turned, 1)


def add_means(nc, tag, units, w_rel, rows, sums, plan, src_index, slot_dst, row_index, row_inv, targets):
    width = rows.shape[1]
    fc = width // 128
    half = width // 2
    with ExitStack() as ctx:
        def sb(name, shape, dt):
            return ctx.enter_context(nc.sbuf_tensor(f"{tag}_{name}", shape, dt))

        sem = semaphores(nc, tag, ctx)
        src_now = sb("src_now", [SLOT, UNIT], I32)
        row_now = sb("row_now", [SLOT, UNIT], I32)
        list_now = sb("list_now", [SLOT, UNIT_COLS], F32)
        pick = sb("pick", [SLOT, UNIT, UNIT_COLS], F32R)
        e_raw = sb("e_raw", [SLOT, UNIT, width], F32)
        e_hi = sb("e_hi", [SLOT, UNIT, width], F32R)
        e_lo = sb("e_lo", [SLOT, UNIT, width], F32R)
        g_hi = sb("g_hi", [128, fc, UNIT_COLS], F32R)
        g_lo = sb("g_lo", [128, fc, UNIT_COLS], F32R)
        w_raw = sb("w_raw", [128, fc, width], F32)
        w_hi = sb("w_hi", [128, fc, width], F32R)
        w_lo = sb("w_lo", [128, fc, width], F32R)
        y = sb("y", [SLOT, UNIT, width], F32)
        ps_g = ctx.enter_context(nc.psum_tensor(f"{tag}_ps_g", [128, 2, BANK], F32))
        ps_y = ctx.enter_context(nc.psum_tensor(f"{tag}_ps_y", [SLOT, UNIT, 2, BANK], F32))

        list_loaded = sem("list_loaded")
        w_loaded = [sem(f"w_loaded{f}") for f in range(fc)]
        index_ready = sem("index_ready")
        gathered = [sem(f"gathered{j}") for j in range(UNIT)]
        scattered = [sem(f"scattered{j}") for j in range(UNIT)]
        picked = sem("picked")
        e_hi_ready = sem("e_hi_ready")
        e_ready = sem("e_ready")
        w_hi_ready = sem("w_hi_ready")
        w_ready = sem("w_ready")
        w_used = sem("w_used")
        g_summed = sem("g_summed")
        g_hi_ready = sem("g_hi_ready")
        g_ready = sem("g_ready")
        y_ready = sem("y_ready")
        y_free = sem("y_free")
        waited = sem("waited")

        def count(eng):
            return eng.value_load(plan[0:1, 3, 0:1], min_val=1, max_val=units - 1)

        def unit(u):
            return nc.s_assert_within(u, 0, units - 2, skip_runtime_bounds_check_because="units - 1 bounds their number")

        def has_third(eng, u):
            return eng.value_load(plan[0:1, 1, bass.ds(u, 1)], min_val=0, max_val=1)

        def if_third(eng, third, body):
            with eng.If(third):
                body(3)
            with eng.Else():
                body(2)

        block = ctx.enter_context(nc.Block())

        @block.sync
        def _(sp):
            def load(u, first):
                kind = sp.value_load(plan[0:1, 0, bass.ds(u, 1)], min_val=0, max_val=w_rel.shape[0] - 1)
                if not first:
                    sp.wait_ge(picked, u)
                sp.dma_start(list_now[:], targets[bass.ds(u, 1), :].broadcast_to([SLOT, UNIT_COLS])).then_inc(list_loaded, 16)
                for f in range(fc):
                    if not first:
                        sp.wait_ge(w_ready, fc * u - fc + f + 1)
                    sp.dma_start(w_raw[:, f, :], w_rel[bass.ds(kind, 1), f * 128:(f + 1) * 128, :].rearrange("a f o -> f (a o)"))\
                        .then_inc(w_loaded[f], 16)

            load(0, True)
            with sp.Fori(1, count(sp) + 1) as u:
                load(nc.s_assert_within(u, 1, units - 1, skip_runtime_bounds_check_because="as above"), False)

        @block.gpsimd
        def _(pool):
            def wait(semaphore, value):
                pool.wait_ge(semaphore, value)
                pool.sem_inc(waited, 1)

            def gather(u, n):
                nc.gpsimd.tensor_copy(src_now[:], src_index[:, bass.ds(UNIT * u, UNIT)]).then_inc(index_ready, 1)
                wait(index_ready, n)
                for j in range(UNIT):
                    nc.gpsimd.indirect_dma_start(out=e_raw[:, j, :], out_offset=None, in_=rows,
                                                 in_offset=bass.IndirectOffsetOnAxis(ap=src_now[:, j:j + 1], axis=0))\
                        .then_inc(gathered[j], 16)

            nc.gpsimd.nop().then_inc(y_free, 1)
            gather(0, 1)
            with pool.Fori(0, count(pool)) as n:
                u = unit(n)
                third = has_third(pool, u)
                thirds = pool.value_load(plan[0:1, 2, bass.ds(u, 1)], min_val=0, max_val=units)
                pool.wait_ge(e_ready, UNIT * u + UNIT)
                gather(u + 1, 2 * u + 2)
                nc.gpsimd.tensor_copy(row_now[:], row_index[:, bass.ds(UNIT * u, UNIT)]).then_inc(index_ready, 1)
                wait(index_ready, 2 * u + 3)
                wait(y_ready, 2 * u + 4)

                def scatter(tiles):
                    for j in range(tiles):
                        nc.gpsimd.indirect_dma_start(out=sums, in_=y[:, j, :], in_offset=None, compute_op=ALU.add,
                                                     out_offset=bass.IndirectOffsetOnAxis(ap=row_now[:, j:j + 1], axis=0))\
                            .then_inc(scattered[j], 16)
                    if tiles == 3:
                        pool.wait_ge(scattered[2], 16 * thirds)

                if_third(pool, third, scatter)
                for j in range(2):
                    pool.wait_ge(scattered[j], 16 * u + 16)
                nc.gpsimd.nop().then_inc(y_free, 1)

        @block.scalar
        def _(act):
            nc.scalar.preload_act_table(ACT.Copy)

            def split_e(u):
                for j in range(UNIT):
                    act.wait_ge(gathered[j], 16 * u + 16)
                    nc.scalar.copy(e_hi[:, j, :], e_raw[:, j, :]).then_inc(e_hi_ready, 1)

            def split_w(u, f):
                act.wait_ge(w_loaded[f], 16 * u + 16)
                nc.scalar.copy(w_hi[:, f, :], w_raw[:, f, :]).then_inc(w_hi_ready, 1)

            split_e(0)
            for f in range(fc):
                split_w(0, f)
            nc.scalar.nop().then_inc(y_ready, 2)
            with act.Fori(0, count(act)) as n:
                u = unit(n)
                third = has_third(act, u)

                def split_g(tiles):
                    for f in range(fc):
                        act.wait_ge(g_summed, fc * u + f + 1)
                        nc.scalar.copy(g_hi[:, f, 0:tiles * SLOT], ps_g[:, f % 2, 0:tiles * SLOT]).then_inc(g_hi_ready, 1)

                if_third(act, third, split_g)
                split_e(u + 1)
                for f in range(fc):
                    act.wait_ge(w_used, fc * u + f + 1)
                    if f == fc - 1:
                        act.wait_ge(y_free, u + 1)
                        nc.scalar.activation(y[:, 1, :].rearrange("p (a o) -> p a o", a=2), ps_y[:, 1, :, 0:half], ACT.Copy,
                                             scale=row_inv[:, bass.ds(UNIT * u + 1, 1)]).then_inc(y_ready, 1)
                    split_w(u + 1, f)

        @block.vector
        def _(dve):
            v = nc.vector

            def make_pick(u):
                dve.wait_ge(list_loaded, 16 * u + 16)
                for j in range(UNIT):
                    ins = v.tensor_scalar(pick[:, j, :], list_now[:], slot_dst[:, bass.ds(UNIT * u + j, 1)], None,
                                          ALU.is_equal)
                ins.then_inc(picked, 1)

            def split_e(u):
                for j in range(UNIT):
                    dve.wait_ge(e_hi_ready, UNIT * u + j + 1)
                    v.tensor_tensor(e_lo[:, j, :], e_raw[:, j, :], e_hi[:, j, :].bitcast(F32), ALU.subtract)\
                        .then_inc(e_ready, 1)

            def split_w(u, f):
                dve.wait_ge(w_hi_ready, fc * u + f + 1)
                v.tensor_tensor(w_lo[:, f, :], w_raw[:, f, :], w_hi[:, f, :].bitcast(F32), ALU.subtract)\
                    .then_inc(w_ready, 1)

            v.engine_nop().then_inc(g_ready, 2)
            make_pick(0)
            split_e(0)
            for f in range(fc):
                split_w(0, f)
            with dve.Fori(0, count(dve)) as n:
                u = unit(n)
                third = has_third(dve, u)

                def split_g(tiles):
                    for f in range(fc):
                        dve.wait_ge(g_hi_ready, fc * u + f + 1)
                        at = slice(0, tiles * SLOT)
                        v.tensor_tensor(g_lo[:, f, at], ps_g[:, f % 2, at], g_hi[:, f, at].bitcast(F32),
                                        ALU.subtract).then_inc(g_ready, 1)

                def take_y(tiles):
                    dve.wait_ge(w_used, fc * u + fc)
                    dve.wait_ge(y_free, u + 1)
                    for j in range(0, tiles, 2):
                        ins = v.tensor_scalar(y[:, j, :].rearrange("p (a o) -> p a o", a=2), ps_y[:, j, :, 0:half],
                                              row_inv[:, bass.ds(UNIT * u + j, 1)], None, ALU.mult)
                    ins.then_inc(y_ready, 1)

                if_third(dve, third, split_g)
                make_pick(u + 1)
                split_e(u + 1)
                for f in range(fc):
                    if f == fc - 1:
                        if_third(dve, third, take_y)
                    split_w(u + 1, f)

        @block.tensor
        def _(pe):
            t = nc.tensor
            with pe.Fori(0, count(pe)) as n:
                u = unit(n)
                third = has_third(pe, u)

                def sums_and_products(tiles):
                    cols = tiles * SLOT
                    pe.wait_ge(picked, u + 1)
                    pe.wait_ge(e_ready, UNIT * u + UNIT)
                    for f in range(fc):
                        pe.wait_ge(g_ready, fc * u + f + 1)
                        for j in range(UNIT):
                            for part, e in enumerate((e_hi, e_lo)):
                                mm = t.matmul(ps_g[:, f % 2, 0:cols], e[:, j, f * 128:(f + 1) * 128], pick[:, j, 0:cols],
                                              start=(j == 0 and part == 0), stop=(j == UNIT - 1 and part == 1))
                        mm.then_inc(g_summed, 1)
                    pe.wait_ge(y_ready, 2 * u + 2)
                    for f in range(fc):
                        pe.wait_ge(g_ready, fc * u + f + 3)
                        pe.wait_ge(w_ready, fc * u + f + 1)
                        for j in range(tiles):
                            at = slice(j * SLOT, (j + 1) * SLOT)
                            for g, w in ((g_hi, w_hi), (g_hi, w_lo), (g_lo, w_hi)):
                                for o in range(2):
                                    mm = t.matmul(ps_y[:, j, o, 0:half], g[:, f, at], w[:, f, o * half:(o + 1) * half],
                                                  start=(f == 0 and g is g_hi and w is w_hi),
                                                  stop=(f == fc - 1 and g is g_lo))
                        mm.then_inc(w_used, 1)

                if_third(pe, third, sums_and_products)


def store_rows(nc, tag, rows, to, zero_from=None):
    width = rows.shape[2]
    with ExitStack() as ctx:
        sem = semaphores(nc, tag, ctx)
        zeros = ctx.enter_context(nc.sbuf_tensor(f"{tag}_zeros", [SLOT, width], F32))
        cleared = sem("cleared")
        stored = sem("stored")
        block = ctx.enter_context(nc.Block())

        @block.vector
        def _(dve):
            nc.vector.memset(zeros[:], 0.0).then_inc(cleared, 1)

        @block.sync
        def _(sp):
            sp.dma_start(to[0:N, :].rearrange("(k p) f -> p k f", p=NP), rows).then_inc(stored, 16)
            sp.wait_ge(stored, 16)
            if to.shape[0] > N:
                sp.wait_ge(cleared, 1)
                sp.dma_start(to[N:N + SLOT, :], zeros[:]).then_inc(stored, 16)
                sp.wait_ge(stored, 32)


def load_rows(nc, tag, source, rows):
    with ExitStack() as ctx:
        sem = semaphores(nc, tag, ctx)
        loaded = sem("loaded")
        block = ctx.enter_context(nc.Block())

        @block.sync
        def _(sp):
            sp.dma_start(rows, source[0:N, :].rearrange("(k p) f -> p k f", p=NP)).then_inc(loaded, 16)
            sp.wait_ge(loaded, 16)


def setup(nc, x_dram, x, ident):
    with ExitStack() as ctx:
        x_loaded = ctx.enter_context(nc.semaphore("x_loaded"))
        ident_cleared = ctx.enter_context(nc.semaphore("ident_cleared"))
        block = ctx.enter_context(nc.Block())

        @block.sync
        def _(sp):
            sp.dma_start(x[:], x_dram.rearrange("(k p) f -> p k f", p=NP)).then_inc(x_loaded, 16)
            sp.wait_ge(x_loaded, 16)

        @block.gpsimd
        def _(pool):
            nc.gpsimd.memset(ident[:], 0.0).then_inc(ident_cleared, 1)
            pool.wait_ge(ident_cleared, 1)
            nc.gpsimd.affine_select(out=ident[:], in_=ident[:], compare_op=ALU.not_equal, fill=1.0, base=0,
                                    pattern=[[-1, 128]], channel_multiplier=1)


def gnn_kernel(nc, d, out):
    dim = d["x"].shape[1]
    wide = dim + d["L2_gnn_node_emb"].shape[1]
    types0 = d["L0_gnn_W_rel"].shape[0]
    types2 = d["L2_gnn_w_rel1"].shape[0]
    keys0, keys2 = (t * NT + t * NT % 2 for t in (types0, types2))
    keys2 = types2 * NT + types2 * NT % 2
    units = slots_of(types0, UNIT) // UNIT
    adj2 = nc.dram_tensor("adj2", (keys2, NP, NC), U16, kind="Internal").ap()
    targets = nc.dram_tensor("targets", (units, UNIT_COLS), F32, kind="Internal").ap()
    rows0 = nc.dram_tensor("rows0", (N, dim), F32, kind="Internal").ap()
    sums0 = nc.dram_tensor("sums0", (N + SLOT, dim), F32, kind="Internal").ap()
    with ExitStack() as ctx:
        def sb(name, shape, dt):
            return ctx.enter_context(nc.sbuf_tensor(name, shape, dt))

        slot_src = sb("s2_slot_src", [SLOT, slots_of(keys2)], F32)
        slot_dst = sb("s2_slot_dst", [SLOT, slots_of(keys2)], F32)
        counts = sb("s2_counts", [1, 2, keys2], I32)
        sort_edges(nc, "s2_sort", d["src"], d["dst"], d["edge_type_3"], keys2, 1, slot_src, slot_dst, counts)
        build_adjacency(nc, "s2_build", keys2, slot_src, slot_dst, counts, adj2)
    with ExitStack() as ctx:
        x = ctx.enter_context(nc.sbuf_tensor("x_rows", [NP, NT, dim], F32))
        h = ctx.enter_context(nc.sbuf_tensor("h_rows", [NP, NT, wide], F32))
        ident = ctx.enter_context(nc.sbuf_tensor("ident", [128, 128], F32))
        adj_all = ctx.enter_context(nc.sbuf_tensor("adj_all", [NP, NT, NC], U16))
        dinv = ctx.enter_context(nc.sbuf_tensor("dinv", [NP, NT], F32))
        setup(nc, d["x"], x, ident)
        sum_adjacency(nc, "all", adj2, types2, adj_all, dinv, ident)

        def gcn(tag, w, b, **how):
            layer(nc, tag, h, dim, dim, d[b], d[w], 1, adj_all=adj_all, dinv=dinv, **how)

        normalise(nc, "n0", x, h)
        store_rows(nc, "n0_rows", h[:, :, 0:dim], rows0)
        layer(nc, "l0_root", h, dim, dim, d["L0_gnn_b_rgcn"], None, 0, w_root=d["L0_gnn_W_root"], ident=ident)
        store_rows(nc, "l0_sums", h[:, :, 0:dim], sums0)
        with ExitStack() as part:
            def sb(name, shape, dt):
                return part.enter_context(nc.sbuf_tensor(name, shape, dt))

            slot_src = sb("s0_slot_src", [SLOT, UNIT * units], F32)
            slot_dst = sb("s0_slot_dst", [SLOT, UNIT * units], F32)
            src_index = sb("s0_src_index", [SLOT, UNIT * units], I32)
            row_index = sb("s0_row_index", [SLOT, UNIT * units], I32)
            row_inv = sb("s0_row_inv", [SLOT, UNIT * units], F32)
            plan = sb("s0_plan", [1, 4, units], I32)
            with ExitStack() as early:
                counts = early.enter_context(nc.sbuf_tensor("s0_counts", [1, 2, types0], I32))
                lots = early.enter_context(nc.sbuf_tensor("s0_lots", [EP, types0], F32))
                tile_of = early.enter_context(nc.sbuf_tensor("s0_tile_of", [EP, EC], F32))
                sort_edges(nc, "s0_sort", d["src"], d["dst"], d["edge_type_34"], types0, UNIT, slot_src, slot_dst,
                           counts, lots, tile_of)
                plan_units(nc, "s0_plan", d["dst"], types0, tile_of, lots, slot_src, slot_dst, units, src_index,
                           row_index, row_inv, targets, plan)
            add_means(nc, "l0_means", units, d["L0_gnn_W_rel"], rows0, sums0, plan, src_index, slot_dst, row_index,
                      row_inv, targets)
        load_rows(nc, "l0_load", sums0, h[:, :, 0:dim])
        gcn("l0b", "L0_gnn_W_gcn", "L0_gnn_b_gcn", x=x)
        normalise(nc, "n1", x, h)
        gcn("l1a", "L1_gnn_W1", "L1_gnn_b1", relu=True)
        gcn("l1b", "L1_gnn_W2", "L1_gnn_b2", x=x)
        normalise(nc, "n2", x, h, extra=(d["node_type_3"], d["L2_gnn_node_emb"]))
        for i, (a, b) in enumerate(((wide, wide), (wide, dim), (dim, dim)), 1):
            layer(nc, f"l2{i}", h, a, b, d[f"L2_gnn_b{i}"], d[f"L2_gnn_w_rel{i}"], types2, adj=adj2,
                  w_root=d[f"L2_gnn_w_root{i}"], ident=ident, relu=True, x=x if i == 3 else None)
        normalise(nc, "n3", x, h)
        gcn("l3", "L3_gnn_W", "L3_gnn_b", x=x)
        stored = ctx.enter_context(nc.semaphore("out_stored"))
        with nc.Block() as block:
            @block.sync
            def _(sp):
                sp.dma_start(out.rearrange("(k p) f -> p k f", p=NP), x[:]).then_inc(stored, 16)
                sp.wait_ge(stored, 16)


_INS = ["x", "src", "dst", "edge_type_3", "edge_type_34", "node_type_3", "L0_gnn_W_rel", "L0_gnn_W_root",
        "L0_gnn_b_rgcn", "L0_gnn_W_gcn", "L0_gnn_b_gcn", "L1_gnn_W1", "L1_gnn_b1", "L1_gnn_W2", "L1_gnn_b2",
        "L2_gnn_node_emb", "L2_gnn_w_rel1", "L2_gnn_w_root1", "L2_gnn_b1", "L2_gnn_w_rel2", "L2_gnn_w_root2",
        "L2_gnn_b2", "L2_gnn_w_rel3", "L2_gnn_w_root3", "L2_gnn_b3", "L3_gnn_W", "L3_gnn_b"]


def kernel(**inputs):
    import numpy as _np
    import concourse.bacc as _bacc
    from concourse import mybir as _mybir
    from concourse.bass_utils import run_bass_kernel_spmd as _run

    nc = _bacc.Bacc("TRN2", target_bir_lowering=False, num_devices=1)
    arrays, aps = {}, {}
    for name in _INS:
        a = _np.ascontiguousarray(inputs[name])
        arrays[f"in_{name}"] = a
        aps[name] = nc.dram_tensor(f"in_{name}", a.shape, _mybir.dt.from_np(a.dtype), kind="ExternalInput").ap()
    out = nc.dram_tensor("out_0", arrays["in_x"].shape, F32, kind="ExternalOutput").ap()
    gnn_kernel(nc, aps, out)
    r = _run(nc, [arrays], core_ids=[0])
    return r.results[0]["out_0"]
```

```python
from contextlib import ExitStack

import concourse.bass as bass
from concourse import mybir

ALU = mybir.AluOpType
ACT = mybir.ActivationFunctionType
AX_X = mybir.AxisListType.X
F32 = mybir.dt.float32
F32R = mybir.dt.float32r
F16 = mybir.dt.float16
I32 = mybir.dt.int32
U16 = mybir.dt.uint16

N = 625
NT = 5
NP = N // NT
NPC = NP + 1
NC = NT * NPC
PART = (3 * NPC, 2 * NPC)
BANK = 512
LEFT = BANK - PART[0]
ROOT_LEFT = BANK - 3 * NP
E = 10625
EP = 125
EC = E // EP
SLOT = 128
LOT = 6
UNIT = 3
UNIT_COLS = UNIT * SLOT
EPS = 1e-5


def column(n_tile):
    return n_tile * NPC


def slots_of(keys, lot):
    return (E // (lot * SLOT) + keys + 1) * lot


def semaphores(nc, tag, ctx):
    made = []

    def clear():
        nc.clear_and_free_semaphores(made)
        nc.all_engine_barrier()

    ctx.callback(clear)

    def sem(name):
        made.append(nc.alloc_semaphore(f"{tag}_{name}"))
        return made[-1]

    return sem


def sort_edges(nc, tag, src, dst, etype, keys, lot, slot_src, slot_dst, counts=None, lots=None, tile_of=None,
               beside=None, aside=None):
    slots = slots_of(keys, lot)
    by_tile = tile_of is None
    chunk = 17
    assert EC % chunk == 0 and slots <= BANK // 2
    with ExitStack() as ctx:
        def sb(name, shape, dt):
            return ctx.enter_context(nc.sbuf_tensor(f"{tag}_{name}", shape, dt))

        sem = semaphores(nc, tag, ctx)

        raw = sb("raw", [EP, 3, EC], I32)
        val = sb("val", [EP, 3, EC], F32)
        node_tile = sb("node_tile", [EP, 2, EC], F32)
        key = sb("key", [EP, EC], F32)
        local_src = sb("local_src", [EP, EC], F32)
        col_dst = sb("col_dst", [EP, EC], F32)
        key_iota = sb("key_iota", [EP, keys], F32)
        is_key = sb("is_key", [EP, keys, EC], F16)
        running = sb("running", [EP, keys, EC], F32)
        zeros = sb("zeros", [EP, 1], F32)
        part_cnt = sb("part_cnt", [EP, keys], F16)
        before = sb("before", [EP, keys], F32)
        lower = sb("lower", [EP, EP], F16)
        ones = sb("ones", [EP, 128], F16)
        total_i = sb("total_i", [EP, keys], I32)
        tiles_f = sb("tiles_f", [EP, keys], F32)
        tiles_end = sb("tiles_end", [EP, keys], F32)
        base = sb("base", [EP, keys], F32)
        pos = sb("pos", [EP, EC], F32)
        pos_i = sb("pos_i", [EP, EC], I32)
        hi_i = sb("hi_i", [EP, EC], I32)
        lo_i = sb("lo_i", [EP, EC], I32)
        hi = sb("hi", [EP, EC], F32)
        slot_iota = sb("slot_iota", [EP, SLOT, chunk], F16)
        tile_iota = sb("tile_iota", [EP, slots], F16)
        slot_of = sb("slot_of", [EP, EC], F16)
        loads = sb("loads", [EP, 2, EC], F16)
        is_slot = sb("is_slot", [EP, 2, SLOT, chunk], F16)
        at_slot = sb("at_slot", [EP, 2, 2, SLOT, chunk], F16)
        is_tile = sb("is_tile", [EP, 2, chunk, slots], F16)
        lots_i = sb("lots_i", [EP, keys], I32)
        if beside is not None:
            spare = sb("spare", [SLOT, UNIT, beside[3].shape[1]], F32)
            x_loaded = sem("x_loaded")
            spare_ready = sem("spare_ready")
            spare_stored = sem("spare_stored")
            ident_cleared = sem("ident_cleared")
        ps_cnt = ctx.enter_context(nc.psum_tensor(f"{tag}_ps_cnt", [EP, 2, BANK // 2], F32))
        ps_slot = ctx.enter_context(nc.psum_tensor(f"{tag}_ps_slot", [SLOT, 2, BANK // 2], F32))

        loaded = sem("loaded")
        consts_ready = sem("consts_ready")
        counted = sem("counted")
        summed = sem("summed")
        chunk_ready = sem("chunk_ready")
        chunk_used = sem("chunk_used")
        step = sem("step")
        done = sem("done")

        block = ctx.enter_context(nc.Block())

        @block.sync
        def _(sp):
            for i, a in enumerate((src, dst, etype)):
                sp.dma_start(raw[:, i, :], a.rearrange("(p c) -> p c", p=EP)).then_inc(loaded, 16)
            if beside is not None:
                x_dram, x, _, spare_rows = beside
                sp.dma_start(x[:], x_dram.rearrange("(k p) f -> p k f", p=NP)).then_inc(x_loaded, 16)
                sp.wait_ge(spare_ready, 1)
                sp.dma_start(spare_rows.rearrange("(t p) f -> p t f", p=SLOT), spare[:]).then_inc(spare_stored, 16)
                sp.wait_ge(x_loaded, 16)
                sp.wait_ge(spare_stored, 16)

        @block.gpsimd
        def _(pool):
            nc.gpsimd.iota(key_iota[:], [[1, keys]], base=0, channel_multiplier=0,
                           allow_small_or_imprecise_dtypes=True).then_inc(consts_ready, 1)
            nc.gpsimd.iota(tile_iota[:], [[1, slots]], base=0, channel_multiplier=0,
                           allow_small_or_imprecise_dtypes=True).then_inc(consts_ready, 1)
            nc.gpsimd.memset(ones[:], 1.0).then_inc(consts_ready, 1)
            nc.gpsimd.memset(zeros[:], 0.0).then_inc(consts_ready, 1)
            nc.gpsimd.memset(lower[:], 1.0).then_inc(consts_ready, 1)
            pool.wait_ge(consts_ready, 5)
            nc.gpsimd.affine_select(out=lower[:], in_=lower[:], compare_op=ALU.is_gt, fill=0.0, base=0,
                                    pattern=[[1, EP]], channel_multiplier=-1).then_inc(consts_ready, 1)
            nc.gpsimd.iota(slot_iota[:], [[1, SLOT], [0, chunk]], base=0, channel_multiplier=0,
                           allow_small_or_imprecise_dtypes=True).then_inc(consts_ready, 1)
            if beside is not None:
                ident = beside[2]
                nc.gpsimd.memset(spare[:], 0.0).then_inc(spare_ready, 1)
                nc.gpsimd.memset(ident[:], 0.0).then_inc(ident_cleared, 1)
                pool.wait_ge(ident_cleared, 1)
                nc.gpsimd.affine_select(out=ident[:], in_=ident[:], compare_op=ALU.not_equal, fill=1.0, base=0,
                                        pattern=[[-1, 128]], channel_multiplier=1)

        @block.vector
        def _(dve):
            chain = [0]

            def then(ins):
                chain[0] += 1
                ins.then_inc(step, 1)
                dve.wait_ge(step, chain[0])

            v = nc.vector
            dve.wait_ge(loaded, 48)
            then(v.tensor_copy(val[:], raw[:]))
            if by_tile:
                then(v.tensor_scalar(node_tile[:], val[:, 0:2, :], float(NP), None, ALU.is_ge))
                for j in range(2, NT):
                    then(v.scalar_tensor_tensor(node_tile[:], val[:, 0:2, :], float(j * NP), node_tile[:],
                                                ALU.is_ge, ALU.add))
                then(v.scalar_tensor_tensor(local_src[:], node_tile[:, 0, :], float(-NP), val[:, 0, :],
                                            ALU.mult, ALU.add))
                then(v.tensor_tensor(col_dst[:], node_tile[:, 1, :], val[:, 1, :], ALU.add))
                then(v.scalar_tensor_tensor(key[:], val[:, 2, :], float(NT), node_tile[:, 0, :], ALU.mult, ALU.add))
            else:
                then(v.tensor_copy(local_src[:], val[:, 0, :]))
                then(v.tensor_copy(col_dst[:], val[:, 1, :]))
                then(v.tensor_copy(key[:], val[:, 2, :]))
            dve.wait_ge(consts_ready, 6)
            then(v.tensor_tensor(is_key[:], key_iota[:].unsqueeze(2).broadcast_to([EP, keys, EC]),
                                 key[:].unsqueeze(1).broadcast_to([EP, keys, EC]), ALU.is_equal))
            flat = is_key[:].rearrange("p k c -> p (k c)")
            then(v.tensor_tensor_scan(running[:].rearrange("p k c -> p (k c)"), flat,
                                      zeros[:].broadcast_to([EP, keys * EC]), 0.0, ALU.add, ALU.add))
            ends = running[:, :, EC - 1]
            then(v.tensor_copy(part_cnt[:, 0:1], ends[:, 0:1]))
            v.tensor_tensor(part_cnt[:, 1:keys], ends[:, 1:keys], ends[:, 0:keys - 1], ALU.subtract).then_inc(counted, 1)
            dve.wait_ge(summed, 1)
            then(v.tensor_scalar(total_i[:], ps_cnt[:, 1, 0:keys], float(SLOT - 1), None, ALU.add))
            then(v.tensor_scalar(total_i[:], total_i[:], 7, None, ALU.logical_shift_right))
            then(v.tensor_scalar(lots_i[:], total_i[:], 1.0 / lot, (lot - 1) / (2 * lot), ALU.mult, ALU.add))
            then(v.tensor_scalar(tiles_f[:], lots_i[:], 1.0, float(lot), ALU.max, ALU.mult))
            then(v.tensor_tensor_scan(tiles_end[:], tiles_f[:], zeros[:].broadcast_to([EP, keys]), 0.0, ALU.add, ALU.add))
            then(v.tensor_tensor(base[:], tiles_end[:], tiles_f[:], ALU.subtract))
            if by_tile:
                then(v.tensor_scalar(counts[0:1, 0, 0:keys], base[0:1, :], 1.0 / lot, None, ALU.mult))
                then(v.tensor_scalar(counts[0:1, 1, 0:keys], tiles_f[0:1, :], 1.0 / lot, None, ALU.mult))
            then(v.scalar_tensor_tensor(before[:], base[:], float(SLOT), ps_cnt[:, 0, 0:keys], ALU.mult, ALU.add))
            then(v.tensor_scalar(before[:], before[:], 1.0, None, ALU.subtract))
            then(v.tensor_tensor(before[:, 1:keys], before[:, 1:keys], ends[:, 0:keys - 1], ALU.subtract))
            then(v.tensor_tensor(running[:], running[:], before[:].unsqueeze(2).broadcast_to([EP, keys, EC]), ALU.add))
            then(v.tensor_tensor(running[:], running[:], is_key[:], ALU.mult))
            then(v.tensor_reduce(pos[:], running[:].rearrange("p k c -> p c k"), AX_X, ALU.add))
            then(v.tensor_copy(pos_i[:], pos[:]))
            then(v.tensor_scalar(hi_i[:], pos_i[:], 7, None, ALU.logical_shift_right))
            then(v.tensor_scalar(lo_i[:], pos_i[:], SLOT - 1, None, ALU.bitwise_and))
            then(v.tensor_copy(hi[:], hi_i[:]))
            if not by_tile:
                then(v.tensor_copy(tile_of[:], hi_i[:]))
                then(v.tensor_scalar(lots[:], tiles_end[:], 1.0 / lot, None, ALU.mult))
            then(v.tensor_copy(slot_of[:], lo_i[:]))
            then(v.tensor_scalar(loads[:, 0, :], local_src[:], 1.0, None, ALU.add))
            then(v.tensor_scalar(loads[:, 1, :], col_dst[:], 1.0, None, ALU.add))
            for n in range(EC // chunk):
                if n >= 2:
                    dve.wait_ge(chunk_used, n - 1)
                at = slice(n * chunk, (n + 1) * chunk)

                def over_slots(row):
                    return row[:, at].unsqueeze(1).broadcast_to([EP, SLOT, chunk])

                if n == 0:
                    dve.wait_ge(consts_ready, 7)
                then(v.tensor_tensor(is_slot[:, n % 2], slot_iota[:], over_slots(slot_of), ALU.is_equal))
                for c in range(chunk):
                    col = n * chunk + c
                    v.tensor_scalar(is_tile[:, n % 2, c, :], tile_iota[:], hi[:, col:col + 1], None, ALU.is_equal)
                for i in range(2):
                    last = v.tensor_tensor(at_slot[:, n % 2, i], is_slot[:, n % 2], over_slots(loads[:, i, :]), ALU.mult)
                last.then_inc(chunk_ready, 1)
            dve.wait_ge(done, 1)
            then(v.tensor_scalar(slot_src[:, 0:slots], ps_slot[:, 0, 0:slots], 1.0, None, ALU.subtract))
            then(v.tensor_scalar(slot_dst[:, 0:slots], ps_slot[:, 1, 0:slots], 1.0, None, ALU.subtract))

        if aside is not None:
            aside_steps = aside(ctx, block, sem)

        @block.tensor
        def _(pe):
            if aside is not None:
                aside_steps[0](pe)
            pe.wait_ge(consts_ready, 6)
            pe.wait_ge(counted, 1)
            nc.tensor.matmul(ps_cnt[:, 0, 0:keys], lower[:], part_cnt[:], start=True, stop=True)
            nc.tensor.matmul(ps_cnt[:, 1, 0:keys], ones[:, 0:EP], part_cnt[:], start=True, stop=True).then_inc(summed, 1)
            for n in range(EC // chunk):
                if aside is not None:
                    aside_steps[1 + n](pe)
                pe.wait_ge(chunk_ready, n + 1)
                for c in range(chunk):
                    for i in range(2):
                        last = nc.tensor.matmul(ps_slot[:, i, 0:slots], at_slot[:, n % 2, i, :, c], is_tile[:, n % 2, c, :],
                                                start=(n == 0 and c == 0 and i == 0),
                                                stop=(n == EC // chunk - 1 and c == chunk - 1), skip_group_check=True)
                last.then_inc(chunk_used, 1)
            pe.wait_ge(chunk_used, EC // chunk)
            nc.tensor.nop().then_inc(done, 1)


def newton_rsqrt(v, then, out, d, tmp):
    then(v.tensor_tensor(tmp, out, out, ALU.mult))
    then(v.tensor_tensor(tmp, tmp, d, ALU.mult))
    then(v.tensor_scalar(tmp, tmp, -0.5, 1.5, ALU.mult, ALU.add))
    then(v.tensor_tensor(out, out, tmp, ALU.mult))


def row_statistics(v, stats, x, k):
    half = x.shape[2] // 2
    for i in range(2):
        last = v.bn_stats(stats[:, k, i, :], x[:, k, i * half:(i + 1) * half])
    return last


def row_scales(v, then, dve, inverted, rooted, count, moments, stats, var, rstd, tmp, tiles):
    at = slice(tiles[0], tiles[-1] + 1)
    for d in tiles:
        last = v.bn_aggr(moments[:, d, :], stats[:, d])
    then(last)
    then(v.tensor_scalar(var[:, at], moments[:, at, 1], EPS, None, ALU.add))
    v.reciprocal(rstd[:, at], var[:, at]).then_inc(inverted, 1)
    dve.wait_ge(rooted, count)
    newton_rsqrt(v, then, rstd[:, at], var[:, at], tmp[:, at])


def build_adjacency(nc, tag, keys, lot, types, slot_src, slot_dst, counts, adj, adj_all, ident, x, h,
                    node_types, emb):
    width = x.shape[2]
    rows, dim = emb.shape
    with ExitStack() as ctx:
        def sb(name, shape, dt):
            return ctx.enter_context(nc.sbuf_tensor(f"{tag}_{name}", shape, dt))

        sem = semaphores(nc, tag, ctx)

        node_iota = sb("node_iota", [SLOT, NC], F16)
        ring = 2
        is_src = sb("is_src", [SLOT, ring, lot, NP], F16)
        is_dst = sb("is_dst", [SLOT, ring, lot, NC], F16)
        zeros = sb("zeros", [SLOT, NP], F16)
        cnt = sb("cnt", [NP, keys, NC], U16)
        type_i = sb("type_i", [NP, NT], I32)
        type_f = sb("type_f", [NP, NT], F32)
        is_type = sb("is_type", [NP, rows, NT], F32)
        emb_rows = sb("emb_rows", [NP, rows, dim], F32)
        stats = sb("stats", [NP, NT, 2, 6], F32)
        moments = sb("moments", [NP, NT, 2], F32)
        var = sb("var", [NP, NT], F32)
        rstd = sb("rstd", [NP, NT], F32)
        tmp = sb("tmp", [NP, NT], F32)
        ps = ctx.enter_context(nc.psum_tensor(f"{tag}_ps", [NP, 2, 2 * BANK], F32))

        types_loaded = sem("types_loaded")
        consts_ready = sem("consts_ready")
        onehots_ready = sem("onehots_ready")
        onehots_free = sem("onehots_free")
        counted = sem("counted")
        copied = sem("copied")
        stored = sem("stored")
        inverted = sem("inverted")
        rooted = sem("rooted")
        step = sem("step")

        lots = slots_of(keys, lot) // lot

        def lot_number(i):
            return nc.s_assert_within(i, 0, lots - 1, skip_runtime_bounds_check_because="all edges fit slots_of tiles")

        block = ctx.enter_context(nc.Block())

        @block.gpsimd
        def _(pool):
            nc.gpsimd.iota(node_iota[:], [[1, NC]], base=0, channel_multiplier=0,
                           allow_small_or_imprecise_dtypes=True).then_inc(consts_ready, 1)
            nc.gpsimd.memset(zeros[:], 0.0).then_inc(consts_ready, 1)

        @block.vector
        def _(dve):
            chain = [0]

            def then(ins):
                chain[0] += 1
                ins.then_inc(step, 1)
                dve.wait_ge(step, chain[0])

            v = nc.vector
            dve.wait_ge(consts_ready, 2)
            first = dve.value_load(counts[0:1, 0, keys - 1:keys], min_val=0, max_val=lots - 1)
            last = dve.value_load(counts[0:1, 1, keys - 1:keys], min_val=1, max_val=lots)
            with dve.Fori(0, first + last) as n:
                i = lot_number(n)
                dve.wait_ge(onehots_free, i + 1)
                for j in range(lot):
                    at = bass.ds(lot * i + j, 1)
                    v.tensor_scalar(is_src[:, i % ring, j, :], node_iota[:, 0:NP], slot_src[:, at], None, ALU.is_equal)
                    ins = v.tensor_scalar(is_dst[:, i % ring, j, :], node_iota[:], slot_dst[:, at], None, ALU.is_equal)
                ins.then_inc(onehots_ready, 1)
            dve.wait_ge(types_loaded, 32)
            then(v.tensor_copy(type_f[:], type_i[:]))
            for t in range(rows):
                ins = v.tensor_scalar(is_type[:, t, :], type_f[:], float(t), None, ALU.is_equal)
            then(ins)
            for t in range(rows):
                for k in range(NT):
                    to = h[:, k, width:width + dim]
                    if t == 0:
                        ins = v.tensor_scalar(to, emb_rows[:, t, :], is_type[:, t, k:k + 1], None, ALU.mult)
                    else:
                        ins = v.scalar_tensor_tensor(to, emb_rows[:, t, :], is_type[:, t, k:k + 1], to, ALU.mult, ALU.add)
                then(ins)
            dve.wait_ge(copied, keys + 2)
            for t in range(1, types):
                before = cnt[:, 0:NT, :] if t == 1 else adj_all[:]
                then(v.tensor_tensor(adj_all[:], before, cnt[:, t * NT:(t + 1) * NT, :], ALU.add))
            for k in range(NT):
                own = adj_all[:, k, column(k):column(k) + NP]
                v.tensor_tensor(own, own, ident[0:NP, 0:NP], ALU.add)
            for k in range(NT):
                ins = row_statistics(v, stats, x, k)
            then(ins)
            row_scales(v, then, dve, inverted, rooted, 1, moments, stats, var, rstd, tmp, range(NT))
            for k in range(NT):
                ins = v.tensor_scalar(h[:, k, 0:width], x[:, k, :], moments[:, k, 0:1], rstd[:, k:k + 1],
                                      ALU.subtract, ALU.mult)
            then(ins)
            v.tensor_scalar(h[:, :, 0:width], h[:, :, 0:width], 0.0, None, ALU.max)

        @block.tensor
        def _(pe):
            t = nc.tensor
            pe.wait_ge(consts_ready, 2)
            t.nop().then_inc(onehots_free, ring)

            def count_key(key, b):
                pe.wait_ge(copied, key + 1)
                for at in (LEFT, BANK):
                    t.matmul(ps[:, b, at:at + 2], zeros[:], zeros[:, 0:2], start=True, stop=False)
                first = pe.value_load(counts[0:1, 0, bass.ds(key, 1)], min_val=0, max_val=lots - 1)
                number = pe.value_load(counts[0:1, 1, bass.ds(key, 1)], min_val=1, max_val=lots)
                with pe.Fori(first, first + number) as n:
                    i = lot_number(n)
                    pe.wait_ge(onehots_ready, i + 1)
                    for j in range(lot):
                        for h in range(2):
                            cols = slice(0, PART[0]) if h == 0 else slice(PART[0], NC)
                            at = LEFT if h == 0 else BANK
                            mm = t.matmul(ps[:, b, at:at + PART[h]], is_src[:, i % ring, j, :],
                                          is_dst[:, i % ring, j, cols], start=False, stop=False, skip_group_check=True)
                    mm.then_inc(onehots_free, 1)
                for at in (LEFT, BANK):
                    mm = t.matmul(ps[:, b, at:at + 2], zeros[:], zeros[:, 0:2], start=False, stop=True)
                mm.then_inc(counted, 1)

            with pe.Fori(0, keys // 2) as pair:
                for b in range(2):
                    count_key(2 * pair + b, b)
            if keys % 2:
                count_key(keys - 1, 0)

        @block.scalar
        def _(act):
            nc.scalar.preload_act_table(ACT.Sqrt)
            nc.scalar.nop().then_inc(copied, 2)

            def copy_key(key, b):
                act.wait_ge(counted, key + 1)
                nc.scalar.copy(cnt[:, bass.ds(key, 1), :].rearrange("p k c -> p (k c)"),
                               ps[:, b, LEFT:LEFT + NC]).then_inc(copied, 1)

            with act.Fori(0, keys // 2) as pair:
                for b in range(2):
                    copy_key(2 * pair + b, b)
            if keys % 2:
                copy_key(keys - 1, 0)
            act.wait_ge(inverted, 1)
            nc.scalar.activation(rstd[:], rstd[:], ACT.Sqrt).then_inc(rooted, 1)

        @block.sync
        def _(sp):
            with nc.allow_non_contiguous_dma(reason="five node types per partition"):
                sp.dma_start(type_i[:], node_types.rearrange("(k p) -> p k", p=NP)).then_inc(types_loaded, 16)
            sp.dma_start(emb_rows[:], emb.unsqueeze(0).broadcast_to([NP, rows, dim])).then_inc(types_loaded, 16)
            sp.wait_ge(copied, keys + 2)
            sp.dma_start(adj.rearrange("k p c -> p k c"), cnt[:]).then_inc(stored, 16)
            sp.wait_ge(stored, 16)


def load_rows(nc, block, sem, source, h, parts, dinv, adj_all, a, ones_f, ones):
    width = source.shape[1]
    wide = h.shape[2]
    h_hi, h_lo = parts
    loaded = [sem(f"load_rows{k}") for k in range(NT)]
    rows_ready = sem("load_ready")
    hi_ready = sem("load_hi_ready")
    split = sem("load_split")
    ones_ready = sem("load_ones_ready")

    @block.sync
    def _(sp):
        for k in range(NT):
            sp.dma_start(h[:, k, 0:width], source[k * NP:(k + 1) * NP, :]).then_inc(loaded[k], 16)

    @block.gpsimd
    def _(pool):
        nc.gpsimd.memset(ones_f[:], 1.0).then_inc(ones_ready, 1)
        pool.wait_ge(ones_ready, 1)
        nc.gpsimd.tensor_copy(ones[:], ones_f[:]).then_inc(ones_ready, 1)

    @block.scalar
    def _(act):
        nc.scalar.preload_act_table(ACT.Sqrt)
        nc.scalar.copy(a[:], adj_all[:])
        for k in range(NT):
            act.wait_ge(rows_ready, k + 1)
            nc.scalar.copy(h_hi[:, k, 0:width], h[:, k, 0:width]).then_inc(hi_ready, 1)
        nc.scalar.copy(h_hi[:, :, width:wide], h[:, :, width:wide]).then_inc(hi_ready, 1)

    @block.vector
    def _(dve):
        v = nc.vector

        def scale(k):
            dve.wait_ge(loaded[k], 16)
            v.tensor_scalar(h[:, k, 0:width], h[:, k, 0:width], dinv[:, k:k + 1], None, ALU.mult).then_inc(rows_ready, 1)

        scale(0)
        for k in range(NT):
            if k < NT - 1:
                scale(k + 1)
            dve.wait_ge(hi_ready, k + 1)
            v.tensor_tensor(h_lo[:, k, 0:width], h[:, k, 0:width], h_hi[:, k, 0:width].bitcast(F32),
                            ALU.subtract).then_inc(split, 1)
        dve.wait_ge(hi_ready, NT + 1)
        v.tensor_tensor(h_lo[:, :, width:wide], h[:, :, width:wide], h_hi[:, :, width:wide].bitcast(F32), ALU.subtract)
        dve.wait_ge(ones_ready, 2)

    return split


RING = 3


def layer_buffers(nc, tag, ctx, width, out_width, mean):
    fc = width // 128
    made = {}

    def sb(name, shape, dt):
        made[name] = ctx.enter_context(nc.sbuf_tensor(f"{tag}_{name}", shape, dt))

    if mean:
        sb("a_raw", [NP, NT, NC], U16)
        sb("ones", [NP, 128], F32R)
        sb("ones_f", [NP, 128], F32)
        sb("inv", [128, NC], F32)
        sb("scaled", [128, 2, NC], F32)
    sb("g_hi", [128, fc, NC], F32R)
    sb("g_lo", [128, fc, NC], F32R)
    sb("w_raw", [128, RING, out_width], F32)
    sb("w_hi", [128, fc, out_width], F32R)
    sb("w_lo", [128, fc, out_width], F32R)
    sb("bias_rows", [NP, 2, out_width], F32)
    sb("stats", [NP, NT, 2, 6], F32)
    sb("moments", [NP, NT, 2], F32)
    sb("var", [NP, NT], F32)
    sb("rstd", [NP, NT], F32)
    sb("tmp", [NP, NT], F32)
    made["ps_g"] = ctx.enter_context(nc.psum_tensor(f"{tag}_ps_g", [128, 2, 2 * BANK], F32))
    made["ps_o"] = ctx.enter_context(nc.psum_tensor(f"{tag}_ps_o", [128, 2, 2, BANK], F32))
    return made


def root_rows(nc, ctx, block, sem, h, bias, w_root, ident, store_first, store_to):
    width = w_root.shape[0]
    fc = width // 128
    half = width // 2

    def sb(name, shape, dt):
        return ctx.enter_context(nc.sbuf_tensor(f"root_{name}", shape, dt))

    g_raw = sb("g_raw", [128, 2, NT, NP], F32)
    g_hi = sb("g_hi", [128, fc, NT, NP + 1], F32R)
    g_lo = sb("g_lo", [128, fc, NT, NP + 1], F32R)
    w_raw = sb("w_raw", [128, RING, width], F32)
    w_hi = sb("w_hi", [128, fc, width], F32R)
    w_lo = sb("w_lo", [128, fc, width], F32R)
    bias_row = sb("bias_row", [1, width], F32)
    bias_hi = sb("bias_hi", [1, width], F32R)
    bias_lo = sb("bias_lo", [1, width], F32R)
    ones_f = sb("ones_f", [1, 128], F32)
    ones = sb("ones", [1, 128], F32R)
    ps_g = ctx.enter_context(nc.psum_tensor("root_ps_g", [128, 2 * BANK], F32))
    ps_o = ctx.enter_context(nc.psum_tensor("root_ps_o", [128, 2, 2, BANK], F32))

    bias_loaded = sem("bias_loaded")
    ones_ready = sem("ones_ready")
    bias_hi_ready = sem("bias_hi_ready")
    bias_ready = sem("bias_ready")
    w_loaded = [sem(f"w_loaded{f}") for f in range(fc)]
    w_hi_ready = sem("w_hi_ready")
    w_ready = sem("w_ready")
    rows_stored = sem("rows_stored")
    turned = sem("turned")
    g_raw_ready = sem("g_raw_ready")
    g_hi_ready = sem("g_hi_ready")
    g_ready = sem("g_ready")
    o_summed = sem("o_summed")
    o_taken = sem("o_taken")
    result_stored = sem("result_stored")

    def nodes(cols):
        return cols.rearrange("p (k c) -> p k c", c=NP)

    @block.sync
    def _(sp):
        sp.dma_start(bias_row[:], bias.unsqueeze(0)).then_inc(bias_loaded, 16)
        sp.dma_start(store_first.rearrange("(k p) f -> p k f", p=NP), h[:, :, 0:width]).then_inc(rows_stored, 16)
        for f in range(fc):
            if f >= RING:
                sp.wait_ge(w_ready, f - RING + 1)
            sp.dma_start(w_raw[:, f % RING, :], w_root[f * 128:(f + 1) * 128, :]).then_inc(w_loaded[f], 16)
        for d in range(NT):
            sp.wait_ge(o_taken, d + 1)
            sp.dma_start(store_to[d * NP:(d + 1) * NP, :], h[:, d, 0:width]).then_inc(result_stored, 16)
        sp.wait_ge(result_stored, 16 * NT)

    @block.gpsimd
    def _(pool):
        nc.gpsimd.memset(ones_f[:], 1.0).then_inc(ones_ready, 1)
        pool.wait_ge(ones_ready, 1)
        nc.gpsimd.tensor_copy(ones[:], ones_f[:]).then_inc(ones_ready, 1)
        for f in range(fc):
            pool.wait_ge(g_hi_ready, f + 1)
            nc.gpsimd.tensor_tensor(g_lo[:, f, :, 0:NP], g_raw[:, f % 2], g_hi[:, f, :, 0:NP].bitcast(F32),
                                    ALU.subtract).then_inc(g_ready, 1)
            pool.wait_ge(w_hi_ready, f + 1)
            nc.gpsimd.tensor_tensor(w_lo[:, f, :], w_raw[:, f % RING, :], w_hi[:, f, :].bitcast(F32), ALU.subtract)\
                .then_inc(w_ready, 1)
            if f == 0:
                pool.wait_ge(bias_hi_ready, 1)
                nc.gpsimd.tensor_tensor(bias_lo[:], bias_row[:], bias_hi[:].bitcast(F32), ALU.subtract)\
                    .then_inc(bias_ready, 1)

    @block.scalar
    def _(act):
        nc.scalar.preload_act_table(ACT.Copy)
        act.wait_ge(bias_loaded, 16)
        nc.scalar.copy(bias_hi[:], bias_row[:]).then_inc(bias_hi_ready, 1)
        for f in range(fc):
            act.wait_ge(turned, f + 1)
            if f >= 2:
                act.wait_ge(g_ready, f - 1)
            nc.scalar.copy(g_raw[:, f % 2], nodes(ps_g[:, ROOT_LEFT:ROOT_LEFT + N])).then_inc(g_raw_ready, 1)
            act.wait_ge(g_raw_ready, f + 1)
            nc.scalar.copy(g_hi[:, f, :, 0:NP], g_raw[:, f % 2]).then_inc(g_hi_ready, 1)
            act.wait_ge(w_loaded[f], 16)
            nc.scalar.copy(w_hi[:, f, :], w_raw[:, f % RING, :]).then_inc(w_hi_ready, 1)
        act.wait_ge(rows_stored, 16)
        for d in range(NT):
            act.wait_ge(o_summed, d + 1)
            nc.scalar.copy(h[:, d, 0:width].rearrange("p (a o) -> p a o", a=2), ps_o[0:NP, d % 2, :, 0:half])\
                .then_inc(o_taken, 1)

    t = nc.tensor

    def turn(pe, chunks):
        for f in chunks:
            if f:
                pe.wait_ge(g_raw_ready, f)
            for d in range(NT):
                at = ROOT_LEFT + d * NP
                mm = t.transpose(ps_g[:, at:at + NP], h[:, d, f * 128:(f + 1) * 128], ident[0:NP, 0:NP])
            mm.then_inc(turned, 1)

    def products(pe, d):
        if d == 0:
            pe.wait_ge(ones_ready, 2)
            pe.wait_ge(bias_ready, 1)
        if d >= 2:
            pe.wait_ge(o_taken, d - 1)
        for a in range(2):
            cols = slice(a * half, (a + 1) * half)
            out = ps_o[0:NP, d % 2, a, 0:half]
            t.matmul(out, ones[:, 0:NP], bias_hi[:, cols], start=True, stop=False)
            t.matmul(out, ones[:, 0:NP], bias_lo[:, cols], start=False, stop=False)
            for f in range(fc):
                if d == 0 and a == 0:
                    pe.wait_ge(g_ready, f + 1)
                    pe.wait_ge(w_ready, f + 1)
                for g, w in ((g_hi, w_hi), (g_hi, w_lo), (g_lo, w_hi)):
                    mm = t.matmul(out, g[:, f, d, 0:NP], w[:, f, cols], start=False, stop=(f == fc - 1 and g is g_lo))
        mm.then_inc(o_summed, 1)

    def step(*tiles, chunks=()):
        def run(pe):
            turn(pe, chunks)
            for d in tiles:
                products(pe, d)

        return run

    return step(chunks=range(2)), step(0, 1, chunks=range(2, fc)), step(2), step(3), step(4), step()


GROUPS = ((0, 1, 2), (3, 4))
LAG = 2


def layer(nc, block, sem, buffers, index, before, tag, h, parts, a, width, out_width, bias, w_rel, relations,
          adj=None, w_root=None, adj_all=None, dinv=None, relu=False, x=None, norm=False, next_scale=None,
          keep_rows=False, ident=None, store_to=None):
    mean = adj is not None
    fc = width // 128
    half = out_width // 2
    steps = relations + (w_root is not None)
    ring = RING
    h_hi, h_lo = parts or (None, None)
    g_hi, g_lo, ps_g, ps_o = (buffers[name] for name in ("g_hi", "g_lo", "ps_g", "ps_o"))
    stats, moments, var, rstd, tmp = (buffers[name] for name in ("stats", "moments", "var", "rstd", "tmp"))
    w_raw, w_hi, w_lo = (buffers[name][:, :, 0:out_width] for name in ("w_raw", "w_hi", "w_lo"))
    bias_rows = buffers["bias_rows"][:, index % 2, 0:out_width]
    if mean:
        a_raw, ones, inv, scaled = (buffers[name] for name in ("a_raw", "ones", "inv", "scaled"))
    rows_split_before, weights_split_before, weights_before = before or (None, None, 0)

    def named(name, used=True):
        return sem(f"{tag}_{name}") if used else None

    bias_loaded = named("bias_loaded")
    w_loaded = [named(f"w_loaded{s}") for s in range(ring)]
    w_hi_ready = named("w_hi_ready")
    w_ready = named("w_ready")
    a_loaded = named("a_loaded", mean)
    a_ready = named("a_ready", mean)
    inv_ready = named("inv_ready", mean)
    g_freed = named("g_freed", mean)
    g_summed = named("g_summed")
    g_hi_ready = named("g_hi_ready")
    g_ready = named("g_ready")
    o_summed = named("o_summed")
    o_taken = named("o_taken")
    result_ready = named("result_ready", x is not None or store_to is not None)
    result_stored = named("result_stored", store_to is not None)
    inverted = named("inverted", norm)
    rooted = named("rooted", norm)
    step = named("step", norm)
    rows_ready = named("rows_ready", norm or relu)
    hi_ready = named("hi_ready", norm or relu)
    rows_split = named("rows_split", norm or relu)

    root = w_root is not None
    per = fc + 1 if mean else fc

    def sums_before(r):
        return (fc if root else 0) + r * per

    def step_of(r):
        return r + root

    def all_nodes(cols):
        return cols.rearrange("p (k c) -> p k c", c=NPC)[:, :, 0:NP]

    @block.sync
    def _(sp):
        def load_w(w, s):
            for f in range(fc):
                if f >= ring:
                    sp.wait_ge(w_ready, s * fc + f - ring + 1)
                elif not (isinstance(s, int) and s == 0):
                    sp.wait_ge(w_ready, s * fc - (fc - 1 - last_in(f)))
                sp.dma_start(w_raw[:, f % ring, :], w(f)).then_inc(w_loaded[f % ring], 16)

        def last_in(place):
            return max(f for f in range(fc) if f % ring == place)

        if weights_split_before is not None:
            sp.wait_ge(weights_split_before, weights_before)
        sp.dma_start(bias_rows, bias.unsqueeze(0).broadcast_to([NP, out_width])).then_inc(bias_loaded, 16)
        if root:
            load_w(lambda f: w_root[f * 128:(f + 1) * 128, :], 0)
        if mean:
            with sp.Fori(0, relations) as r:
                sp.wait_ge(a_ready, r + 1)
                sp.dma_start(a_raw[:], adj[bass.ds(r * NT, NT), :, :].rearrange("k p c -> p k c")).then_inc(a_loaded, 16)
                load_w(lambda f: w_rel[bass.ds(r, 1), f * 128:(f + 1) * 128, :].rearrange("a f o -> f (a o)"), step_of(r))
        elif relations:
            load_w(lambda f: w_rel[f * 128:(f + 1) * 128, :], 0)
        if store_to is not None:
            result = h if x is None else x
            for d in range(NT):
                sp.wait_ge(result_ready, d + 1)
                sp.dma_start(store_to[d * NP:(d + 1) * NP, :], result[:, d, 0:out_width]).then_inc(result_stored, 16)
            sp.wait_ge(result_stored, NT * 16)

    @block.scalar
    def _(act):
        if before is None:
            nc.scalar.preload_act_table(ACT.Sqrt)

        def weights(s, f, uses):
            act.wait_ge(w_loaded[f % ring], 16 * (s * uses + f // ring + 1))
            if f == 0 and not (isinstance(s, int) and s == 0):
                act.wait_ge(o_summed, s * NT)
            nc.scalar.copy(w_hi[:, f, :], w_raw[:, f % ring, :]).then_inc(w_hi_ready, 1)

        def chunk(s, f, to, source, uses, which, k):
            weights(s, f, uses)
            act.wait_ge(which, k)
            nc.scalar.copy(to, source).then_inc(g_hi_ready, 1)

        def uses_of(f):
            return len([g for g in range(fc) if g % ring == f % ring])

        if root:
            for f in range(fc + LAG):
                if f < fc:
                    act.wait_ge(g_summed, f + 1)
                    nc.scalar.copy(all_nodes(g_hi[:, f, :]), all_nodes(ps_g[:, f % 2, LEFT:LEFT + NC]))\
                        .then_inc(g_hi_ready, 1)
                if f >= LAG:
                    weights(0, f - LAG, uses_of(f - LAG))
        if mean:
            nc.scalar.nop().then_inc(a_ready, 1)
            with act.Fori(0, relations) as r:
                act.wait_ge(a_loaded, 16 * r + 16)
                act.wait_ge(g_summed, sums_before(r))
                nc.scalar.copy(a[:], a_raw[:]).then_inc(a_ready, 1)
                for f in range(fc):
                    chunk(step_of(r), f, g_hi[:, f, :], scaled[:, f % 2, :], uses_of(f), g_freed, r * per + f + 3)
        elif relations:
            for f in range(fc):
                chunk(0, f, g_hi[:, f, :], ps_g[:, f % 2, LEFT:LEFT + NC], uses_of(f), g_summed, f + 1)
        if mean and adj_all is not None:
            act.wait_ge(g_summed, sums_before(relations))
            nc.scalar.copy(a[:], adj_all[:])
        if norm:
            for i, group in enumerate(GROUPS):
                at = slice(group[0], group[-1] + 1)
                act.wait_ge(inverted, i + 1)
                nc.scalar.activation(rstd[:, at], rstd[:, at], ACT.Sqrt).then_inc(rooted, 1)
                for d in group:
                    act.wait_ge(rows_ready, d + 1)
                    nc.scalar.activation(h_hi[:, d, 0:out_width], h[:, d, 0:out_width], ACT.Relu).then_inc(hi_ready, 1)
        elif x is None and relu:
            for d in range(NT):
                act.wait_ge(rows_ready, d + 1)
                nc.scalar.copy(h_hi[:, d, 0:out_width], h[:, d, 0:out_width]).then_inc(hi_ready, 1)

    @block.vector
    def _(dve):
        v = nc.vector
        chain = [0]

        def then(ins):
            chain[0] += 1
            ins.then_inc(step, 1)
            dve.wait_ge(step, chain[0])

        def w_low(s, f):
            dve.wait_ge(w_hi_ready, s * fc + f + 1)
            v.tensor_tensor(w_lo[:, f, :], w_raw[:, f % ring, :], w_hi[:, f, :].bitcast(F32),
                            ALU.subtract).then_inc(w_ready, 1)

        def g_low(s, f, source, only=lambda cols: cols):
            dve.wait_ge(g_hi_ready, s * fc + f + 1)
            v.tensor_tensor(only(g_lo[:, f, :]), only(source), only(g_hi[:, f, :].bitcast(F32)),
                            ALU.subtract).then_inc(g_ready, 1)

        def take(s, first, last):
            for d in range(NT):
                dve.wait_ge(o_summed, s * NT + d + 1)
                ps = ps_o[0:NP, d % 2, :, 0:half]
                to = h[:, d, 0:out_width].rearrange("p (a o) -> p a o", a=2)
                by = dinv[:, d:d + 1] if dinv is not None else 1.0
                if first:
                    base = bias_rows.rearrange("p (a o) -> p a o", a=2)
                else:
                    base = to
                v.scalar_tensor_tensor(to, ps, by, base, ALU.mult, ALU.add).then_inc(o_taken, 1)
                if last:
                    dve.wait_ge(o_taken, s * NT + d + 1)
                    finish(d)

        def finish(d):
            rows = h[:, d, 0:out_width]
            if x is None:
                if relu:
                    v.tensor_scalar(rows, rows, 0.0, 1.0 if next_scale is None else next_scale[:, d:d + 1],
                                    ALU.max, ALU.mult).then_inc(rows_ready, 1)
                    dve.wait_ge(hi_ready, d + 1)
                    v.tensor_tensor(h_lo[:, d, 0:out_width], rows, h_hi[:, d, 0:out_width].bitcast(F32),
                                    ALU.subtract).then_inc(rows_split, 1)
                return
            if relu:
                ins = v.scalar_tensor_tensor(x[:, d, :], rows, 0.0, x[:, d, :], ALU.max, ALU.add)
            else:
                ins = v.tensor_tensor(x[:, d, :], x[:, d, :], rows, ALU.add)
            ins.then_inc(result_ready, 1)
            if norm:
                dve.wait_ge(result_ready, d + 1)
                ins = row_statistics(v, stats, x, d)
                for i, group in enumerate(GROUPS):
                    if d == group[-1]:
                        then(ins)
                        normalise_group(i, group)

        def normalise_group(i, group):
            at = slice(group[0], group[-1] + 1)
            row_scales(v, then, dve, inverted, rooted, i + 1, moments, stats, var, rstd, tmp, group)
            if next_scale is not None:
                then(v.tensor_tensor(rstd[:, at], rstd[:, at], next_scale[:, at], ALU.mult))
            for d in group:
                v.tensor_scalar(h[:, d, 0:out_width], x[:, d, :], moments[:, d, 0:1], rstd[:, d:d + 1],
                                ALU.subtract, ALU.mult).then_inc(rows_ready, 1)
            for d in group:
                rows = h[:, d, 0:out_width]
                dve.wait_ge(hi_ready, d + 1)
                ins = v.scalar_tensor_tensor(h_lo[:, d, 0:out_width], rows, 0.0, h_hi[:, d, 0:out_width].bitcast(F32),
                                             ALU.max, ALU.subtract)
                if keep_rows:
                    ins = v.tensor_scalar(rows, rows, 0.0, None, ALU.max)
                ins.then_inc(rows_split, 1)

        dve.wait_ge(bias_loaded, 16)
        if root:
            for f in range(fc + LAG):
                if f < fc:
                    g_low(0, f, ps_g[:, f % 2, LEFT:LEFT + NC], all_nodes)
                if f >= LAG:
                    w_low(0, f - LAG)
            take(0, True, steps == 1)
        if mean:
            v.engine_nop().then_inc(g_freed, 1)

            def mean_step(r, last):
                s = step_of(r)
                dve.wait_ge(g_summed, sums_before(r) + 1)
                v.tensor_scalar(inv[:], ps_g[:, 0, LEFT:LEFT + NC], 1.0, None, ALU.max).then_inc(g_freed, 1)
                dve.wait_ge(g_freed, r * per + 2)
                v.reciprocal(inv[:], inv[:]).then_inc(inv_ready, 1)
                dve.wait_ge(inv_ready, r + 1)
                for f in range(fc + 1):
                    if f < fc:
                        dve.wait_ge(g_summed, sums_before(r) + f + 2)
                        if f >= 2:
                            dve.wait_ge(g_ready, s * fc + f - 1)
                        v.tensor_tensor(scaled[:, f % 2, :], ps_g[:, (f + 1) % 2, LEFT:LEFT + NC], inv[:],
                                        ALU.mult).then_inc(g_freed, 1)
                        w_low(s, f)
                    if f >= 1:
                        dve.wait_ge(g_freed, r * per + f + 2)
                        g_low(s, f - 1, scaled[:, (f - 1) % 2, :])
                take(s, False, last)

            with dve.Fori(0, relations - 1) as r:
                mean_step(r, False)
            mean_step(relations - 1, True)
        elif relations:
            for f in range(fc):
                w_low(0, f)
                g_low(0, f, ps_g[:, f % 2, LEFT:LEFT + NC])
            take(0, True, True)

    @block.tensor
    def _(pe):
        t = nc.tensor

        def products(s):
            for d in range(NT):
                if d >= 2:
                    pe.wait_ge(o_taken, s * NT + d - 1)
                elif not (isinstance(s, int) and s == 0):
                    pe.wait_ge(o_taken, s * NT)
                for a_half in range(2):
                    cols = slice(a_half * half, (a_half + 1) * half)
                    for f in range(fc):
                        if d == 0 and a_half == 0:
                            pe.wait_ge(g_ready, s * fc + f + 1)
                            pe.wait_ge(w_ready, s * fc + f + 1)
                        rows = slice(column(d), column(d) + NP)
                        out = ps_o[0:NP, d % 2, a_half, 0:half]
                        t.matmul(out, g_hi[:, f, rows], w_hi[:, f, cols], start=(f == 0), stop=False)
                        t.matmul(out, g_hi[:, f, rows], w_lo[:, f, cols], start=False, stop=False)
                        mm = t.matmul(out, g_lo[:, f, rows], w_hi[:, f, cols], start=False, stop=(f == fc - 1))
                mm.then_inc(o_summed, 1)

        def wait_rows(k):
            if rows_split_before is not None:
                pe.wait_ge(rows_split_before, k + 1)

        def over_edges(r, first):
            for f in range(fc):
                if mean:
                    pe.wait_ge(g_freed, r * per + f + 1)
                elif f >= 2:
                    pe.wait_ge(g_ready, f - 1)
                buf = (first + f) % 2
                for k in range(NT):
                    if not mean and f == 0:
                        wait_rows(k)
                    for part, rows in enumerate((h_hi, h_lo)):
                        for p in range(2):
                            at, cols = (LEFT, slice(0, PART[0])) if p == 0 else (BANK, slice(PART[0], NC))
                            mm = t.matmul(ps_g[:, buf, at:at + PART[p]], rows[:, k, f * 128:(f + 1) * 128],
                                          a[:, k, cols], start=(k == 0 and part == 0),
                                          stop=(k == NT - 1 and part == 1))
                mm.then_inc(g_summed, 1)

        if root:
            for f in range(fc):
                if f >= 2:
                    pe.wait_ge(g_ready, f - 1)
                for d in range(NT):
                    if f == 0:
                        wait_rows(d)
                    at = LEFT + column(d)
                    mm = t.transpose(ps_g[:, f % 2, at:at + NP], h[:, d, f * 128:(f + 1) * 128], ident[0:NP, 0:NP])
                mm.then_inc(g_summed, 1)
            products(0)
        if mean:
            with pe.Fori(0, relations) as r:
                pe.wait_ge(a_ready, r + 2)
                pe.wait_ge(g_freed, r * per + 1)
                for k in range(NT):
                    for p in range(2):
                        at, cols = (LEFT, slice(0, PART[0])) if p == 0 else (BANK, slice(PART[0], NC))
                        mm = t.matmul(ps_g[:, 0, at:at + PART[p]], ones[:], a[:, k, cols],
                                      start=(k == 0), stop=(k == NT - 1))
                mm.then_inc(g_summed, 1)
                over_edges(r, 1)
                products(step_of(r))
        elif relations:
            over_edges(0, 0)
            products(0)

    return rows_split, w_ready, steps * fc


TWO = 2 * SLOT


def plan_units(nc, tag, dst, types, tile_of, lots, slot_src, slot_dst, units, src_index, row_index, row_inv, targets,
               plan, dinv):
    u_max = units
    with ExitStack() as ctx:
        def sb(name, shape, dt):
            return ctx.enter_context(nc.sbuf_tensor(f"{tag}_{name}", shape, dt))

        sem = semaphores(nc, tag, ctx)
        node_half = (320, N - 320)
        cols = 3 * UNIT
        dst_i = sb("dst_i", [EP, EC], I32)
        dst_f = sb("dst_f", [EP, EC], F32)
        unit_i = sb("unit_i", [EP, EC], I32)
        unit = sb("unit", [EP, EC], F32)
        node_iota = sb("node_iota", [EP, N], F16)
        unit_iota = sb("unit_iota", [EP, u_max], F32)
        is_unit = sb("is_unit", [EP, EC, u_max], F16)
        is_node = sb("is_node", [EP, 4, N], F16)
        lot_ge = sb("lot_ge", [EP, u_max, types], F32)
        type_of = sb("type_of", [EP, u_max], F32)
        type_col = sb("type_col", [u_max, 1], F32)
        same_type = sb("same_type", [u_max, u_max], F32)
        cnt = sb("cnt", [u_max, N], F32)
        present = sb("present", [u_max, N], F32)
        zeros = sb("zeros", [u_max, 1], F32)
        rank = sb("rank", [u_max, N], F32)
        third = sb("third", [u_max, 1], F32)
        type_cnt = sb("type_cnt", [u_max, N], F32)
        rank_t = sb("rank_t", [NP, NT, u_max], F32)
        cnt_t = sb("cnt_t", [NP, NT, u_max], F32)
        rank_ti = sb("rank_ti", [NP, NT, u_max], I32)
        hi_i = sb("hi_i", [NP, NT, u_max], I32)
        lo_i = sb("lo_i", [NP, NT, u_max], I32)
        rank_hi = sb("rank_hi", [NP, NT, u_max], F32)
        rank_lo = sb("rank_lo", [NP, NT, u_max], F16)
        cnt_hi = sb("cnt_hi", [NP, NT, u_max], F32)
        cnt_lo = sb("cnt_lo", [NP, NT, u_max], F32)
        node_num = sb("node_num", [NP, NT], F32)
        slot_iota = sb("slot_iota", [NP, SLOT, u_max], F16)
        tile_iota = sb("tile_iota", [NP, UNIT], F32)
        is_slot = sb("is_slot", [NP, 2, SLOT, u_max], F16)
        is_tile = sb("is_tile", [NP, 2, u_max, UNIT], F32)
        load = sb("load", [NP, 2, u_max, 3, UNIT], F16)
        ident = sb("ident", [128, 128], F32)
        spare = sb("spare", [SLOT, UNIT], F32)
        row_dst = sb("row_dst", [SLOT, u_max, UNIT], F32)
        empty = sb("empty", [SLOT, u_max, UNIT], F32)
        row_cnt = sb("row_cnt", [SLOT, u_max, UNIT], F32)
        row_f = sb("row_f", [SLOT, u_max, UNIT], F32)
        list_rows = sb("list_rows", [128, 2, SLOT], F32)
        flags = sb("flags", [1, u_max], F32)
        ones = sb("ones", [u_max, 2], F32)
        deg = sb("deg", [NP, NT], F32)
        tmp = sb("tmp", [NP, NT], F32)
        ps_cnt = ctx.enter_context(nc.psum_tensor(f"{tag}_ps_cnt", [u_max, 2, BANK], F32))
        ps_t = ctx.enter_context(nc.psum_tensor(f"{tag}_ps_t", [NP, 2, BANK], F32))
        per_bank = BANK // cols
        ps_row = ctx.enter_context(nc.psum_tensor(f"{tag}_ps_row", [SLOT, 2, BANK], F32))
        ps_x = ctx.enter_context(nc.psum_tensor(f"{tag}_ps_x", [128, 2, 256], F32))
        assert u_max <= 2 * per_bank

        loaded = sem("loaded")
        consts_ready = sem("consts_ready")
        nodes_ready = sem("nodes_ready")
        nodes_used = sem("nodes_used")
        counted = sem("counted")
        type_ready = sem("type_ready")
        type_turned = sem("type_turned")
        same_ready = sem("same_ready")
        type_counted = sem("type_counted")
        ranked = sem("ranked")
        turned = sem("turned")
        rows_ready = sem("rows_ready")
        rows_used = sem("rows_used")
        rows_done = sem("rows_done")
        lists_ready = sem("lists_ready")
        lists_turned = sem("lists_turned")
        lists_copied = sem("lists_copied")
        degrees_summed = sem("degrees_summed")
        inverted = sem("inverted")
        rooted = sem("rooted")
        stored = sem("stored")
        step = sem("step")

        block = ctx.enter_context(nc.Block())

        @block.sync
        def _(sp):
            sp.dma_start(dst_i[:], dst.rearrange("(p c) -> p c", p=EP)).then_inc(loaded, 16)
            sp.wait_ge(lists_copied, 1)
            flat = targets.rearrange("u (t s) -> (u t) s", s=SLOT)
            sp.dma_start(flat[0:128, :], list_rows[:, 0, :]).then_inc(stored, 16)
            sp.dma_start(flat[128:UNIT * u_max, :], list_rows[0:UNIT * u_max - 128, 1, :]).then_inc(stored, 16)
            sp.wait_ge(stored, 32)

        @block.gpsimd
        def _(pool):
            def iota(to, pattern, channel=0, base=0):
                nc.gpsimd.iota(to, pattern, base=base, channel_multiplier=channel,
                               allow_small_or_imprecise_dtypes=True).then_inc(consts_ready, 1)

            iota(node_iota[:], [[1, N]])
            iota(unit_iota[:], [[1, u_max]])
            iota(tile_iota[:], [[1, UNIT]])
            iota(node_num[:], [[NP, NT]], channel=1, base=1)
            iota(spare[:], [[SLOT, UNIT]], channel=1, base=N)
            nc.gpsimd.memset(zeros[:], 0.0).then_inc(consts_ready, 1)
            nc.gpsimd.memset(ones[:], 1.0).then_inc(consts_ready, 1)
            nc.gpsimd.memset(ident[:], 0.0).then_inc(consts_ready, 1)
            pool.wait_ge(consts_ready, 8)
            nc.gpsimd.affine_select(out=ident[:], in_=ident[:], compare_op=ALU.not_equal, fill=1.0, base=0,
                                    pattern=[[-1, 128]], channel_multiplier=1).then_inc(consts_ready, 1)
            iota(slot_iota[:], [[1, SLOT], [0, u_max]])

        @block.scalar
        def _(act):
            nc.scalar.preload_act_table(ACT.Sqrt)
            act.wait_ge(inverted, 1)
            nc.scalar.activation(dinv[:], dinv[:], ACT.Sqrt).then_inc(rooted, 1)

        @block.vector
        def _(dve):
            chain = [0]

            def then(ins):
                chain[0] += 1
                ins.then_inc(step, 1)
                dve.wait_ge(step, chain[0])

            v = nc.vector
            dve.wait_ge(loaded, 16)
            dve.wait_ge(consts_ready, 9)
            then(v.tensor_copy(dst_f[:], dst_i[:]))
            then(v.tensor_scalar(unit_i[:], tile_of[:], 1.0 / UNIT, -1.0 / UNIT, ALU.mult, ALU.add))
            then(v.tensor_copy(unit[:], unit_i[:]))
            then(v.tensor_tensor(is_unit[:], unit_iota[:].unsqueeze(1).broadcast_to([EP, EC, u_max]),
                                 unit[:].unsqueeze(2).broadcast_to([EP, EC, u_max]), ALU.is_equal))
            for c in range(EC):
                if c >= 4:
                    dve.wait_ge(nodes_used, c - 3)
                v.tensor_scalar(is_node[:, c % 4, :], node_iota[:], dst_f[:, c:c + 1], None,
                                ALU.is_equal).then_inc(nodes_ready, 1)
            then(v.tensor_tensor(lot_ge[:], unit_iota[:].unsqueeze(2).broadcast_to([EP, u_max, types]),
                                 lots[:].unsqueeze(1).broadcast_to([EP, u_max, types]), ALU.is_ge))
            then(v.tensor_reduce(type_of[:], lot_ge[:], AX_X, ALU.add))
            v.tensor_scalar(type_of[:], type_of[:], float(types - 1), None, ALU.min).then_inc(type_ready, 1)
            dve.wait_ge(type_ready, 1)
            then(v.tensor_copy(plan[0:1, 0, 0:u_max], type_of[0:1, :]))
            then(v.tensor_copy(plan[0:1, 3, 0:1], lots[0:1, types - 1:types]))
            dve.wait_ge(type_turned, 1)
            then(v.tensor_copy(type_col[:], ps_x[0:u_max, 0, 0:1]))
            v.tensor_scalar(same_type[:], type_of[0:u_max, :], type_col[:], None, ALU.is_equal).then_inc(same_ready, 1)
            dve.wait_ge(counted, 1)
            then(v.tensor_copy(cnt[:, 0:node_half[0]], ps_cnt[:, 0, 0:node_half[0]]))
            v.tensor_copy(cnt[:, node_half[0]:N], ps_cnt[:, 1, 0:node_half[1]]).then_inc(same_ready, 1)
            dve.wait_ge(same_ready, 2)
            then(v.tensor_scalar(present[:], cnt[:], 1.0, None, ALU.min))
            then(v.tensor_tensor_scan(rank[:], present[:], zeros[:].broadcast_to([u_max, N]), 0.0, ALU.add, ALU.add))
            then(v.tensor_scalar(third[:], rank[:, N - 1:N], float(TWO), None, ALU.is_gt))
            then(v.tensor_scalar(rank[:], rank[:], -1.0 - (4 * SLOT - 1), None, ALU.add))
            then(v.tensor_tensor(rank[:], rank[:], present[:], ALU.mult))
            then(v.tensor_scalar(rank[:], rank[:], float(4 * SLOT - 1), None, ALU.add))
            dve.wait_ge(degrees_summed, 1)
            then(v.tensor_scalar(deg[:], ps_x[0:NP, 0, SLOT:SLOT + 2 * NT].rearrange("p (k a) -> p k a", a=2)[:, :, 0], 1.0,
                                 None, ALU.add))
            v.reciprocal(dinv[:], deg[:]).then_inc(inverted, 1)
            dve.wait_ge(type_counted, 1)
            then(v.tensor_copy(type_cnt[:, 0:node_half[0]], ps_cnt[:, 0, 0:node_half[0]]))
            v.tensor_copy(type_cnt[:, node_half[0]:N], ps_cnt[:, 1, 0:node_half[1]]).then_inc(ranked, 1)
            dve.wait_ge(turned, 1)
            then(v.tensor_copy(rank_t[:], ps_t[:, 0, 0:NT * u_max].rearrange("p (k u) -> p k u", k=NT)))
            then(v.tensor_copy(cnt_t[:], ps_t[:, 1, 0:NT * u_max].rearrange("p (k u) -> p k u", k=NT)))
            then(v.tensor_copy(plan[0:1, 1, 0:u_max], ps_x[0:1, 1, 0:u_max]))
            then(v.tensor_tensor_scan(flags[:], ps_x[0:1, 1, 0:u_max], zeros[0:1, :].broadcast_to([1, u_max]), 0.0,
                                      ALU.add, ALU.add))
            then(v.tensor_copy(plan[0:1, 2, 0:u_max], flags[:]))
            dve.wait_ge(rooted, 1)
            newton_rsqrt(v, then, dinv[:], deg[:], tmp[:])
            for whole, high, low in ((rank_t, rank_hi, rank_lo), (cnt_t, cnt_hi, cnt_lo)):
                then(v.tensor_copy(rank_ti[:], whole[:]))
                then(v.tensor_scalar(hi_i[:], rank_ti[:], 7, None, ALU.logical_shift_right))
                then(v.tensor_scalar(lo_i[:], rank_ti[:], SLOT - 1, None, ALU.bitwise_and))
                then(v.tensor_copy(high[:], hi_i[:]))
                then(v.tensor_copy(low[:], lo_i[:]))
            dve.wait_ge(consts_ready, 10)
            for k in range(NT):
                if k >= 2:
                    dve.wait_ge(rows_used, k - 1)
                here = is_tile[:, k % 2]

                def over_tiles(a):
                    return a[:, k, :].unsqueeze(2).broadcast_to([NP, u_max, UNIT])

                then(v.tensor_tensor(here, tile_iota[:].unsqueeze(1).broadcast_to([NP, u_max, UNIT]),
                                     over_tiles(rank_hi), ALU.is_equal))
                v.tensor_scalar(load[:, k % 2, :, 0, :], here, node_num[:, k:k + 1], None, ALU.mult)
                v.tensor_tensor(load[:, k % 2, :, 1, :], here, over_tiles(cnt_hi), ALU.mult)
                v.tensor_tensor(load[:, k % 2, :, 2, :], here, over_tiles(cnt_lo), ALU.mult)
                v.tensor_tensor(is_slot[:, k % 2], slot_iota[:], rank_lo[:, k, :].unsqueeze(1).broadcast_to([NP, SLOT, u_max]),
                                ALU.is_equal).then_inc(rows_ready, 1)
            dve.wait_ge(rows_done, 1)
            for bank in range(2):
                u0, u1 = bank * per_bank, min(u_max, (bank + 1) * per_bank)
                ps = ps_row[:, bank, 0:(u1 - u0) * cols].rearrange("p (u a t) -> p u a t", a=3, t=UNIT)
                v.tensor_scalar(row_dst[:, u0:u1, :], ps[:, :, 0, :], -1.0, None, ALU.add)
                v.tensor_scalar(row_f[:, u0:u1, :], ps[:, :, 1, :], float(SLOT), None, ALU.mult)
                then(v.tensor_copy(row_cnt[:, u0:u1, :], ps[:, :, 2, :]))
            then(v.tensor_tensor(row_cnt[:], row_cnt[:], row_f[:], ALU.add))
            then(v.tensor_scalar(row_cnt[:], row_cnt[:], 1.0, None, ALU.max))
            v.reciprocal(row_inv[:].rearrange("p (u t) -> p u t", t=UNIT), row_cnt[:])
            then(v.tensor_scalar(empty[:], row_dst[:], 0.0, None, ALU.is_lt))
            then(v.tensor_tensor(row_f[:], empty[:], spare[:].unsqueeze(1).broadcast_to([SLOT, u_max, UNIT]), ALU.mult))
            then(v.tensor_tensor(row_f[:], row_f[:], empty[:], ALU.add))
            then(v.tensor_tensor(row_index[:].rearrange("p (u t) -> p u t", t=UNIT), row_f[:], row_dst[:], ALU.add))
            v.tensor_tensor(row_dst[:], row_dst[:], empty[:], ALU.subtract).then_inc(lists_ready, 1)
            then(v.tensor_scalar(src_index[:], slot_src[:], 0.0, None, ALU.max))
            dve.wait_ge(lists_turned, 1)
            then(v.tensor_copy(list_rows[:, 0, :], ps_x[:, 0, 0:SLOT]))
            v.tensor_copy(list_rows[0:UNIT * u_max - 128, 1, :],
                          ps_x[0:UNIT * u_max - 128, 1, 0:SLOT]).then_inc(lists_copied, 1)

        @block.tensor
        def _(pe):
            t = nc.tensor
            for c in range(EC):
                pe.wait_ge(nodes_ready, c + 1)
                t.matmul(ps_cnt[:, 0, 0:node_half[0]], is_unit[:, c, :], is_node[:, c % 4, 0:node_half[0]],
                         start=(c == 0), stop=(c == EC - 1))
                t.matmul(ps_cnt[:, 1, 0:node_half[1]], is_unit[:, c, :], is_node[:, c % 4, node_half[0]:N],
                         start=(c == 0), stop=(c == EC - 1)).then_inc(nodes_used, 1)
            pe.wait_ge(nodes_used, EC)
            t.nop().then_inc(counted, 1)
            pe.wait_ge(type_ready, 1)
            t.transpose(ps_x[0:u_max, 0, 0:1], type_of[0:1, :], ident[0:1, 0:1]).then_inc(type_turned, 1)
            pe.wait_ge(same_ready, 2)
            for k in range(NT):
                at = SLOT + 2 * k
                mm = t.matmul(ps_x[0:NP, 0, at:at + 2], cnt[:, k * NP:(k + 1) * NP], ones[:], start=True, stop=True)
            mm.then_inc(degrees_summed, 1)
            pe.wait_ge(same_ready, 2)
            t.matmul(ps_cnt[:, 0, 0:node_half[0]], same_type[:], cnt[:, 0:node_half[0]], start=True, stop=True)
            t.matmul(ps_cnt[:, 1, 0:node_half[1]], same_type[:], cnt[:, node_half[0]:N],
                     start=True, stop=True).then_inc(type_counted, 1)
            pe.wait_ge(ranked, 1)
            for k in range(NT):
                for i, a in enumerate((rank, type_cnt)):
                    t.transpose(ps_t[:, i, k * u_max:(k + 1) * u_max], a[:, k * NP:(k + 1) * NP], ident[0:u_max, 0:u_max])
            t.transpose(ps_x[0:1, 1, 0:u_max], third[:], ident[0:u_max, 0:u_max]).then_inc(turned, 1)
            for k in range(NT):
                pe.wait_ge(rows_ready, k + 1)
                for u in range(u_max):
                    at = u % per_bank * cols
                    mm = t.matmul(ps_row[:, u // per_bank, at:at + cols], is_slot[:, k % 2, :, u],
                                  load[:, k % 2, u].rearrange("p a t -> p (a t)"), start=(k == 0 and u % per_bank == 0),
                                  stop=(k == NT - 1 and u in (per_bank - 1, u_max - 1)), skip_group_check=True)
                mm.then_inc(rows_used, 1)
            pe.wait_ge(rows_used, NT)
            t.nop().then_inc(rows_done, 1)
            pe.wait_ge(lists_ready, 1)
            flat = row_dst[:].rearrange("p u t -> p (u t)")
            t.transpose(ps_x[:, 0, 0:SLOT], flat[:, 0:128], ident[:])
            t.transpose(ps_x[0:UNIT * u_max - 128, 1, 0:SLOT], flat[:, 128:UNIT * u_max], ident[:]).then_inc(lists_turned, 1)


def add_means(nc, tag, units, w_rel, rows, sums, plan, src_index, slot_dst, row_index, row_inv, targets):
    width = rows.shape[1]
    fc = width // 128
    half = width // 2
    with ExitStack() as ctx:
        def sb(name, shape, dt):
            return ctx.enter_context(nc.sbuf_tensor(f"{tag}_{name}", shape, dt))

        sem = semaphores(nc, tag, ctx)
        src_now = sb("src_now", [SLOT, UNIT], I32)
        row_now = sb("row_now", [SLOT, UNIT], I32)
        list_now = sb("list_now", [SLOT, UNIT_COLS], F32)
        pick = sb("pick", [SLOT, UNIT, UNIT_COLS], F32R)
        e_raw = sb("e_raw", [SLOT, UNIT, width], F32)
        e_hi = sb("e_hi", [SLOT, UNIT, width], F32R)
        e_lo = sb("e_lo", [SLOT, UNIT, width], F32R)
        g_hi = sb("g_hi", [128, fc, UNIT_COLS], F32R)
        g_lo = sb("g_lo", [128, fc, UNIT_COLS], F32R)
        w_raw = sb("w_raw", [128, fc, width], F32)
        w_hi = sb("w_hi", [128, fc, width], F32R)
        w_lo = sb("w_lo", [128, fc, width], F32R)
        y = sb("y", [SLOT, UNIT, width], F32)
        ps_g = ctx.enter_context(nc.psum_tensor(f"{tag}_ps_g", [128, 2, BANK], F32))
        ps_y = ctx.enter_context(nc.psum_tensor(f"{tag}_ps_y", [SLOT, UNIT, 2, BANK], F32))

        list_loaded = sem("list_loaded")
        w_loaded = [sem(f"w_loaded{f}") for f in range(fc)]
        index_ready = sem("index_ready")
        gathered = [sem(f"gathered{j}") for j in range(UNIT)]
        scattered = [sem(f"scattered{j}") for j in range(UNIT)]
        picked = sem("picked")
        e_hi_ready = sem("e_hi_ready")
        e_ready = sem("e_ready")
        w_hi_ready = sem("w_hi_ready")
        w_ready = sem("w_ready")
        w_used = sem("w_used")
        g_summed = sem("g_summed")
        g_hi_ready = sem("g_hi_ready")
        g_ready = sem("g_ready")
        y_ready = sem("y_ready")
        y_free = sem("y_free")
        waited = sem("waited")

        def count(eng):
            return eng.value_load(plan[0:1, 3, 0:1], min_val=1, max_val=units - 1)

        def unit(u):
            return nc.s_assert_within(u, 0, units - 2, skip_runtime_bounds_check_because="units - 1 bounds their number")

        def has_third(eng, u):
            return eng.value_load(plan[0:1, 1, bass.ds(u, 1)], min_val=0, max_val=1)

        def if_third(eng, third, body):
            with eng.If(third):
                body(3)
            with eng.Else():
                body(2)

        def per_bank(tiles):
            return BANK // (tiles * SLOT)

        def sums_in_bank(i, tiles):
            per = per_bank(tiles)
            bank = ps_y[:, 2, 0, :] if is_spare(i, tiles) else ps_g[:, i % 2, :]
            return bank[:, 0:per * tiles * SLOT].rearrange("p (c s) -> p c s", c=per)

        def is_spare(i, tiles):
            return tiles == 2 and i == 2

        assert fc % 2 == 0 and fc <= 3 * per_bank(2)

        block = ctx.enter_context(nc.Block())

        @block.sync
        def _(sp):
            def load(u, first):
                kind = sp.value_load(plan[0:1, 0, bass.ds(u, 1)], min_val=0, max_val=w_rel.shape[0] - 1)
                if not first:
                    sp.wait_ge(picked, u)
                sp.dma_start(list_now[:], targets[bass.ds(u, 1), :].broadcast_to([SLOT, UNIT_COLS])).then_inc(list_loaded, 16)
                for f in range(fc):
                    if not first:
                        sp.wait_ge(w_ready, fc * u - fc + f + 1)
                    sp.dma_start(w_raw[:, f, :], w_rel[bass.ds(kind, 1), f * 128:(f + 1) * 128, :].rearrange("a f o -> f (a o)"))\
                        .then_inc(w_loaded[f], 16)

            load(0, True)
            end = count(sp)
            with sp.Fori(1, end + 1) as u:
                load(nc.s_assert_within(u, 1, units - 1, skip_runtime_bounds_check_because="as above"), False)
            sp.wait_ge(w_loaded[fc - 1], 16 * end + 16)
            sp.sem_inc(waited, 1)

        @block.gpsimd
        def _(pool):
            def wait(semaphore, value):
                pool.wait_ge(semaphore, value)
                pool.sem_inc(waited, 1)

            def gather(u, n):
                nc.gpsimd.tensor_copy(src_now[:], src_index[:, bass.ds(UNIT * u, UNIT)]).then_inc(index_ready, 1)
                wait(index_ready, n)
                for j in range(UNIT):
                    nc.gpsimd.indirect_dma_start(out=e_raw[:, j, :], out_offset=None, in_=rows,
                                                 in_offset=bass.IndirectOffsetOnAxis(ap=src_now[:, j:j + 1], axis=0))\
                        .then_inc(gathered[j], 16)

            def scatter(u, n, third):
                nc.gpsimd.tensor_copy(row_now[:], row_index[:, bass.ds(UNIT * u, UNIT)]).then_inc(index_ready, 1)
                wait(index_ready, n)
                wait(y_ready, 2 * u + 4)

                def add(tiles):
                    for j in range(tiles):
                        nc.gpsimd.indirect_dma_start(out=sums, in_=y[:, j, :], in_offset=None, compute_op=ALU.add,
                                                     out_offset=bass.IndirectOffsetOnAxis(ap=row_now[:, j:j + 1], axis=0))\
                            .then_inc(scattered[j], 16)

                if_third(pool, third, add)

            def added(u, third, thirds):
                for j in range(2):
                    pool.wait_ge(scattered[j], 16 * u + 16)
                pool.sem_inc(waited, 1)
                with pool.If(third):
                    pool.wait_ge(scattered[2], 16 * thirds)
                    pool.sem_inc(waited, 1)

            def thirds_to(u):
                return pool.value_load(plan[0:1, 2, bass.ds(u, 1)], min_val=0, max_val=units)

            nc.gpsimd.nop().then_inc(y_free, 1)
            gather(0, 1)
            third = has_third(pool, 0)
            pool.wait_ge(e_ready, UNIT)
            gather(1, 2)
            scatter(0, 3, third)
            with pool.Fori(1, count(pool)) as n:
                u = nc.s_assert_within(n, 1, units - 2, skip_runtime_bounds_check_because="units - 1 bounds their number")
                third, third_before, thirds_before = has_third(pool, u), has_third(pool, u - 1), thirds_to(u - 1)
                wait(e_ready, UNIT * u + UNIT)
                gather(u + 1, 2 * u + 2)
                added(u - 1, third_before, thirds_before)
                nc.gpsimd.nop().then_inc(y_free, 1)
                scatter(u, 2 * u + 3, third)
            end = count(pool)
            last = nc.s_assert_within(end - 1, 0, units - 2, skip_runtime_bounds_check_because="units - 1 bounds their number")
            third, thirds = has_third(pool, last), thirds_to(last)
            added(last, third, thirds)

        @block.scalar
        def _(act):
            nc.scalar.preload_act_table(ACT.Copy)

            def split_e(u, j):
                act.wait_ge(gathered[j], 16 * u + 16)
                nc.scalar.copy(e_hi[:, j, :], e_raw[:, j, :]).then_inc(e_hi_ready, 1)

            def split_w(u, f):
                act.wait_ge(w_loaded[f], 16 * u + 16)
                nc.scalar.copy(w_hi[:, f, :], w_raw[:, f, :]).then_inc(w_hi_ready, 1)

            for j in range(UNIT):
                split_e(0, j)
            for f in range(fc - 1):
                split_w(0, f)
            nc.scalar.nop().then_inc(y_ready, 2)
            with act.Fori(0, count(act)) as n:
                u = unit(n)
                third = has_third(act, u)

                def split_g(tiles):
                    per = per_bank(tiles)
                    for f in range(0, fc, per):
                        act.wait_ge(g_summed, fc * u + f + per)
                        nc.scalar.copy(g_hi[:, f:f + per, 0:tiles * SLOT], sums_in_bank(f // per, tiles)).then_inc(g_hi_ready, per)
                        if f == 0:
                            split_w(u, fc - 1)

                if_third(act, third, split_g)
                for f in range(fc):
                    act.wait_ge(w_used, fc * u + f + 1)
                    if f == fc - 1:
                        act.wait_ge(y_free, u + 1)
                        nc.scalar.activation(y[:, 1, :].rearrange("p (a o) -> p a o", a=2), ps_y[:, 1, :, 0:half], ACT.Copy,
                                             scale=row_inv[:, bass.ds(UNIT * u + 1, 1)]).then_inc(y_ready, 1)
                    else:
                        split_w(u + 1, f)
                    if 0 < f <= UNIT:
                        split_e(u + 1, f - 1)

        @block.vector
        def _(dve):
            v = nc.vector

            def make_pick(u):
                dve.wait_ge(list_loaded, 16 * u + 16)
                for j in range(UNIT):
                    ins = v.tensor_scalar(pick[:, j, :], list_now[:], slot_dst[:, bass.ds(UNIT * u + j, 1)], None,
                                          ALU.is_equal)
                ins.then_inc(picked, 1)

            def split_e(u, j):
                dve.wait_ge(e_hi_ready, UNIT * u + j + 1)
                v.tensor_tensor(e_lo[:, j, :], e_raw[:, j, :], e_hi[:, j, :].bitcast(F32), ALU.subtract)\
                    .then_inc(e_ready, 1)

            def split_w(u, f):
                dve.wait_ge(w_hi_ready, fc * u + f + 1)
                v.tensor_tensor(w_lo[:, f, :], w_raw[:, f, :], w_hi[:, f, :].bitcast(F32), ALU.subtract)\
                    .then_inc(w_ready, 1)

            v.engine_nop().then_inc(g_ready, 2)
            make_pick(0)
            for j in range(UNIT):
                split_e(0, j)
            for f in range(fc - 1):
                split_w(0, f)
            with dve.Fori(0, count(dve)) as n:
                u = unit(n)
                third = has_third(dve, u)

                def split_g(tiles):
                    per = per_bank(tiles)
                    for f in range(0, fc, per):
                        dve.wait_ge(g_hi_ready, fc * u + f + per)
                        at = slice(0, tiles * SLOT)
                        v.tensor_tensor(g_lo[:, f:f + per, at], sums_in_bank(f // per, tiles),
                                        g_hi[:, f:f + per, at].bitcast(F32), ALU.subtract).then_inc(g_ready, per)
                        if f == 0:
                            split_w(u, fc - 1)

                def take_y(tiles):
                    dve.wait_ge(w_used, fc * u + fc)
                    dve.wait_ge(y_free, u + 1)
                    for j in range(0, tiles, 2):
                        ins = v.tensor_scalar(y[:, j, :].rearrange("p (a o) -> p a o", a=2), ps_y[:, j, :, 0:half],
                                              row_inv[:, bass.ds(UNIT * u + j, 1)], None, ALU.mult)
                    ins.then_inc(y_ready, 1)

                if_third(dve, third, split_g)
                make_pick(u + 1)
                for f in range(fc - 1):
                    split_w(u + 1, f)
                    if 0 < f <= UNIT:
                        split_e(u + 1, f - 1)
                if_third(dve, third, take_y)

        @block.tensor
        def _(pe):
            t = nc.tensor
            with pe.Fori(0, count(pe)) as n:
                u = unit(n)
                third = has_third(pe, u)

                def sums_and_products(tiles):
                    cols = tiles * SLOT
                    pe.wait_ge(picked, u + 1)
                    pe.wait_ge(e_ready, UNIT * u + UNIT)
                    per = per_bank(tiles)
                    for f in range(fc):
                        if f % per == 0 and is_spare(f // per, tiles):
                            pe.wait_ge(y_ready, 2 * u + 2)
                        elif f % per == 0:
                            pe.wait_ge(g_ready, fc * u + max(f - per, 0) + 2)
                        sums = sums_in_bank(f // per, tiles)[:, f % per, :]
                        for j in range(UNIT):
                            for part, e in enumerate((e_hi, e_lo)):
                                mm = t.matmul(sums, e[:, j, f * 128:(f + 1) * 128], pick[:, j, 0:cols],
                                              start=(j == 0 and part == 0), stop=(j == UNIT - 1 and part == 1))
                        if f % per == per - 1:
                            mm.then_inc(g_summed, per)
                    pe.wait_ge(y_ready, 2 * u + 2)
                    for f in range(fc):
                        pe.wait_ge(g_ready, fc * u + f + 3)
                        pe.wait_ge(w_ready, fc * u + f + 1)
                        for j in range(tiles):
                            at = slice(j * SLOT, (j + 1) * SLOT)
                            for g, w in ((g_hi, w_hi), (g_hi, w_lo), (g_lo, w_hi)):
                                for o in range(2):
                                    mm = t.matmul(ps_y[:, j, o, 0:half], g[:, f, at], w[:, f, o * half:(o + 1) * half],
                                                  start=(f == 0 and g is g_hi and w is w_hi),
                                                  stop=(f == fc - 1 and g is g_lo))
                        mm.then_inc(w_used, 1)

                if_third(pe, third, sums_and_products)


def gnn_kernel(nc, d, out):
    dim = d["x"].shape[1]
    wide = dim + d["L2_gnn_node_emb"].shape[1]
    types0 = d["L0_gnn_W_rel"].shape[0]
    types2 = d["L2_gnn_w_rel1"].shape[0]
    keys2 = types2 * NT
    units = slots_of(types0, UNIT) // UNIT
    adj2 = nc.dram_tensor("adj2", (keys2, NP, NC), U16, kind="Internal").ap()
    targets = nc.dram_tensor("targets", (units, UNIT_COLS), F32, kind="Internal").ap()
    rows0 = nc.dram_tensor("rows0", (N, dim), F32, kind="Internal").ap()
    sums0 = nc.dram_tensor("sums0", (N + UNIT_COLS, dim), F32, kind="Internal").ap()
    with ExitStack() as ctx:
        x = ctx.enter_context(nc.sbuf_tensor("x_rows", [NP, NT, dim], F32))
        h = ctx.enter_context(nc.sbuf_tensor("h_rows", [NP, NT, wide], F32))
        ident = ctx.enter_context(nc.sbuf_tensor("ident", [128, 128], F32))
        adj_all = ctx.enter_context(nc.sbuf_tensor("adj_all", [NP, NT, NC], U16))
        dinv = ctx.enter_context(nc.sbuf_tensor("dinv", [NP, NT], F32))
        with ExitStack() as part:
            def sb(name, shape, dt):
                return part.enter_context(nc.sbuf_tensor(name, shape, dt))

            slot_src = sb("s2_slot_src", [SLOT, slots_of(keys2, LOT)], F32)
            slot_dst = sb("s2_slot_dst", [SLOT, slots_of(keys2, LOT)], F32)
            counts = sb("s2_counts", [1, 2, keys2], I32)
            sort_edges(nc, "s2_sort", d["src"], d["dst"], d["edge_type_3"], keys2, LOT, slot_src, slot_dst, counts,
                       beside=(d["x"], x, ident, sums0[N:N + UNIT_COLS, :]))
            build_adjacency(nc, "s2_build", keys2, LOT, types2, slot_src, slot_dst, counts, adj2, adj_all, ident,
                            x, h, d["node_type_3"], d["L2_gnn_node_emb"])

        with ExitStack() as part:
            def sb(name, shape, dt):
                return part.enter_context(nc.sbuf_tensor(name, shape, dt))

            slot_src = sb("s0_slot_src", [SLOT, UNIT * units], F32)
            slot_dst = sb("s0_slot_dst", [SLOT, UNIT * units], F32)
            src_index = sb("s0_src_index", [SLOT, UNIT * units], I32)
            row_index = sb("s0_row_index", [SLOT, UNIT * units], I32)
            row_inv = sb("s0_row_inv", [SLOT, UNIT * units], F32)
            plan = sb("s0_plan", [1, 4, units], I32)
            with ExitStack() as early:
                lots = early.enter_context(nc.sbuf_tensor("s0_lots", [EP, types0], F32))
                tile_of = early.enter_context(nc.sbuf_tensor("s0_tile_of", [EP, EC], F32))
                sort_edges(nc, "s0_sort", d["src"], d["dst"], d["edge_type_34"], types0, UNIT, slot_src, slot_dst,
                           lots=lots, tile_of=tile_of,
                           aside=lambda where, block, sem: root_rows(nc, where, block, sem, h, d["L0_gnn_b_rgcn"],
                                                                     d["L0_gnn_W_root"], ident, rows0, sums0[0:N, :]))
                plan_units(nc, "s0_plan", d["dst"], types0, tile_of, lots, slot_src, slot_dst, units, src_index,
                           row_index, row_inv, targets, plan, dinv)
            add_means(nc, "l0_means", units, d["L0_gnn_W_rel"], rows0, sums0, plan, src_index, slot_dst, row_index,
                      row_inv, targets)
        parts = [ctx.enter_context(nc.sbuf_tensor(f"h_{part}", [NP, NT, wide], F32R)) for part in ("hi", "lo")]
        a = ctx.enter_context(nc.sbuf_tensor("a", [NP, NT, NC], F32R))
        sem = semaphores(nc, "layers", ctx)
        buffers = layer_buffers(nc, "layers", ctx, wide, wide, True)
        block = ctx.enter_context(nc.Block())
        rows_split = load_rows(nc, block, sem, sums0[0:N, :], h, parts, dinv, adj_all, a, buffers["ones_f"],
                               buffers["ones"])
        before = (rows_split, None, 0)
        done = 0

        def next_layer(*args, **how):
            nonlocal before, done
            before = layer(nc, block, sem, buffers, done, before, *args, **how)
            done += 1

        def gcn(tag, w, b, **how):
            next_layer(tag, h, parts, a, dim, dim, d[b], d[w], 1, dinv=dinv, **how)

        def rgcn(i, width, out_width, **how):
            next_layer(f"l2{i}", h, parts, a, width, out_width, d[f"L2_gnn_b{i}"], d[f"L2_gnn_w_rel{i}"], types2,
                       adj=adj2, w_root=d[f"L2_gnn_w_root{i}"], ident=ident, relu=True, **how)

        gcn("l0b", "L0_gnn_W_gcn", "L0_gnn_b_gcn", x=x, norm=True, next_scale=dinv)
        gcn("l1a", "L1_gnn_W1", "L1_gnn_b1", relu=True, next_scale=dinv)
        gcn("l1b", "L1_gnn_W2", "L1_gnn_b2", x=x, norm=True, keep_rows=True)
        rgcn(1, wide, wide)
        rgcn(2, wide, dim)
        rgcn(3, dim, dim, x=x, norm=True, next_scale=dinv, adj_all=adj_all)
        gcn("l3", "L3_gnn_W", "L3_gnn_b", x=x, store_to=out)


_INS = ["x", "src", "dst", "edge_type_3", "edge_type_34", "node_type_3", "L0_gnn_W_rel", "L0_gnn_W_root",
        "L0_gnn_b_rgcn", "L0_gnn_W_gcn", "L0_gnn_b_gcn", "L1_gnn_W1", "L1_gnn_b1", "L1_gnn_W2", "L1_gnn_b2",
        "L2_gnn_node_emb", "L2_gnn_w_rel1", "L2_gnn_w_root1", "L2_gnn_b1", "L2_gnn_w_rel2", "L2_gnn_w_root2",
        "L2_gnn_b2", "L2_gnn_w_rel3", "L2_gnn_w_root3", "L2_gnn_b3", "L3_gnn_W", "L3_gnn_b"]


def kernel(**inputs):
    import numpy as _np
    import concourse.bacc as _bacc
    from concourse import mybir as _mybir
    from concourse.bass_utils import run_bass_kernel_spmd as _run

    nc = _bacc.Bacc("TRN2", target_bir_lowering=False, num_devices=1)
    arrays, aps = {}, {}
    for name in _INS:
        a = _np.ascontiguousarray(inputs[name])
        arrays[f"in_{name}"] = a
        aps[name] = nc.dram_tensor(f"in_{name}", a.shape, _mybir.dt.from_np(a.dtype), kind="ExternalInput").ap()
    out = nc.dram_tensor("out_0", arrays["in_x"].shape, F32, kind="ExternalOutput").ap()
    gnn_kernel(nc, aps, out)
    r = _run(nc, [arrays], core_ids=[0])
    return r.results[0]["out_0"]
```
